# Optimizing a Trainium2 kernel written in Bass

```python
import numpy as np
import jax
import jax.numpy as jnp

def _softmax(x, axis=-1):
    return jax.nn.softmax(x, axis=axis)

def _gelu(x):
    return jax.nn.gelu(x, approximate=True)

def _silu(x):
    return jax.nn.silu(x)

def _sigmoid(x):
    return jax.nn.sigmoid(x)

def _layernorm(x, axis=-1, eps=1e-05):
    m = jnp.mean(x, axis=axis, keepdims=True)
    v = jnp.var(x, axis=axis, keepdims=True)
    return (x - m) / jnp.sqrt(v + eps)

def _scatter_add(tgt, idx, src, axis=0):
    return tgt.at[idx].add(src)

def _segment_sum(src, seg, n):
    return jax.ops.segment_sum(src, seg, n)
kernel_name = 'mk_xattn_seq_d4_seqx_r8_6ab4b0'

def setup_inputs(seed: int=0):
    np.random.seed(seed)
    _w = jnp.asarray

    def _rec_inputs():
        import jax
        import jax.numpy as jnp
        _rk = jax.random.key(seed)
        x = 7.22e-05 + 1 * jax.random.normal(jax.random.fold_in(_rk, 1), (16, 128, 256), jnp.float32)
        _lenS = 128 - jax.random.randint(jax.random.fold_in(_rk, 7), (16,), 0, max(1, 128 // 4) + 1, jnp.int32)
        _lenS2 = 128 - jax.random.randint(jax.random.fold_in(_rk, 8), (16,), 0, max(1, 128 // 4) + 1, jnp.int32)
        _ctx_2048P = jax.random.normal(jax.random.fold_in(_rk, 11), (16, 16, 256), jnp.float32)
        _ctx_2048c = jax.random.dirichlet(jax.random.fold_in(_rk, 511), 0.3 * jnp.ones((16,), jnp.float32), (16, 128))
        _ctx_2048t = jnp.einsum('bsk,bkd->bsd', _ctx_2048c, _ctx_2048P)
        _ctx_2048t = _ctx_2048t * jax.lax.rsqrt(jnp.mean(jnp.square(_ctx_2048t)) + 1e-12) * 0.953939
        ctx_2048 = 4.13588e-05 + 0.999923 * (_ctx_2048t + 0.3 * jax.random.normal(jax.random.fold_in(_rk, 611), (16, 128, 256), jnp.float32))
        _validS = jnp.arange(128)[None, :] < _lenS[:, None]
        _validS2 = jnp.arange(128)[None, :] < _lenS2[:, None]
        _causal = jnp.tril(jnp.ones((128, 128), dtype=bool))
        mask_BxS2_bf1 = jnp.ones((16, 128), dtype=bool)
        mask_Bx1xSxS2_ff0 = jnp.where(jnp.ones((16, 1, 128, 128), dtype=bool), 0.0, -1000000000.0).astype(jnp.float32)
        return (x, ctx_2048, mask_BxS2_bf1, mask_Bx1xSxS2_ff0)
    x, ctx_2048, mask_BxS2_bf1, mask_Bx1xSxS2_ff0 = _rec_inputs()

    def _L0_xattn_setup():
        import jax, jax.numpy as jnp
        import numpy as np
        B, CQ, CKV, LQ, LKV, HEADS = (4, 128, 128, 256, 256, 16)

        def _conv1x1(W, x):
            return jnp.einsum('oi,bil->bol', W, x)

        def _linear_interp(x, L_out):
            B_, C_, L_in = x.shape
            if L_in == L_out:
                return x
            scale = L_in / L_out
            pos = (jnp.arange(L_out, dtype=x.dtype) + 0.5) * scale - 0.5
            pos = jnp.clip(pos, 0.0, L_in - 1)
            lo = jnp.floor(pos).astype(jnp.int32)
            hi = jnp.minimum(lo + 1, L_in - 1)
            w = pos - lo.astype(x.dtype)
            return x[:, :, lo] * (1.0 - w) + x[:, :, hi] * w
        key = jax.random.key(seed)
        ks = jax.random.split(key, 7)
        winit = 1.0 / np.sqrt(CQ)
        return {'query': jax.random.normal(ks[0], (B, CQ, LQ), dtype=jnp.float32), 'context': jax.random.normal(ks[1], (B, CKV, LKV), dtype=jnp.float32), 'Wq': jax.random.normal(ks[2], (CQ, CQ), dtype=jnp.float32) * winit, 'Wk': jax.random.normal(ks[3], (CQ, CKV), dtype=jnp.float32) * winit, 'Wv': jax.random.normal(ks[4], (CQ, CKV), dtype=jnp.float32) * winit, 'Wo': jax.random.normal(ks[5], (CQ, CQ), dtype=jnp.float32) * winit, 'bo': jnp.zeros((CQ,), dtype=jnp.float32), 'heads': HEADS}
    _L0_xattn_all = _L0_xattn_setup()
    _L0_xattn_in = {k: v for k, v in _L0_xattn_all.items() if k in ('Wq', 'Wk', 'Wv', 'Wo', 'bo')}
    del _L0_xattn_all

    def _L1_xattn_setup():
        import jax, jax.numpy as jnp
        import numpy as np
        D = 256
        H = 16
        HD = D // H
        INNER = 4 * D
        EPS = 1e-05

        def layer_norm(x, w, b):
            mu = jnp.mean(x, axis=-1, keepdims=True)
            var = jnp.mean(jnp.square(x - mu), axis=-1, keepdims=True)
            return (x - mu) * jax.lax.rsqrt(var + EPS) * w + b
        key = jax.random.key(seed)
        ks = jax.random.split(key, 12)
        B, LQ, LK = (4, 128, 256)
        std = 0.02
        inp = {'hidden_states': jax.random.normal(ks[0], (B, LQ, D), jnp.float32), 'encoder_hidden_states': jax.random.normal(ks[1], (B, LK, D), jnp.float32), 'encoder_attention_mask': jnp.ones((B, LK), dtype=bool), 'ln1_w': jnp.ones((D,), jnp.float32), 'ln1_b': jnp.zeros((D,), jnp.float32), 'q_w': jax.random.normal(ks[2], (D, D), jnp.float32) * std, 'q_b': jnp.zeros((D,), jnp.float32), 'k_w': jax.random.normal(ks[3], (D, D), jnp.float32) * std, 'k_b': jnp.zeros((D,), jnp.float32), 'v_w': jax.random.normal(ks[4], (D, D), jnp.float32) * std, 'v_b': jnp.zeros((D,), jnp.float32), 'cproj_w': jax.random.normal(ks[5], (D, D), jnp.float32) * std, 'cproj_b': jnp.zeros((D,), jnp.float32), 'ln2_w': jnp.ones((D,), jnp.float32), 'ln2_b': jnp.zeros((D,), jnp.float32), 'fc_w': jax.random.normal(ks[6], (D, INNER), jnp.float32) * std, 'fc_b': jnp.zeros((INNER,), jnp.float32), 'proj_w': jax.random.normal(ks[7], (INNER, D), jnp.float32) * std, 'proj_b': jnp.zeros((D,), jnp.float32)}
        return inp
    _L1_xattn_all = _L1_xattn_setup()
    _L1_xattn_in = {k: v for k, v in _L1_xattn_all.items() if k in ('ln1_w', 'ln1_b', 'q_w', 'q_b', 'k_w', 'k_b', 'v_w', 'v_b', 'cproj_w', 'cproj_b', 'ln2_w', 'ln2_b', 'fc_w', 'fc_b', 'proj_w', 'proj_b')}
    del _L1_xattn_all

    def _L2_xattn_setup():
        import jax, jax.numpy as jnp
        import numpy as np
        B, Q, S1, S2 = (4, 32, 256, 256)
        D, H, K, F = (256, 16, 128, 1024)
        LN_EPS = 1e-05

        def _layer_norm(x, scale, offset):
            mu = jnp.mean(x, axis=-1, keepdims=True)
            var = jnp.var(x, axis=-1, keepdims=True)
            return (x - mu) * jax.lax.rsqrt(var + LN_EPS) * scale + offset

        def _cross_attention(q_in, kv_in, wq, bq, wk, bk, wv, bv, wo, bo, bias_k, bias_v):
            b, q_len, _ = q_in.shape
            t = kv_in.shape[1]
            qh = (q_in @ wq + bq).reshape(b, q_len, H, K)
            kh = (kv_in @ wk + bk).reshape(b, t, H, K)
            vh = (kv_in @ wv + bv).reshape(b, t, H, K)
            kh = jnp.concatenate([kh, jnp.broadcast_to(bias_k, (b, 1, H, K))], axis=1)
            vh = jnp.concatenate([vh, jnp.broadcast_to(bias_v, (b, 1, H, K))], axis=1)
            scale = jnp.sqrt(jnp.asarray(K, q_in.dtype))
            logits = jnp.einsum('bqhk,bthk->bhqt', qh, kh) / scale
            weights = jax.nn.softmax(logits, axis=-1)
            ctx = jnp.einsum('bhqt,bthk->bqhk', weights, vh).reshape(b, q_len, H * K)
            return ctx @ wo + bo

        def _forward(x, xf_1, xf_2, ln1_scale, ln1_offset, wq1, bq1, wk1, bk1, wv1, bv1, wo1, bo1, bias_k1, bias_v1, ln2_scale, ln2_offset, wq2, bq2, wk2, bk2, wv2, bv2, wo2, bo2, bias_k2, bias_v2, ln_mlp_scale, ln_mlp_offset, w_fc1, b_fc1, w_fc2, b_fc2):
            res = x
            h = _layer_norm(x, ln1_scale, ln1_offset)
            x = res + _cross_attention(h, xf_1, wq1, bq1, wk1, bk1, wv1, bv1, wo1, bo1, bias_k1, bias_v1)
            res = x
            h = _layer_norm(x, ln2_scale, ln2_offset)
            x = res + _cross_attention(h, xf_2, wq2, bq2, wk2, bk2, wv2, bv2, wo2, bo2, bias_k2, bias_v2)
            h = _layer_norm(x, ln_mlp_scale, ln_mlp_offset)
            h = jax.nn.gelu(h @ w_fc1 + b_fc1, approximate=False) @ w_fc2 + b_fc2
            return x + h
        key = jax.random.key(seed)
        ks = iter(jax.random.split(key, 64))

        def rn(shape, s=0.02):
            return jax.random.normal(next(ks), shape, jnp.float32) * s
        inp = {'x': rn((B, Q, D), 1.0), 'xf_1': rn((B, S1, D), 1.0), 'xf_2': rn((B, S2, D), 1.0)}
        for i in (1, 2):
            inp[f'ln{i}_scale'] = jnp.ones((D,), jnp.float32)
            inp[f'ln{i}_offset'] = jnp.zeros((D,), jnp.float32)
            inp[f'wq{i}'] = rn((D, H * K))
            inp[f'bq{i}'] = jnp.zeros((H * K,), jnp.float32)
            inp[f'wk{i}'] = rn((D, H * K))
            inp[f'bk{i}'] = jnp.zeros((H * K,), jnp.float32)
            inp[f'wv{i}'] = rn((D, H * K))
            inp[f'bv{i}'] = jnp.zeros((H * K,), jnp.float32)
            inp[f'wo{i}'] = rn((H * K, D))
            inp[f'bo{i}'] = jnp.zeros((D,), jnp.float32)
            inp[f'bias_k{i}'] = rn((1, 1, H, K))
            inp[f'bias_v{i}'] = rn((1, 1, H, K))
        inp['ln_mlp_scale'] = jnp.ones((D,), jnp.float32)
        inp['ln_mlp_offset'] = jnp.zeros((D,), jnp.float32)
        inp['w_fc1'] = rn((D, F))
        inp['b_fc1'] = jnp.zeros((F,), jnp.float32)
        inp['w_fc2'] = rn((F, D))
        inp['b_fc2'] = jnp.zeros((D,), jnp.float32)
        return inp
    _L2_xattn_all = _L2_xattn_setup()
    _L2_xattn_in = {k: v for k, v in _L2_xattn_all.items() if k in ('ln1_scale', 'ln1_offset', 'wq1', 'bq1', 'wk1', 'bk1', 'wv1', 'bv1', 'wo1', 'bo1', 'bias_k1', 'bias_v1', 'ln2_scale', 'ln2_offset', 'wq2', 'bq2', 'wk2', 'bk2', 'wv2', 'bv2', 'wo2', 'bo2', 'bias_k2', 'bias_v2', 'ln_mlp_scale', 'ln_mlp_offset', 'w_fc1', 'b_fc1', 'w_fc2', 'b_fc2')}
    del _L2_xattn_all

    def _L3_xattn_setup():
        import jax, jax.numpy as jnp
        import numpy as np
        H = 256
        NH = 32
        KVH = 8
        HD = H // NH
        GROUPS = NH // KVH
        EPS = 1e-06
        B, L, S = (4, 128, 128)

        def _gqa_forward(hidden_state, encoder_hidden_state, encoder_attention_mask, Wq, bq, Wk, bk, Wv, bv, Wo, bo, gamma, beta):
            b, l, _ = hidden_state.shape
            s = encoder_hidden_state.shape[1]
            q = hidden_state @ Wq + bq
            k = encoder_hidden_state @ Wk + bk
            v = encoder_hidden_state @ Wv + bv
            q = q.reshape(b, l, KVH, GROUPS, HD).transpose(0, 2, 3, 1, 4)
            k = k.reshape(b, s, KVH, HD).transpose(0, 2, 1, 3)
            v = v.reshape(b, s, KVH, HD).transpose(0, 2, 1, 3)
            scale = 1.0 / jnp.sqrt(jnp.asarray(HD, q.dtype))
            scores = jnp.einsum('bkgld,bksd->bkgls', q, k) * scale
            scores = scores + encoder_attention_mask[:, :, None, :, :]
            attn = jax.nn.softmax(scores, axis=-1)
            out = jnp.einsum('bkgls,bksd->bkgld', attn, v)
            out = out.transpose(0, 3, 1, 2, 4).reshape(b, l, H)
            out = out @ Wo + bo
            x = out + hidden_state
            mu = jnp.mean(x, axis=-1, keepdims=True)
            var = jnp.var(x, axis=-1, keepdims=True)
            return (x - mu) * jax.lax.rsqrt(var + EPS) * gamma + beta
        key = jax.random.key(seed)
        ks = jax.random.split(key, 12)
        sd = 0.02
        return {'hidden_state': jax.random.normal(ks[0], (B, L, H), jnp.float32), 'encoder_hidden_state': jax.random.normal(ks[1], (B, S, H), jnp.float32), 'encoder_attention_mask': jnp.zeros((B, 1, L, S), jnp.float32), 'Wq': jax.random.normal(ks[2], (H, H), jnp.float32) * sd, 'bq': jnp.zeros((H,), jnp.float32), 'Wk': jax.random.normal(ks[3], (H, KVH * HD), jnp.float32) * sd, 'bk': jnp.zeros((KVH * HD,), jnp.float32), 'Wv': jax.random.normal(ks[4], (H, KVH * HD), jnp.float32) * sd, 'bv': jnp.zeros((KVH * HD,), jnp.float32), 'Wo': jax.random.normal(ks[5], (H, H), jnp.float32) * sd, 'bo': jnp.zeros((H,), jnp.float32), 'gamma': jnp.ones((H,), jnp.float32), 'beta': jnp.zeros((H,), jnp.float32)}
    _L3_xattn_all = _L3_xattn_setup()
    _L3_xattn_in = {k: v for k, v in _L3_xattn_all.items() if k in ('Wq', 'bq', 'Wk', 'bk', 'Wv', 'bv', 'Wo', 'bo', 'gamma', 'beta')}
    del _L3_xattn_all
    return {'x': x, 'ctx_2048': ctx_2048, 'mask_BxS2_bf1': mask_BxS2_bf1, 'mask_Bx1xSxS2_ff0': mask_Bx1xSxS2_ff0, 'L0_xattn_Wq': _L0_xattn_in['Wq'], 'L0_xattn_Wk': _L0_xattn_in['Wk'], 'L0_xattn_Wv': _L0_xattn_in['Wv'], 'L0_xattn_Wo': _L0_xattn_in['Wo'], 'L0_xattn_bo': _L0_xattn_in['bo'], 'L1_xattn_ln1_w': _L1_xattn_in['ln1_w'], 'L1_xattn_ln1_b': _L1_xattn_in['ln1_b'], 'L1_xattn_q_w': _L1_xattn_in['q_w'], 'L1_xattn_q_b': _L1_xattn_in['q_b'], 'L1_xattn_k_w': _L1_xattn_in['k_w'], 'L1_xattn_k_b': _L1_xattn_in['k_b'], 'L1_xattn_v_w': _L1_xattn_in['v_w'], 'L1_xattn_v_b': _L1_xattn_in['v_b'], 'L1_xattn_cproj_w': _L1_xattn_in['cproj_w'], 'L1_xattn_cproj_b': _L1_xattn_in['cproj_b'], 'L1_xattn_ln2_w': _L1_xattn_in['ln2_w'], 'L1_xattn_ln2_b': _L1_xattn_in['ln2_b'], 'L1_xattn_fc_w': _L1_xattn_in['fc_w'], 'L1_xattn_fc_b': _L1_xattn_in['fc_b'], 'L1_xattn_proj_w': _L1_xattn_in['proj_w'], 'L1_xattn_proj_b': _L1_xattn_in['proj_b'], 'L2_xattn_ln1_scale': _L2_xattn_in['ln1_scale'], 'L2_xattn_ln1_offset': _L2_xattn_in['ln1_offset'], 'L2_xattn_wq1': _L2_xattn_in['wq1'], 'L2_xattn_bq1': _L2_xattn_in['bq1'], 'L2_xattn_wk1': _L2_xattn_in['wk1'], 'L2_xattn_bk1': _L2_xattn_in['bk1'], 'L2_xattn_wv1': _L2_xattn_in['wv1'], 'L2_xattn_bv1': _L2_xattn_in['bv1'], 'L2_xattn_wo1': _L2_xattn_in['wo1'], 'L2_xattn_bo1': _L2_xattn_in['bo1'], 'L2_xattn_bias_k1': _L2_xattn_in['bias_k1'], 'L2_xattn_bias_v1': _L2_xattn_in['bias_v1'], 'L2_xattn_ln2_scale': _L2_xattn_in['ln2_scale'], 'L2_xattn_ln2_offset': _L2_xattn_in['ln2_offset'], 'L2_xattn_wq2': _L2_xattn_in['wq2'], 'L2_xattn_bq2': _L2_xattn_in['bq2'], 'L2_xattn_wk2': _L2_xattn_in['wk2'], 'L2_xattn_bk2': _L2_xattn_in['bk2'], 'L2_xattn_wv2': _L2_xattn_in['wv2'], 'L2_xattn_bv2': _L2_xattn_in['bv2'], 'L2_xattn_wo2': _L2_xattn_in['wo2'], 'L2_xattn_bo2': _L2_xattn_in['bo2'], 'L2_xattn_bias_k2': _L2_xattn_in['bias_k2'], 'L2_xattn_bias_v2': _L2_xattn_in['bias_v2'], 'L2_xattn_ln_mlp_scale': _L2_xattn_in['ln_mlp_scale'], 'L2_xattn_ln_mlp_offset': _L2_xattn_in['ln_mlp_offset'], 'L2_xattn_w_fc1': _L2_xattn_in['w_fc1'], 'L2_xattn_b_fc1': _L2_xattn_in['b_fc1'], 'L2_xattn_w_fc2': _L2_xattn_in['w_fc2'], 'L2_xattn_b_fc2': _L2_xattn_in['b_fc2'], 'L3_xattn_Wq': _L3_xattn_in['Wq'], 'L3_xattn_bq': _L3_xattn_in['bq'], 'L3_xattn_Wk': _L3_xattn_in['Wk'], 'L3_xattn_bk': _L3_xattn_in['bk'], 'L3_xattn_Wv': _L3_xattn_in['Wv'], 'L3_xattn_bv': _L3_xattn_in['bv'], 'L3_xattn_Wo': _L3_xattn_in['Wo'], 'L3_xattn_bo': _L3_xattn_in['bo'], 'L3_xattn_gamma': _L3_xattn_in['gamma'], 'L3_xattn_beta': _L3_xattn_in['beta']}

def reference(x, ctx_2048, mask_BxS2_bf1, mask_Bx1xSxS2_ff0, L0_xattn_Wq, L0_xattn_Wk, L0_xattn_Wv, L0_xattn_Wo, L0_xattn_bo, L1_xattn_ln1_w, L1_xattn_ln1_b, L1_xattn_q_w, L1_xattn_q_b, L1_xattn_k_w, L1_xattn_k_b, L1_xattn_v_w, L1_xattn_v_b, L1_xattn_cproj_w, L1_xattn_cproj_b, L1_xattn_ln2_w, L1_xattn_ln2_b, L1_xattn_fc_w, L1_xattn_fc_b, L1_xattn_proj_w, L1_xattn_proj_b, L2_xattn_ln1_scale, L2_xattn_ln1_offset, L2_xattn_wq1, L2_xattn_bq1, L2_xattn_wk1, L2_xattn_bk1, L2_xattn_wv1, L2_xattn_bv1, L2_xattn_wo1, L2_xattn_bo1, L2_xattn_bias_k1, L2_xattn_bias_v1, L2_xattn_ln2_scale, L2_xattn_ln2_offset, L2_xattn_wq2, L2_xattn_bq2, L2_xattn_wk2, L2_xattn_bk2, L2_xattn_wv2, L2_xattn_bv2, L2_xattn_wo2, L2_xattn_bo2, L2_xattn_bias_k2, L2_xattn_bias_v2, L2_xattn_ln_mlp_scale, L2_xattn_ln_mlp_offset, L2_xattn_w_fc1, L2_xattn_b_fc1, L2_xattn_w_fc2, L2_xattn_b_fc2, L3_xattn_Wq, L3_xattn_bq, L3_xattn_Wk, L3_xattn_bk, L3_xattn_Wv, L3_xattn_bv, L3_xattn_Wo, L3_xattn_bo, L3_xattn_gamma, L3_xattn_beta):
    import jax
    import jax.numpy as jnp

    def _L0_xattn_ref(query, context, Wq, Wk, Wv, Wo, bo, heads):
        import jax, jax.numpy as jnp
        import numpy as np
        B, CQ, CKV, LQ, LKV, HEADS = (4, 128, 128, 256, 256, 16)

        def _conv1x1(W, x):
            return jnp.einsum('oi,bil->bol', W, x)

        def _linear_interp(x, L_out):
            B_, C_, L_in = x.shape
            if L_in == L_out:
                return x
            scale = L_in / L_out
            pos = (jnp.arange(L_out, dtype=x.dtype) + 0.5) * scale - 0.5
            pos = jnp.clip(pos, 0.0, L_in - 1)
            lo = jnp.floor(pos).astype(jnp.int32)
            hi = jnp.minimum(lo + 1, L_in - 1)
            w = pos - lo.astype(x.dtype)
            return x[:, :, lo] * (1.0 - w) + x[:, :, hi] * w
        B_, Cq, Lq = query.shape
        H = heads
        D = Cq // H
        scale = D ** (-0.5)
        q = _conv1x1(Wq, query).reshape(B_, H, D, Lq)
        k = _conv1x1(Wk, context)
        v = _conv1x1(Wv, context)
        if k.shape[2] != Lq:
            k = _linear_interp(k, Lq)
            v = _linear_interp(v, Lq)
        k = k.reshape(B_, H, D, Lq)
        v = v.reshape(B_, H, D, Lq)
        attn = jnp.einsum('bhdi,bhdj->bhij', q, k) * scale
        attn = jax.nn.softmax(attn, axis=-1)
        out = jnp.einsum('bhij,bhdj->bhdi', attn, v).reshape(B_, Cq, Lq)
        return _conv1x1(Wo, out) + bo[None, :, None] + query

    def _L1_xattn_ref(hidden_states, encoder_hidden_states, encoder_attention_mask, ln1_w, ln1_b, q_w, q_b, k_w, k_b, v_w, v_b, cproj_w, cproj_b, ln2_w, ln2_b, fc_w, fc_b, proj_w, proj_b):
        import jax, jax.numpy as jnp
        import numpy as np
        D = 256
        H = 16
        HD = D // H
        INNER = 4 * D
        EPS = 1e-05

        def layer_norm(x, w, b):
            mu = jnp.mean(x, axis=-1, keepdims=True)
            var = jnp.mean(jnp.square(x - mu), axis=-1, keepdims=True)
            return (x - mu) * jax.lax.rsqrt(var + EPS) * w + b
        B, LQ, _ = hidden_states.shape
        LK = encoder_hidden_states.shape[1]
        residual = hidden_states
        x = layer_norm(hidden_states, ln1_w, ln1_b)
        q = (x @ q_w + q_b).reshape(B, LQ, H, HD).transpose(0, 2, 1, 3)
        k = (encoder_hidden_states @ k_w + k_b).reshape(B, LK, H, HD).transpose(0, 2, 1, 3)
        v = (encoder_hidden_states @ v_w + v_b).reshape(B, LK, H, HD).transpose(0, 2, 1, 3)
        scale = 1.0 / np.sqrt(HD).astype(np.float32)
        scores = jnp.einsum('bhqd,bhkd->bhqk', q, k) * scale
        mask = encoder_attention_mask[:, None, None, :]
        mask_value = jnp.finfo(scores.dtype).min
        scores = jnp.where(mask, scores, mask_value)
        attn = jax.nn.softmax(scores, axis=-1)
        out = jnp.einsum('bhqk,bhkd->bhqd', attn, v)
        out = out.transpose(0, 2, 1, 3).reshape(B, LQ, D)
        out = out @ cproj_w + cproj_b
        hidden = out + residual
        residual = hidden
        y = layer_norm(hidden, ln2_w, ln2_b)
        y = jax.nn.gelu(y @ fc_w + fc_b, approximate=True)
        y = y @ proj_w + proj_b
        return residual + y

    def _L2_xattn_ref(x, xf_1, xf_2, ln1_scale, ln1_offset, wq1, bq1, wk1, bk1, wv1, bv1, wo1, bo1, bias_k1, bias_v1, ln2_scale, ln2_offset, wq2, bq2, wk2, bk2, wv2, bv2, wo2, bo2, bias_k2, bias_v2, ln_mlp_scale, ln_mlp_offset, w_fc1, b_fc1, w_fc2, b_fc2):
        import jax, jax.numpy as jnp
        import numpy as np
        B, Q, S1, S2 = (4, 32, 256, 256)
        D, H, K, F = (256, 16, 128, 1024)
        LN_EPS = 1e-05

        def _layer_norm(x, scale, offset):
            mu = jnp.mean(x, axis=-1, keepdims=True)
            var = jnp.var(x, axis=-1, keepdims=True)
            return (x - mu) * jax.lax.rsqrt(var + LN_EPS) * scale + offset

        def _cross_attention(q_in, kv_in, wq, bq, wk, bk, wv, bv, wo, bo, bias_k, bias_v):
            b, q_len, _ = q_in.shape
            t = kv_in.shape[1]
            qh = (q_in @ wq + bq).reshape(b, q_len, H, K)
            kh = (kv_in @ wk + bk).reshape(b, t, H, K)
            vh = (kv_in @ wv + bv).reshape(b, t, H, K)
            kh = jnp.concatenate([kh, jnp.broadcast_to(bias_k, (b, 1, H, K))], axis=1)
            vh = jnp.concatenate([vh, jnp.broadcast_to(bias_v, (b, 1, H, K))], axis=1)
            scale = jnp.sqrt(jnp.asarray(K, q_in.dtype))
            logits = jnp.einsum('bqhk,bthk->bhqt', qh, kh) / scale
            weights = jax.nn.softmax(logits, axis=-1)
            ctx = jnp.einsum('bhqt,bthk->bqhk', weights, vh).reshape(b, q_len, H * K)
            return ctx @ wo + bo

        def _forward(x, xf_1, xf_2, ln1_scale, ln1_offset, wq1, bq1, wk1, bk1, wv1, bv1, wo1, bo1, bias_k1, bias_v1, ln2_scale, ln2_offset, wq2, bq2, wk2, bk2, wv2, bv2, wo2, bo2, bias_k2, bias_v2, ln_mlp_scale, ln_mlp_offset, w_fc1, b_fc1, w_fc2, b_fc2):
            res = x
            h = _layer_norm(x, ln1_scale, ln1_offset)
            x = res + _cross_attention(h, xf_1, wq1, bq1, wk1, bk1, wv1, bv1, wo1, bo1, bias_k1, bias_v1)
            res = x
            h = _layer_norm(x, ln2_scale, ln2_offset)
            x = res + _cross_attention(h, xf_2, wq2, bq2, wk2, bk2, wv2, bv2, wo2, bo2, bias_k2, bias_v2)
            h = _layer_norm(x, ln_mlp_scale, ln_mlp_offset)
            h = jax.nn.gelu(h @ w_fc1 + b_fc1, approximate=False) @ w_fc2 + b_fc2
            return x + h
        return _forward(x, xf_1, xf_2, ln1_scale, ln1_offset, wq1, bq1, wk1, bk1, wv1, bv1, wo1, bo1, bias_k1, bias_v1, ln2_scale, ln2_offset, wq2, bq2, wk2, bk2, wv2, bv2, wo2, bo2, bias_k2, bias_v2, ln_mlp_scale, ln_mlp_offset, w_fc1, b_fc1, w_fc2, b_fc2)

    def _L3_xattn_ref(hidden_state, encoder_hidden_state, encoder_attention_mask, Wq, bq, Wk, bk, Wv, bv, Wo, bo, gamma, beta):
        import jax, jax.numpy as jnp
        import numpy as np
        H = 256
        NH = 32
        KVH = 8
        HD = H // NH
        GROUPS = NH // KVH
        EPS = 1e-06
        B, L, S = (4, 128, 128)

        def _gqa_forward(hidden_state, encoder_hidden_state, encoder_attention_mask, Wq, bq, Wk, bk, Wv, bv, Wo, bo, gamma, beta):
            b, l, _ = hidden_state.shape
            s = encoder_hidden_state.shape[1]
            q = hidden_state @ Wq + bq
            k = encoder_hidden_state @ Wk + bk
            v = encoder_hidden_state @ Wv + bv
            q = q.reshape(b, l, KVH, GROUPS, HD).transpose(0, 2, 3, 1, 4)
            k = k.reshape(b, s, KVH, HD).transpose(0, 2, 1, 3)
            v = v.reshape(b, s, KVH, HD).transpose(0, 2, 1, 3)
            scale = 1.0 / jnp.sqrt(jnp.asarray(HD, q.dtype))
            scores = jnp.einsum('bkgld,bksd->bkgls', q, k) * scale
            scores = scores + encoder_attention_mask[:, :, None, :, :]
            attn = jax.nn.softmax(scores, axis=-1)
            out = jnp.einsum('bkgls,bksd->bkgld', attn, v)
            out = out.transpose(0, 3, 1, 2, 4).reshape(b, l, H)
            out = out @ Wo + bo
            x = out + hidden_state
            mu = jnp.mean(x, axis=-1, keepdims=True)
            var = jnp.var(x, axis=-1, keepdims=True)
            return (x - mu) * jax.lax.rsqrt(var + EPS) * gamma + beta
        return _gqa_forward(hidden_state, encoder_hidden_state, encoder_attention_mask, Wq, bq, Wk, bk, Wv, bv, Wo, bo, gamma, beta)
    x = _L0_xattn_ref(x, ctx_2048, L0_xattn_Wq, L0_xattn_Wk, L0_xattn_Wv, L0_xattn_Wo, L0_xattn_bo, 16)
    x = _L1_xattn_ref(x, ctx_2048, mask_BxS2_bf1, L1_xattn_ln1_w, L1_xattn_ln1_b, L1_xattn_q_w, L1_xattn_q_b, L1_xattn_k_w, L1_xattn_k_b, L1_xattn_v_w, L1_xattn_v_b, L1_xattn_cproj_w, L1_xattn_cproj_b, L1_xattn_ln2_w, L1_xattn_ln2_b, L1_xattn_fc_w, L1_xattn_fc_b, L1_xattn_proj_w, L1_xattn_proj_b)
    x = _L2_xattn_ref(x, ctx_2048, ctx_2048, L2_xattn_ln1_scale, L2_xattn_ln1_offset, L2_xattn_wq1, L2_xattn_bq1, L2_xattn_wk1, L2_xattn_bk1, L2_xattn_wv1, L2_xattn_bv1, L2_xattn_wo1, L2_xattn_bo1, L2_xattn_bias_k1, L2_xattn_bias_v1, L2_xattn_ln2_scale, L2_xattn_ln2_offset, L2_xattn_wq2, L2_xattn_bq2, L2_xattn_wk2, L2_xattn_bk2, L2_xattn_wv2, L2_xattn_bv2, L2_xattn_wo2, L2_xattn_bo2, L2_xattn_bias_k2, L2_xattn_bias_v2, L2_xattn_ln_mlp_scale, L2_xattn_ln_mlp_offset, L2_xattn_w_fc1, L2_xattn_b_fc1, L2_xattn_w_fc2, L2_xattn_b_fc2)
    x = _L3_xattn_ref(x, ctx_2048, mask_Bx1xSxS2_ff0, L3_xattn_Wq, L3_xattn_bq, L3_xattn_Wk, L3_xattn_bk, L3_xattn_Wv, L3_xattn_bv, L3_xattn_Wo, L3_xattn_bo, L3_xattn_gamma, L3_xattn_beta)
    return x

_drawn_inputs = setup_inputs


def setup_inputs(seed=0):
    import zlib

    import numpy as np

    out = dict(_drawn_inputs(seed))
    spreads = {'L0_xattn_bo': (0.0, 0.8),
     'L1_xattn_ln1_w': (1.0, 0.6),
     'L1_xattn_ln1_b': (0.0, 0.8),
     'L1_xattn_q_b': (0.0, 0.8),
     'L1_xattn_k_b': (0.0, 2.0),
     'L1_xattn_v_b': (0.0, 0.289),
     'L1_xattn_cproj_b': (0.0, 0.1),
     'L1_xattn_ln2_w': (1.0, 0.6),
     'L1_xattn_ln2_b': (0.0, 0.8),
     'L1_xattn_fc_b': (0.0, 0.1),
     'L1_xattn_proj_b': (0.0, 0.1),
     'L2_xattn_ln1_scale': (1.0, 0.6),
     'L2_xattn_ln1_offset': (0.0, 0.8),
     'L2_xattn_bq1': (0.0, 0.8),
     'L2_xattn_bk1': (0.0, 2.0),
     'L2_xattn_bv1': (0.0, 0.1),
     'L2_xattn_bo1': (0.0, 0.1),
     'L2_xattn_ln2_scale': (1.0, 0.6),
     'L2_xattn_ln2_offset': (0.0, 0.8),
     'L2_xattn_bq2': (0.0, 0.8),
     'L2_xattn_bk2': (0.0, 2.0),
     'L2_xattn_bv2': (0.0, 0.1),
     'L2_xattn_bo2': (0.0, 0.1),
     'L2_xattn_ln_mlp_scale': (1.0, 0.6),
     'L2_xattn_ln_mlp_offset': (0.0, 0.8),
     'L2_xattn_b_fc1': (0.0, 0.1),
     'L2_xattn_b_fc2': (0.0, 0.1),
     'L3_xattn_bq': (0.0, 0.8),
     'L3_xattn_bk': (0.0, 2.0),
     'L3_xattn_bv': (0.0, 0.296),
     'L3_xattn_bo': (0.0, 0.1),
     'L3_xattn_gamma': (1.0, 0.2),
     'L3_xattn_beta': (0.0, 0.1)}
    factors = {'L1_xattn_q_w': 8.0,
     'L1_xattn_k_w': 8.0,
     'L2_xattn_wq1': 8.0,
     'L2_xattn_wk1': 8.0,
     'L2_xattn_bias_k1': 64.0,
     'L2_xattn_bias_v1': 64.0,
     'L2_xattn_wq2': 8.0,
     'L2_xattn_wk2': 8.0,
     'L2_xattn_bias_k2': 64.0,
     'L2_xattn_bias_v2': 64.0,
     'L3_xattn_Wq': 8.0,
     'L3_xattn_Wk': 8.0}
    for name, (base, spread) in spreads.items():
        noise = np.random.default_rng([zlib.crc32(name.encode()), seed]).standard_normal(out[name].shape)
        drawn = base * np.exp(spread * noise) if base else spread * noise
        out[name] = jnp.asarray(drawn.astype(out[name].dtype))
    for name, factor in factors.items():
        out[name] = (out[name] * factor).astype(out[name].dtype)
    return out
```

```python
import concourse.bass as bass
from concourse import mybir
from contextlib import ExitStack

F32 = mybir.dt.float32
F32R = mybir.dt.float32r
U8 = mybir.dt.uint8
I32 = mybir.dt.int32
ALU = mybir.AluOpType
ACT = mybir.ActivationFunctionType
AX = mybir.AxisListType

P = 128
BATCH = 16
D = 256
GROUP = 4
NG = BATCH // GROUP
TOK = GROUP * P
KT = D // P
PASSES = ((0, 0), (0, 1), (1, 0))
F32_LOWEST = 3.4028234663852886e38


def mm3(pe, out, lhs, rhs, first, last, terms=PASSES):
    for n, (a, b) in enumerate(terms):
        ins = pe.matmul(out, lhs(a), rhs(b), start=first and n == 0, stop=last and n == len(terms) - 1)
    return ins


class Buffers:

    def __init__(self, nc, ctx, phase):
        self.nc, self.ctx, self.phase = nc, ctx, phase

    def sb(self, name, shape, dt=F32):
        return self.ctx.enter_context(self.nc.sbuf_tensor(f"{self.phase}_{name}", shape, dt))

    def bank(self, name):
        return self.ctx.enter_context(self.nc.psum_tensor(f"{self.phase}_{name}", [P, 512], F32))

    def sem(self, name):
        return self.ctx.enter_context(self.nc.semaphore(f"{self.phase}_{name}"))


def clear_semaphores(nc):
    with nc.Block() as block:
        @block.gpsimd
        def _(pool):
            pool.sem_clear(range(min(nc.free_semaphores), max(nc.free_semaphores) + 1))


def identity_phase(nc, ident):
    with ExitStack() as ctx:
        t = Buffers(nc, ctx, "id")
        cleared = t.sem("cleared")
        block = ctx.enter_context(nc.Block())

        @block.gpsimd
        def _(pool):
            pool.memset(ident[:, :], 0.0).then_inc(cleared, 1)
            pool.wait_ge(cleared, 1)
            pool.affine_select(out=ident[:, :], in_=ident[:, :], compare_op=ALU.not_equal, fill=1.0,
                               base=0, pattern=[[-1, P]], channel_multiplier=1)


def context_phase(nc, ctx_dram, ctxT_dram, ident):
    with ExitStack() as ctx:
        t = Buffers(nc, ctx, "cx")
        c = t.sb("c", [P, 2, GROUP, D])
        cT = t.sb("cT", [P, 2, 2, KT, TOK], F32R)
        ps = [[t.bank(f"ps{p}{k}") for k in range(KT)] for p in range(2)]
        loaded = [t.sem(f"loaded{p}") for p in range(2)]
        turned, hi_done, lo_done = t.sem("turned"), t.sem("hi_done"), t.sem("lo_done")
        stored = [t.sem(f"stored{p}") for p in range(2)]
        block = ctx.enter_context(nc.Block())

        @block.sync
        def _(sp):
            def load(g):
                if g >= 2:
                    sp.wait_ge(turned, g - 1)
                sp.dma_start(c[:, g % 2], ctx_dram[g * GROUP:(g + 1) * GROUP].rearrange("b p d -> p b d"))\
                    .then_inc(loaded[g % 2], 16)

            load(0)
            load(1)
            for g in range(NG):
                if g + 2 < NG:
                    load(g + 2)
                sp.wait_ge(lo_done, KT * (g + 1))
                sp.wait_ge(hi_done, KT * (g + 1))
                sp.dma_start(ctxT_dram[g], cT[:, g % 2].rearrange("p s k n -> p (s k n)").bitcast(F32))\
                    .then_inc(stored[g % 2], 16)
            for p in range(2):
                sp.wait_ge(stored[p], 16 * (NG // 2))

        @block.tensor
        def _(pe):
            for g in range(NG):
                pe.wait_ge(loaded[g % 2], 16 * (g // 2 + 1))
                if g >= 2:
                    pe.wait_ge(lo_done, KT * (g - 1))
                for k in range(KT):
                    for b in range(GROUP):
                        ins = pe.transpose(ps[g % 2][k][:, b * P:(b + 1) * P], c[:, g % 2, b, k * P:(k + 1) * P],
                                           ident[:, :])
                ins.then_inc(turned, 1)

        @block.scalar
        def _(act):
            for g in range(NG):
                act.wait_ge(turned, g + 1)
                if g >= 2:
                    act.wait_ge(stored[g % 2], 16 * (g // 2))
                for k in range(KT):
                    act.activation(cT[:, g % 2, 0, k], ps[g % 2][k][:, :], ACT.Copy).then_inc(hi_done, 1)

        @block.vector
        def _(dve):
            for g in range(NG):
                if g >= 2:
                    dve.wait_ge(stored[g % 2], 16 * (g // 2))
                for k in range(KT):
                    dve.wait_ge(hi_done, KT * g + k + 1)
                    dve.tensor_tensor(cT[:, g % 2, 1, k], ps[g % 2][k][:, :], cT[:, g % 2, 0, k].bitcast(F32),
                                      ALU.subtract).then_inc(lo_done, 1)


def layer0_phase(nc, x_dram, ctx_dram, w_dram, cols_dram, X, ident):
    H, DH, L = 16, 8, D
    LB = L // P
    SLOT = 32
    NT = H // 4
    NQ, NK, NV = 0, NT * P, 2 * NT * P
    NO = NV + P
    NW = NO + P
    SCALE = float(DH) ** -0.5
    with ExitStack() as ctx:
        t = Buffers(nc, ctx, "l0")
        w_raw = t.sb("w_raw", [P, NW])
        w = t.sb("w", [P, 2, NW], F32R)
        cols = t.sb("cols", [P, 3])
        xc = t.sb("xc", [P, 2, L])
        xcs = t.sb("xcs", [P, 2, 2, L], F32R)
        top = t.sb("top", [P, 2, 2, L], F32R)
        qk = t.sb("qk", [P, NT, 2, L], F32R)
        v = t.sb("v", [P, LB, H, 32])
        s_sb = t.sb("s_sb", [P, 2, LB, L])
        peak = t.sb("peak", [P, H, LB])
        probs = t.sb("probs", [P, 8, LB, L])
        o_sb = t.sb("o_sb", [P, 2, L])
        rden = t.sb("rden", [P, NT, LB, 4])
        att = t.sb("att", [P, LB, P])
        attT = t.sb("attT", [P, 2, L], F32R)
        psS = [t.bank(f"psS{i}") for i in range(2)]
        psT = [t.bank(f"psT{i}") for i in range(2)]
        psO, psN = t.bank("psO"), t.bank("psN")
        psW = [t.bank(f"psW{i}") for i in range(2)]
        (weights, w_hi, w_lo, loaded, x_hi, x_lo, proj, rounded, stacked, vproj, v_set, v_ones, scored, peaked,
         eased, turned, expd, pved, o_out, o_turned, r_done, normed, a_turned, a_hi, a_lo, outp, done) = [
            t.sem(n) for n in ("weights w_hi w_lo loaded x_hi x_lo proj rounded stacked vproj v_set v_ones scored "
                               "peaked eased turned expd pved o_out o_turned r_done normed a_turned a_hi a_lo outp "
                               "done").split()]
        block = ctx.enter_context(nc.Block())

        @block.sync
        def _(sp):
            sp.dma_start(w_raw[:, :], w_dram).then_inc(weights, 16)
            sp.dma_start(cols[:, :], cols_dram).then_inc(weights, 16)
            with sp.Fori(0, BATCH) as b:
                sp.wait_ge(done, b + 1)
                sp.dma_start(xc[:, 0], x_dram[bass.ds(b, 1)].rearrange("a p l -> p (a l)")).then_inc(loaded, 16)
                sp.dma_start(xc[:, 1], ctx_dram[bass.ds(b, 1)].rearrange("a p l -> p (a l)")).then_inc(loaded, 16)

        @block.gpsimd
        def _(pool):
            pool.memset(v[:, :, :, :], 0.0).then_inc(v_ones, 1)
            pool.wait_ge(v_ones, 1)
            pool.memset(v[:, :, :, DH:DH + 1], 1.0).then_inc(v_ones, 1)

        @block.scalar
        def _(act):
            def evac(act, b, n):
                act.wait_ge(pved, b * NT + n + 1)
                if n >= 2:
                    act.wait_ge(o_turned, b * NT + n - 1)
                act.activation(o_sb[:, n % 2], psO[:, 0:L], ACT.Copy).then_inc(o_out, 1)

            act.wait_ge(weights, 32)
            act.activation(w[:, 0], w_raw[:, :], ACT.Copy).then_inc(w_hi, 1)
            act.wait_ge(v_ones, 2)
            with act.Fori(0, BATCH) as b:
                act.wait_ge(loaded, b * 32 + 32)
                act.wait_ge(done, b + 1)
                act.activation(xcs[:, 0], xc[:, :, :], ACT.Copy).then_inc(x_hi, 1)
                for n in range(NT):
                    act.wait_ge(proj, b * NT + n + 1)
                    if n >= 2:
                        act.wait_ge(stacked, b * 2 * NT + 2 * (n - 1))
                    act.activation(top[:, n % 2], psW[n % 2][:, :].rearrange("p (a l) -> p a l", a=2), ACT.Copy)\
                        .then_inc(rounded, 1)
                act.wait_ge(vproj, b + 1)
                act.activation(v[:, :, :, 0:DH], psN[:, 0:LB * P].rearrange("p (k h d) -> p k h d", k=LB, h=H),
                               ACT.Copy).then_inc(v_set, 1)
                for h in range(H):
                    act.wait_ge(turned, b * H + h + 1)
                    if h >= 8:
                        act.wait_ge(pved, b * NT + h // 4 - 1)
                    act.activation(probs[:, h % 8], psT[h % 2][:, :].rearrange("p (k q) -> p k q", k=LB),
                                   ACT.Exp, scale=SCALE).then_inc(expd, 1)
                    if h % 4 == 3 and h >= 7:
                        evac(act, b, h // 4 - 1)
                evac(act, b, NT - 1)
                act.wait_ge(a_turned, b + 1)
                act.activation(attT[:, 0], psW[0][:, 0:L], ACT.Copy).then_inc(a_hi, 1)

        @block.vector
        def _(dve):
            dve.wait_ge(w_hi, 1)
            dve.tensor_tensor(w[:, 1], w_raw[:, :], w[:, 0].bitcast(F32), ALU.subtract).then_inc(w_lo, 1)
            dve.wait_ge(w_lo, 1)
            dve.memset(peak[:, :, :], 0.0).then_inc(done, 1)
            with dve.Fori(0, BATCH) as b:
                dve.wait_ge(x_hi, b + 1)
                dve.tensor_tensor(xcs[:, 1], xc[:, :, :], xcs[:, 0].bitcast(F32), ALU.subtract).then_inc(x_lo, 1)
                for n in range(NT):
                    dve.wait_ge(rounded, b * NT + n + 1)
                    for j in range(2):
                        dve.scalar_tensor_tensor(qk[:, n, j], top[:, n % 2, j].bitcast(F32), cols[:, j:j + 1],
                                                 psW[n % 2][:, j * L:(j + 1) * L], ALU.mult, ALU.add)\
                            .then_inc(stacked, 1)

                def norm(n):
                    dve.wait_ge(o_turned, b * NT + n + 1)
                    o = psN[:, 0:LB * P].rearrange("p (q i c) -> p q i c", q=LB, i=4)
                    dve.reciprocal(rden[:, n], o[:, :, :, DH]).then_inc(r_done, 1)
                    dve.wait_ge(r_done, b * NT + n + 1)
                    dve.tensor_tensor(att[:, :, n * 32:(n + 1) * 32].rearrange("p q (i d) -> p q i d", i=4),
                                      o[:, :, :, 0:DH],
                                      rden[:, n].rearrange("p q (i a) -> p q i a", a=1).to_broadcast([P, LB, 4, DH]),
                                      ALU.mult).then_inc(normed, 1)

                def ease(h):
                    dve.wait_ge(peaked, b * H + h + 1)
                    if h >= 2:
                        dve.wait_ge(turned, b * H + h - 1)
                    dve.tensor_tensor(s_sb[:, h % 2], psS[h % 2][:, :].rearrange("p (q k) -> p q k", q=LB),
                                      peak[:, h].rearrange("p (q a) -> p q a", a=1).to_broadcast([P, LB, L]),
                                      ALU.subtract).then_inc(eased, 1)

                for h in range(H):
                    dve.wait_ge(scored, b * H + h + 1)
                    dve.tensor_reduce(peak[:, h], psS[h % 2][:, :].rearrange("p (q k) -> p q k", q=LB), AX.X,
                                      ALU.max).then_inc(peaked, 1)
                    ease(h)
                    if h % 4 == 3 and h >= 11:
                        norm(h // 4 - 2)
                norm(NT - 2)
                norm(NT - 1)
                dve.wait_ge(a_hi, b + 1)
                dve.tensor_tensor(attT[:, 1], psW[0][:, 0:L], attT[:, 0].bitcast(F32), ALU.subtract)\
                    .then_inc(a_lo, 1)
                dve.wait_ge(outp, b + 1)
                dve.scalar_tensor_tensor(X[:, bass.ds(b, 1), :].rearrange("p a d -> p (a d)"), psW[1][:, 0:L],
                                         cols[:, 2:3], xc[:, 0], ALU.add, ALU.add).then_inc(done, 1)

        @block.tensor
        def _(pe):
            pe.wait_ge(w_lo, 1)
            pe.wait_ge(v_ones, 2)
            with pe.Fori(0, BATCH) as b:
                pe.wait_ge(done, b + 1)
                pe.wait_ge(x_lo, b + 1)
                for n in range(NT):
                    if n >= 2:
                        pe.wait_ge(stacked, b * 2 * NT + 2 * (n - 1))
                    for j, at in ((0, NQ), (1, NK)):
                        ins = mm3(pe, psW[n % 2][:, j * L:(j + 1) * L],
                                  lambda s: w[:, s, at + n * P:at + (n + 1) * P], lambda s: xcs[:, s, j],
                                  True, True)
                    ins.then_inc(proj, 1)
                for k in range(LB):
                    ins = mm3(pe, psN[:, k * P:(k + 1) * P], lambda s: xcs[:, s, 1, k * P:(k + 1) * P],
                              lambda s: w[:, s, NV:NV + P], True, True)
                ins.then_inc(vproj, 1)

                def scores(h):
                    n, i = h // 4, h % 4
                    rows = slice(i * SLOT, (i + 1) * SLOT)
                    pe.wait_ge(stacked, b * 2 * NT + 2 * (n + 1))
                    if h >= 2:
                        pe.wait_ge(eased, b * H + h - 1)
                    for q in range(LB):
                        ins = pe.matmul(psS[h % 2][:, q * L:(q + 1) * L], qk[rows, n, 0, q * P:(q + 1) * P],
                                        qk[rows, n, 1, :], start=True, stop=True)
                    ins.then_inc(scored, 1)

                def turn(h):
                    pe.wait_ge(eased, b * H + h + 1)
                    if h >= 2:
                        pe.wait_ge(expd, b * H + h - 1)
                    for q in range(LB):
                        for k in range(LB):
                            ins = pe.transpose(psT[h % 2][:, k * L + q * P:k * L + (q + 1) * P],
                                               s_sb[:, h % 2, q, k * P:(k + 1) * P], ident[:, :])
                    ins.then_inc(turned, 1)

                def pv(n):
                    pe.wait_ge(expd, b * H + 4 * (n + 1))
                    pe.wait_ge(v_set, b + 1)
                    if n >= 1:
                        pe.wait_ge(o_out, b * NT + n)
                    for k in range(LB):
                        for i in range(4):
                            h = 4 * n + i
                            ins = pe.matmul(psO[32 * i:32 * i + 32, 0:L], v[:, k, h, :], probs[:, h % 8, k, :],
                                            start=k == 0, stop=k == LB - 1)
                    ins.then_inc(pved, 1)

                def turn_out(n):
                    pe.wait_ge(o_out, b * NT + n + 1)
                    if n == 0:
                        pe.wait_ge(v_set, b + 1)
                    else:
                        pe.wait_ge(normed, b * NT + n)
                    for q in range(LB):
                        ins = pe.transpose(psN[:, q * P:(q + 1) * P], o_sb[:, n % 2, q * P:(q + 1) * P], ident[:, :])
                    ins.then_inc(o_turned, 1)

                for step in range(H + 6):
                    if step < H:
                        scores(step)
                    if 0 <= step - 2 < H:
                        turn(step - 2)
                    n, r = divmod(step - 7, 4)
                    if r == 0 and 0 <= n < NT:
                        pv(n)
                    n, r = divmod(step - 9, 4)
                    if r == 0 and 0 <= n < NT:
                        turn_out(n)
                pe.wait_ge(normed, b * NT + NT)
                for q in range(LB):
                    ins = pe.transpose(psW[0][:, q * P:(q + 1) * P], att[:, q], ident[:, :])
                ins.then_inc(a_turned, 1)
                pe.wait_ge(a_lo, b + 1)
                mm3(pe, psW[1][:, 0:L], lambda s: w[:, s, NO:NO + P], lambda s: attT[:, s], True, True)\
                    .then_inc(outp, 1)


class TokenNorm:

    def __init__(self, t, eps, gamma=None, beta=None, xn=None, full=None):
        self.eps, self.gamma, self.beta = eps, gamma, beta
        self.stats = t.sb("ln_stats", [P, GROUP, 6])
        self.mean_var = t.sb("ln_mean_var", [P, GROUP, 2])
        self.power = t.sb("ln_power", [P, GROUP])
        self.shifted = t.sb("ln_shifted", [P, GROUP])
        self.rstd = t.sb("ln_rstd", [P, GROUP])
        self.xn = t.sb("ln_xn", [P, GROUP, D]) if xn is None else xn
        self.full = t.sb("ln_full", [P, KT, TOK]) if full is None else full
        self.hT = t.sb("hT", [P, 2, KT, TOK], F32R)
        (self.s_gate, self.s_power_set, self.s_gathered, self.s_aggregated, self.s_shift, self.s_rooted,
         self.s_normed, self.s_turned, self.s_affine, self.s_hi, self.s_lo) = [
            t.sem("ln_" + n) for n in ("gate power_set gathered aggregated shift rooted normed turned affine "
                                       "hi lo").split()]

    def pool_setup(self, pool):
        pool.memset(self.power[:, :], -0.5).then_inc(self.s_power_set, 1)

    def dve_statistics(self, dve, g, x):
        for b in range(GROUP):
            dve.bn_stats(self.stats[:, b], x(b)).then_inc(self.s_gathered, 1)
        for b in range(GROUP):
            dve.wait_ge(self.s_gathered, g * GROUP + b + 1)
            dve.sem_inc(self.s_gate, 1)
            dve.bn_aggr(self.mean_var[:, b], self.stats[:, b]).then_inc(self.s_aggregated, 1)

    def pool_rstd(self, pool, g):
        pool.wait_ge(self.s_aggregated, g * GROUP + GROUP)
        pool.sem_inc(self.s_gate, 1)
        pool.wait_ge(self.s_power_set, 1)
        pool.tensor_scalar(self.shifted[:, :], self.mean_var[:, :, 1], self.eps, 1.0, ALU.add, ALU.mult)\
            .then_inc(self.s_shift, 1)
        pool.wait_ge(self.s_shift, g + 1)
        pool.tensor_tensor(self.rstd[:, :], self.shifted[:, :], self.power[:, :], ALU.pow).then_inc(self.s_rooted, 1)

    def dve_normalise(self, dve, g, x, out=None):
        out = self.xn if out is None else out
        if self.eps is None:
            for b in range(GROUP):
                dve.tensor_copy(out[:, b], x(b)).then_inc(self.s_normed, 1)
            return
        dve.wait_ge(self.s_rooted, g + 1)
        for b in range(GROUP):
            dve.tensor_scalar(out[:, b], x(b), self.mean_var[:, b, 0:1], self.rstd[:, b:b + 1],
                              ALU.subtract, ALU.mult).then_inc(self.s_normed, 1)

    def pe_turn(self, pe, g, banks, ident):
        for k in range(KT):
            for b in range(GROUP):
                pe.wait_ge(self.s_normed, g * GROUP + b + 1)
                ins = pe.transpose(banks[k][:, b * P:(b + 1) * P], self.xn[:, b, k * P:(k + 1) * P], ident[:, :])
            ins.then_inc(self.s_turned, 1)

    def act_affine(self, act, g, banks):
        for k in range(KT):
            act.wait_ge(self.s_turned, g * KT + k + 1)
            if self.gamma is None:
                act.activation(self.full[:, k], banks[k][:, :], ACT.Copy).then_inc(self.s_affine, 1)
            else:
                act.activation(self.full[:, k], banks[k][:, :], ACT.Identity, scale=self.gamma[:, k:k + 1],
                               bias=self.beta[:, k:k + 1]).then_inc(self.s_affine, 1)
        for k in range(KT):
            act.wait_ge(self.s_affine, g * KT + k + 1)
            act.activation(self.hT[:, 0, k], self.full[:, k], ACT.Copy).then_inc(self.s_hi, 1)

    def dve_lo(self, dve, g):
        for k in range(KT):
            dve.wait_ge(self.s_hi, g * KT + k + 1)
            dve.tensor_tensor(self.hT[:, 1, k], self.full[:, k], self.hT[:, 0, k].bitcast(F32), ALU.subtract)\
                .then_inc(self.s_lo, 1)

    def pe_ready(self, pe, g):
        pe.wait_ge(self.s_lo, g * KT + KT)


def heads_phase(nc, layer, X, ctxT_dram, w_dram, cols_dram, rows_dram, mask_dram, ident, out_dram=None):
    first = layer == 1
    H, DH, SLOT = (16, 16, 64) if first else (32, 8, 32)
    KV = 16 if first else 8
    QT, KTILES = (8, 8) if first else (8, 2)
    NQD = H // 4
    VC = KV * DH
    SCALE = float(DH) ** -0.5
    NQ, NK, NV = 0, QT * P, (QT + KTILES) * P
    NO = NV + VC
    NW = NO + D
    C_MASK, C_BIAS, C_G, C_B = 0, 2, 2 + QT + KTILES, 2 + QT + KTILES + KT
    NC = C_B + KT
    R_V, R_O, R_G, R_B = 0, VC, VC + D, VC + 2 * D
    NR = VC + 3 * D
    USES = QT + KTILES + GROUP

    def place(c):
        n, i = c // 4, c % 4
        return (c // 2, SLOT * (c % 2), c // 2, c) if first else (n, SLOT * i, n // 4, 4 * (n // 4) + i)

    with ExitStack() as ctx:
        t = Buffers(nc, ctx, f"l{layer}")
        cols = t.sb("cols", [P, NC])
        rows = t.sb("rows", [P, NR])
        w = t.sb("w", [P, 2, KT, NW], F32R)
        w_raw = t.sb("w_raw", [P, KT, NW])
        cT = t.sb("cT", [P, 2, KT, TOK], F32R)
        mask = t.sb("mask", [P, TOK])
        mask_raw = t.sb("mask_raw", [P, TOK // 4], I32)
        full = t.sb("full", [P, 2, TOK])
        top = t.sb("top", [P, 2, TOK], F32R)
        qk = t.sb("qk", [P, QT + KTILES, TOK], F32R)
        vt = t.sb("vt", [P, 2, VC])
        v = t.sb("v", [P, GROUP, KV, 32])
        s_sb = t.sb("s_sb", [P, 3, TOK])
        peak = t.sb("peak", [P, H, GROUP])
        probs = t.sb("probs", [P, 8, TOK])
        o_sb = t.sb("o_sb", [P, 2, TOK])
        rden = t.sb("rden", [P, NQD, GROUP, 4])
        att = t.sb("att", [P, GROUP, D])
        attT = t.sb("attT", [P, 2, KT, TOK], F32R)
        xb = t.sb("xb", [P, GROUP, D])
        y = t.sb("y", [P, GROUP, D])
        yn = t.sb("yn", [P, GROUP, D])
        ln = TokenNorm(t, 1e-5 if first else None, cols[:, C_G:C_G + KT] if first else None,
                       cols[:, C_B:C_B + KT] if first else None)
        psS = [t.bank(f"psS{i}") for i in range(2)]
        psT = [t.bank(f"psT{i}") for i in range(2)]
        psO, psN = t.bank("psO"), t.bank("psN")
        psW = [t.bank(f"psW{i}") for i in range(2)]
        (weights, w_hi, w_lo, loaded, mask_in, mask_set, proj, freed, topped, stacked, v_in, v_set, v_ones, scored,
         masked, peaked, eased, turned, expd, pved, o_out, o_turned, r_done, normed, a_turned, a_hi, a_lo, outp,
         x_biased, done, y_stats, y_mean, y_shift, y_rstd, y_normed, y_scaled, y_set, stored, started) = [
            t.sem(n) for n in ("weights w_hi w_lo loaded mask_in mask_set proj freed topped stacked v_in v_set v_ones "
                               "scored masked peaked eased turned expd pved o_out o_turned r_done normed a_turned "
                               "a_hi a_lo outp x_biased done y_stats y_mean y_shift y_rstd y_normed y_scaled y_set "
                               "stored started").split()]
        block = ctx.enter_context(nc.Block())

        def group(g):
            return bass.ds(g * GROUP, GROUP)

        @block.sync
        def _(sp):
            sp.dma_start(w_raw[:, :, :], w_dram).then_inc(weights, 16)
            sp.dma_start(cols[:, :], cols_dram).then_inc(weights, 16)
            sp.dma_start(rows[:, :], rows_dram.to_broadcast([P, NR])).then_inc(weights, 16)
            with sp.Fori(0, NG) as g:
                sp.wait_ge(done, g + 1)
                sp.wait_ge(weights, 48)
                sp.dma_start(cT[:, :, :, :].rearrange("p s k n -> p (s k n)").bitcast(F32),
                             ctxT_dram[bass.ds(g, 1)].rearrange("a p n -> p (a n)")).then_inc(loaded, 16)
                if first:
                    sp.dma_start(mask_raw[:, :], mask_dram[bass.ds(g, 1)].to_broadcast([P, TOK // 4]))\
                        .then_inc(mask_in, 16)
                else:
                    sp.dma_start(mask[:, :].rearrange("p (b k) -> p b k", b=GROUP),
                                 mask_dram[group(g)].rearrange("b q k -> q b k")).then_inc(mask_in, 16)
                    sp.wait_ge(y_set, g + 1)
                    sp.wait_ge(weights, 48)
                    sp.dma_start(out_dram[group(g)].rearrange("b q d -> q b d"), y[:, :, :]).then_inc(stored, 16)
            if not first:
                sp.wait_ge(stored, 16 * NG)

        @block.gpsimd
        def _(pool):
            pool.memset(v[:, :, :, :], 0.0).then_inc(v_ones, 1)
            pool.wait_ge(v_ones, 1)
            pool.memset(v[:, :, :, DH:DH + 1], 1.0).then_inc(v_ones, 1)
            ln.pool_setup(pool)
            pool.wait_ge(weights, 48)
            with pool.Fori(0, NG) as g:
                pool.wait_ge(done, g + 1)
                pool.wait_ge(ln.s_power_set, 1)
                if first:
                    ln.pool_rstd(pool, g)
                pool.tensor_tensor(xb[:, :, :], X[:, group(g), :],
                                   rows[:, R_O:R_O + D].rearrange("p (a d) -> p a d", a=1)
                                   .to_broadcast([P, GROUP, D]), ALU.add).then_inc(x_biased, 1)
                for c in range(H):
                    pool.wait_ge(peaked, g * H + c + 1)
                    s = s_sb[:, c % 3].rearrange("p (b k) -> p b k", b=GROUP)
                    pool.tensor_tensor(s, s, peak[:, c].rearrange("p (b a) -> p b a", a=1)
                                       .to_broadcast([P, GROUP, P]), ALU.subtract).then_inc(eased, 1)
                if not first:
                    pool.wait_ge(y_mean, g * GROUP + GROUP)
                    pool.sem_inc(ln.s_gate, 1)
                    pool.tensor_scalar(ln.shifted[:, :], ln.mean_var[:, :, 1], 1e-6, 1.0, ALU.add, ALU.mult)\
                        .then_inc(y_shift, 1)
                    pool.wait_ge(y_shift, g + 1)
                    pool.tensor_tensor(ln.rstd[:, :], ln.shifted[:, :], ln.power[:, :], ALU.pow).then_inc(y_rstd, 1)
                    pool.wait_ge(y_normed, g * GROUP + GROUP)
                    pool.tensor_tensor(yn[:, :, :], yn[:, :, :],
                                       rows[:, R_G:R_G + D].rearrange("p (a d) -> p a d", a=1)
                                       .to_broadcast([P, GROUP, D]), ALU.mult).then_inc(y_scaled, 1)
                    pool.wait_ge(y_scaled, g + 1)
                    pool.tensor_tensor(y[:, :, :], yn[:, :, :],
                                       rows[:, R_B:R_B + D].rearrange("p (a d) -> p a d", a=1)
                                       .to_broadcast([P, GROUP, D]), ALU.add).then_inc(y_set, 1)

        @block.scalar
        def _(act):
            def evac(g, n):
                act.wait_ge(pved, g * NQD + n + 1)
                if n >= 2:
                    act.wait_ge(o_turned, g * NQD + n - 1)
                act.activation(o_sb[:, n % 2], psO[:, :], ACT.Copy).then_inc(o_out, 1)

            act.wait_ge(weights, 48)
            act.activation(w[:, 0], w_raw[:, :, :], ACT.Copy).then_inc(w_hi, 1)
            with act.Fori(0, NG) as g:
                act.wait_ge(done, g + 1)
                ln.act_affine(act, g, psW)
                for u in range(USES):
                    act.wait_ge(proj, g * USES + u + 1)
                    if u < QT + KTILES:
                        if u >= 2:
                            act.wait_ge(stacked, g * (QT + KTILES) + u - 1)
                        act.activation(full[:, u % 2], psW[u % 2][:, :], ACT.Identity,
                                       bias=cols[:, C_BIAS + u:C_BIAS + u + 1]).then_inc(freed, 1)
                    else:
                        b = u - QT - KTILES
                        if b >= 2:
                            act.wait_ge(v_set, g * GROUP + b - 1)
                        act.activation(vt[:, b % 2], psW[u % 2][:, 0:VC], ACT.Copy).then_inc(freed, 1)
                for c in range(H):
                    act.wait_ge(turned, g * H + c + 1)
                    if c >= 8:
                        act.wait_ge(pved, g * NQD + c // 4 - 1)
                    act.activation(probs[:, c % 8], psT[c % 2][:, :], ACT.Exp).then_inc(expd, 1)
                    if c % 4 == 3 and c >= 7:
                        evac(g, c // 4 - 1)
                evac(g, NQD - 1)
                for k in range(KT):
                    act.wait_ge(a_turned, g * KT + k + 1)
                    act.activation(attT[:, 0, k], psT[k][:, :], ACT.Copy).then_inc(a_hi, 1)

        @block.vector
        def _(dve):
            dve.wait_ge(w_hi, 1)
            dve.tensor_tensor(w[:, 1], w_raw[:, :, :], w[:, 0].bitcast(F32), ALU.subtract).then_inc(w_lo, 1)
            dve.wait_ge(w_lo, 1)
            dve.wait_ge(v_ones, 2)
            dve.memset(peak[:, :, :], 0.0).then_inc(done, 1)
            with dve.Fori(0, NG) as g:
                dve.wait_ge(done, g + 1)

                def x(b):
                    return X[:, bass.ds(g * GROUP + b, 1), :].rearrange("p a d -> p (a d)")

                if first:
                    ln.dve_statistics(dve, g, x)
                ln.dve_normalise(dve, g, x)
                ln.dve_lo(dve, g)
                dve.wait_ge(mask_in, g * 16 + 16)
                if first:
                    dve.tensor_scalar(mask[:, :], mask_raw[:, :].bitcast(U8), -1.0, F32_LOWEST, ALU.add, ALU.mult)\
                        .then_inc(mask_set, 1)
                for u in range(QT + KTILES):
                    dve.wait_ge(freed, g * USES + u + 1)
                    dve.tensor_copy(top[:, u % 2], full[:, u % 2]).then_inc(topped, 1)
                    dve.wait_ge(topped, g * (QT + KTILES) + u + 1)
                    j = 0 if u < QT else 1
                    dve.scalar_tensor_tensor(qk[:, u], top[:, u % 2].bitcast(F32), cols[:, C_MASK + j:C_MASK + j + 1],
                                             full[:, u % 2], ALU.mult, ALU.add).then_inc(stacked, 1)
                for b in range(GROUP):
                    dve.wait_ge(freed, g * USES + QT + KTILES + b + 1)
                    dve.tensor_tensor(v[:, b, :, 0:DH], vt[:, b % 2].rearrange("p (h d) -> p h d", h=KV),
                                      rows[:, R_V:R_V + VC].rearrange("p (h d) -> p h d", h=KV), ALU.add)\
                        .then_inc(v_set, 1)
                if first:
                    dve.wait_ge(mask_set, g + 1)

                def norm(n):
                    dve.wait_ge(o_turned, g * NQD + n + 1)
                    o = psN[:, :].rearrange("p (b i c) -> p b i c", b=GROUP, i=4)
                    dve.reciprocal(rden[:, n], o[:, :, :, DH]).then_inc(r_done, 1)
                    dve.wait_ge(r_done, g * NQD + n + 1)
                    if first:
                        dst = att[:, :, n * 64:(n + 1) * 64].rearrange("p b (i d) -> p b i d", i=4)
                    else:
                        dst = att[:, :, (n // 4) * P:(n // 4 + 1) * P]\
                            .rearrange("p b (i m d) -> p b i m d", i=4, m=4)[:, :, :, n % 4, :]
                    dve.tensor_tensor(dst, o[:, :, :, 0:DH],
                                      rden[:, n].rearrange("p b (i a) -> p b i a", a=1)
                                      .to_broadcast([P, GROUP, 4, DH]), ALU.mult).then_inc(normed, 1)

                for c in range(H):
                    dve.wait_ge(scored, g * H + c + 1)
                    if c >= 3:
                        dve.wait_ge(turned, g * H + c - 2)
                    dve.scalar_tensor_tensor(s_sb[:, c % 3], psS[c % 2][:, :], SCALE, mask[:, :], ALU.mult, ALU.add)\
                        .then_inc(masked, 1)
                    dve.wait_ge(masked, g * H + c + 1)
                    dve.tensor_reduce(peak[:, c], s_sb[:, c % 3].rearrange("p (b k) -> p b k", b=GROUP), AX.X,
                                      ALU.max).then_inc(peaked, 1)
                    if c % 4 == 3 and c >= 11:
                        norm(c // 4 - 2)
                norm(NQD - 2)
                norm(NQD - 1)
                for k in range(KT):
                    dve.wait_ge(a_hi, g * KT + k + 1)
                    dve.tensor_tensor(attT[:, 1, k], psT[k][:, :], attT[:, 0, k].bitcast(F32), ALU.subtract)\
                        .then_inc(a_lo, 1)
                dve.wait_ge(x_biased, g + 1)
                for m in range(2):
                    dve.wait_ge(outp, g * 2 + m + 1)
                    o = psS[m][:, :].rearrange("p (b d) -> p b d", b=2)
                    if first:
                        dst = X[:, bass.ds(g * GROUP + 2 * m, 2), :]
                        ins = dve.tensor_tensor(dst, o, xb[:, 2 * m:2 * m + 2], ALU.add)
                        if m == 1:
                            ins.then_inc(done, 1)
                    else:
                        dve.tensor_tensor(xb[:, 2 * m:2 * m + 2], o, xb[:, 2 * m:2 * m + 2], ALU.add)\
                            .then_inc(y_stats, 1)
                if not first:
                    dve.wait_ge(y_stats, g * (2 + GROUP) + 2)
                    for b in range(GROUP):
                        dve.bn_stats(ln.stats[:, b], xb[:, b]).then_inc(y_stats, 1)
                    for b in range(GROUP):
                        dve.wait_ge(y_stats, g * (2 + GROUP) + 2 + b + 1)
                        dve.sem_inc(ln.s_gate, 1)
                        dve.bn_aggr(ln.mean_var[:, b], ln.stats[:, b]).then_inc(y_mean, 1)
                    dve.wait_ge(y_rstd, g + 1)
                    for b in range(GROUP):
                        dve.tensor_scalar(yn[:, b], xb[:, b], ln.mean_var[:, b, 0:1], ln.rstd[:, b:b + 1],
                                          ALU.subtract, ALU.mult).then_inc(y_normed, 1)
                    dve.wait_ge(stored, g * 16 + 16)
                    dve.memset(ln.shifted[:, 0:1], 0.0).then_inc(done, 1)

        @block.tensor
        def _(pe):
            pe.wait_ge(w_lo, 1)
            with pe.Fori(0, NG) as g:
                pe.wait_ge(done, g + 1)
                ln.pe_turn(pe, g, psW, ident)
                ln.pe_ready(pe, g)
                pe.wait_ge(loaded, g * 16 + 16)
                for u in range(USES):
                    if u >= 2:
                        pe.wait_ge(freed, g * USES + u - 1)
                    for k in range(KT):
                        if u < QT + KTILES:
                            src = ln.hT if u < QT else cT
                            at = NQ + u * P
                            ins = mm3(pe, psW[u % 2][:, :], lambda s: w[:, s, k, at:at + P], lambda s: src[:, s, k],
                                      k == 0, k == KT - 1)
                        else:
                            b = u - QT - KTILES
                            ins = mm3(pe, psW[u % 2][:, 0:VC], lambda s: cT[:, s, k, b * P:(b + 1) * P],
                                      lambda s: w[:, s, k, NV:NV + VC], k == 0, k == KT - 1)
                    ins.then_inc(proj, 1)
                pe.wait_ge(stacked, g * (QT + KTILES) + QT + KTILES)

                def scores(c):
                    qt, row, kt, _ = place(c)
                    if c >= 2:
                        pe.wait_ge(masked, g * H + c - 1)
                    for b in range(GROUP):
                        at = slice(b * P, (b + 1) * P)
                        ins = pe.matmul(psS[c % 2][:, at], qk[row:row + SLOT, qt, at], qk[row:row + SLOT, QT + kt, at],
                                        start=True, stop=True)
                    ins.then_inc(scored, 1)

                def turn(c):
                    pe.wait_ge(eased, g * H + c + 1)
                    if c >= 2:
                        pe.wait_ge(expd, g * H + c - 1)
                    for b in range(GROUP):
                        at = slice(b * P, (b + 1) * P)
                        ins = pe.transpose(psT[c % 2][:, at], s_sb[:, c % 3, at], ident[:, :])
                    ins.then_inc(turned, 1)

                def pv(n):
                    pe.wait_ge(expd, g * H + 4 * (n + 1))
                    if n >= 1:
                        pe.wait_ge(o_out, g * NQD + n)
                    else:
                        pe.wait_ge(v_set, g * GROUP + GROUP)
                    for b in range(GROUP):
                        at = slice(b * P, (b + 1) * P)
                        for i in range(4):
                            c = 4 * n + i
                            ins = pe.matmul(psO[32 * i:32 * i + 32, at], v[:, b, place(c)[3], :], probs[:, c % 8, at],
                                            start=True, stop=True)
                    ins.then_inc(pved, 1)

                def turn_out(n):
                    pe.wait_ge(o_out, g * NQD + n + 1)
                    if n >= 1:
                        pe.wait_ge(normed, g * NQD + n)
                    for b in range(GROUP):
                        at = slice(b * P, (b + 1) * P)
                        ins = pe.transpose(psN[:, at], o_sb[:, n % 2, at], ident[:, :])
                    ins.then_inc(o_turned, 1)

                for step in range(H + 6):
                    if step < H:
                        scores(step)
                    if 0 <= step - 2 < H:
                        turn(step - 2)
                    n, r = divmod(step - 7, 4)
                    if r == 0 and 0 <= n < NQD:
                        pv(n)
                    n, r = divmod(step - 9, 4)
                    if r == 0 and 0 <= n < NQD:
                        turn_out(n)
                pe.wait_ge(normed, g * NQD + NQD)
                for k in range(KT):
                    for b in range(GROUP):
                        ins = pe.transpose(psT[k][:, b * P:(b + 1) * P], att[:, b, k * P:(k + 1) * P], ident[:, :])
                    ins.then_inc(a_turned, 1)
                pe.wait_ge(a_lo, g * KT + KT)
                for b in range(GROUP):
                    for k in range(KT):
                        ins = mm3(pe, psS[b // 2][:, (b % 2) * D:(b % 2 + 1) * D],
                                  lambda s: attT[:, s, k, b * P:(b + 1) * P], lambda s: w[:, s, k, NO:NO + D],
                                  k == 0, k == KT - 1)
                    if b % 2:
                        ins.then_inc(outp, 1)


def mlp_phase(nc, name, gelu, X, w_dram, cols_dram, rows_dram, ident):
    F = 4 * D
    FT = F // P
    NF, NP_ = 0, KT * F
    NW = NP_ + FT * D
    C_B, C_G, C_O = 0, FT, FT + KT
    NC = C_O + KT
    with ExitStack() as ctx:
        t = Buffers(nc, ctx, name)
        cols = t.sb("cols", [P, NC])
        rows = t.sb("rows", [P, D])
        w = t.sb("w", [P, 2, NW], F32R)
        w_raw = t.sb("w_raw", [P, NW])
        ln = TokenNorm(t, 1e-5, cols[:, C_G:C_G + KT], cols[:, C_O:C_O + KT])
        act_out = t.sb("act_out", [P, 2, TOK])
        y = t.sb("y", [P, 2, FT, TOK], F32R)
        xb = t.sb("xb", [P, GROUP, D])
        psW = [t.bank(f"psW{i}") for i in range(2)]
        psH = [t.bank(f"psH{i}") for i in range(2)]
        psO = [t.bank(f"psO{i}") for i in range(2)]
        (weights, w_hi, w_lo, fc, gelued, y_hi, y_lo, outp, x_biased, done) = [
            t.sem(n) for n in "weights w_hi w_lo fc gelued y_hi y_lo outp x_biased done".split()]
        block = ctx.enter_context(nc.Block())

        @block.sync
        def _(sp):
            sp.dma_start(w_raw[:, :], w_dram).then_inc(weights, 16)
            sp.dma_start(cols[:, :], cols_dram).then_inc(weights, 16)
            sp.dma_start(rows[:, :], rows_dram.to_broadcast([P, D])).then_inc(weights, 16)

        @block.gpsimd
        def _(pool):
            ln.pool_setup(pool)
            pool.wait_ge(weights, 48)
            with pool.Fori(0, NG) as g:
                pool.wait_ge(done, g + 1)
                ln.pool_rstd(pool, g)
                pool.tensor_tensor(xb[:, :, :], X[:, bass.ds(g * GROUP, GROUP), :],
                                   rows[:, :].rearrange("p (a d) -> p a d", a=1).to_broadcast([P, GROUP, D]),
                                   ALU.add).then_inc(x_biased, 1)

        @block.scalar
        def _(act):
            act.wait_ge(weights, 48)
            act.activation(w[:, 0], w_raw[:, :], ACT.Copy).then_inc(w_hi, 1)
            with act.Fori(0, NG) as g:
                act.wait_ge(done, g + 1)
                ln.act_affine(act, g, psW)
                for n in range(FT):
                    act.wait_ge(fc, g * FT + n + 1)
                    if n >= 2:
                        act.wait_ge(y_lo, g * FT + n - 1)
                    act.activation(act_out[:, n % 2], psH[n % 2][:, :], gelu, bias=cols[:, C_B + n:C_B + n + 1])\
                        .then_inc(gelued, 1)

        @block.vector
        def _(dve):
            dve.wait_ge(w_hi, 1)
            dve.tensor_tensor(w[:, 1], w_raw[:, :], w[:, 0].bitcast(F32), ALU.subtract).then_inc(w_lo, 1)
            dve.wait_ge(w_lo, 1)
            dve.memset(act_out[:, 0, 0:1], 0.0).then_inc(done, 1)
            with dve.Fori(0, NG) as g:
                dve.wait_ge(done, g + 1)

                def x(b):
                    return X[:, bass.ds(g * GROUP + b, 1), :].rearrange("p a d -> p (a d)")

                ln.dve_statistics(dve, g, x)
                ln.dve_normalise(dve, g, x)
                ln.dve_lo(dve, g)
                for n in range(FT):
                    dve.wait_ge(gelued, g * FT + n + 1)
                    dve.tensor_copy(y[:, 0, n], act_out[:, n % 2]).then_inc(y_hi, 1)
                    dve.wait_ge(y_hi, g * FT + n + 1)
                    dve.tensor_tensor(y[:, 1, n], act_out[:, n % 2], y[:, 0, n].bitcast(F32), ALU.subtract)\
                        .then_inc(y_lo, 1)
                dve.wait_ge(x_biased, g + 1)
                for m in range(2):
                    dve.wait_ge(outp, g * 2 + m + 1)
                    ins = dve.tensor_tensor(X[:, bass.ds(g * GROUP + 2 * m, 2), :],
                                            psO[m][:, :].rearrange("p (b d) -> p b d", b=2), xb[:, 2 * m:2 * m + 2],
                                            ALU.add)
                    if m == 1:
                        ins.then_inc(done, 1)

        @block.tensor
        def _(pe):
            pe.wait_ge(w_lo, 1)
            with pe.Fori(0, NG) as g:
                pe.wait_ge(done, g + 1)
                ln.pe_turn(pe, g, psW, ident)
                ln.pe_ready(pe, g)
                for n in range(FT):
                    if n >= 2:
                        pe.wait_ge(gelued, g * FT + n - 1)
                    for k in range(KT):
                        at = NF + k * F + n * P
                        ins = mm3(pe, psH[n % 2][:, :], lambda s: w[:, s, at:at + P], lambda s: ln.hT[:, s, k],
                                  k == 0, k == KT - 1)
                    ins.then_inc(fc, 1)
                pe.wait_ge(y_lo, g * FT + FT)
                for b in range(GROUP):
                    for n in range(FT):
                        at = NP_ + n * D
                        ins = mm3(pe, psO[b // 2][:, (b % 2) * D:(b % 2 + 1) * D],
                                  lambda s: y[:, s, n, b * P:(b + 1) * P], lambda s: w[:, s, at:at + D],
                                  n == 0, n == FT - 1)
                    if b % 2:
                        ins.then_inc(outp, 1)


def wide_phase(nc, X, ctxT_dram, d, ident):
    H, QH = 16, 4
    NQD = H // QH
    SCALE = float(P) ** -0.5
    PART = KT * QH * P
    C_BQ, C_BK, C_G, C_B, C_EK, C_EV, C_BV = 0, 16, 32, 34, 36, 52, 68
    NC = 84
    AHEAD = 7
    CREDIT = 8
    SLOTS = 6
    LAST = H + 3
    with ExitStack() as ctx:
        t = Buffers(nc, ctx, "l2")
        cols = t.sb("cols", [P, NC])
        bo = t.sb("bo", [1, D])
        raw = t.sb("raw", [P, 2, 3 * PART])
        raw_o = t.sb("raw_o", [P, 2, PART])
        w = t.sb("w", [P, 2, 2, 4 * PART], F32R)
        qk = t.sb("qk", [P, 2 * SLOTS, TOK])
        v = t.sb("v", [P, 2, GROUP, QH, P + 1])
        cT = t.sb("cT", [P, 2, KT, TOK], F32R)
        s_sb = t.sb("s_sb", [P, 2, TOK])
        probs = t.sb("probs", [P, 3, TOK])
        att = t.sb("att", [P, 2, TOK])
        attT = t.sb("attT", [P, 2, QH, TOK], F32R)
        extra = t.sb("extra", [P, GROUP, H])
        top = t.sb("top", [P, H, GROUP])
        peak = t.sb("peak", [P, H, GROUP])
        gap = t.sb("gap", [P, H, GROUP])
        extra_p = t.sb("extra_p", [P, H, GROUP])
        den = t.sb("den", [P, H, GROUP])
        rden = t.sb("rden", [P, H, GROUP])
        norm_p = t.sb("norm_p", [P, GROUP, H + 1])
        norm_pT = t.sb("norm_pT", [H + 1, TOK])
        u = t.sb("u", [P, KT, H])
        u_parts = t.sb("u_parts", [P, 2, KT, H], F32R)
        ones = t.sb("ones", [P, P])
        c_prod = t.sb("c_prod", [P, H])
        c_row = t.sb("c_row", [P, H])
        dv = t.sb("dv", [P, H * (H + 1)])
        pick = t.sb("pick", [1, H + 1])
        credit = t.sb("credit", [P, 1])
        big_g = t.sb("big_g", [H + 1, D])
        ln = TokenNorm(t, 1e-5, cols[:, C_G:C_G + KT], cols[:, C_B:C_B + KT],
                       att[:, :, :].rearrange("p a (b d) -> p (a b) d", b=2), s_sb)
        psS = [t.bank(f"psS{n}") for n in range(2)]
        psT = [t.bank(f"psT{n}") for n in range(2)]
        psV = ctx.enter_context(nc.psum_tensor("l2_psV", [P, GROUP, 256], F32))
        psW = [t.bank(f"psW{n}") for n in range(2)]
        whole = qk[:, 0:2 * QH].rearrange("p h n -> p (h n)")
        ek_rows = qk[:, 2 * QH:3 * QH].rearrange("p h n -> p (h n)")
        (consts, params, wq_in, wo_in, u_prod, u_sum, u_hi, u_set, c_mul, c_sum, c_set, dv_set, g_sum,
         g_set, w_hi, w_lo, ctx_in, extra_sum, extra_set, q_sum, q_set, k_sum, k_set, v_sum, v_set, scored,
         topped, peaked, eased, gapped, extra_exp, turned, expd, pved, den_set, r_done, np_set, normed, a_turned,
         a_hi, a_lo, outp, added, np_turned, npT_set, done, gate) = [
            t.sem(n) for n in ("consts params wq_in wo_in u_prod u_sum u_hi u_set c_mul c_sum c_set dv_set "
                               "g_sum g_set w_hi w_lo ctx_in extra_sum extra_set q_sum q_set k_sum k_set "
                               "v_sum v_set scored topped peaked eased gapped extra_exp turned expd pved den_set "
                               "r_done np_set normed a_turned a_hi a_lo outp added np_turned npT_set done gate").split()]
        qkv_in = [t.sem(f"qkv_in{n}") for n in range(2)]
        o_in = [t.sem(f"o_in{n}") for n in range(2)]
        block = ctx.enter_context(nc.Block())
        qkv_dram, o_dram = d["l2_qkv"], d["l2_o"]

        def uses():
            order = [("l", 0), ("l", 1), ("x", 0)]
            for n in range(4):
                order += [("q", n), ("k", n), ("v", n)]
            for n in range(LAST):
                if output_at(n) is not None:
                    order += [("o", 2 * output_at(n)), ("o", 2 * output_at(n) + 1)]
                if 0 <= n - 3 < H:
                    order += [("t", n - 3)]
                if n + 4 < H:
                    order += [("q", n + 4), ("k", n + 4), ("v", n + 4)]
            return order + [("o", 2 * NQD - 2), ("o", 2 * NQD - 1)]

        def output_at(n):
            Q, i = divmod(n - 7, 4)
            return Q if i == 0 and 0 <= Q < NQD - 1 else None

        def flat(ap):
            return ap.rearrange("a p n -> p (a n)")

        @block.sync
        def _(sp):
            def load(index, r, Q, stream):
                sp.wait_ge(w_lo, stream * 4 + 3)
                sp.dma_start(raw[:, Q % 2], flat(qkv_dram[index])).then_inc(qkv_in[Q % 2], 16)
                sp.wait_ge(w_lo, stream * 4 + 7)
                sp.dma_start(raw_o[:, Q % 2], flat(o_dram[index])).then_inc(o_in[Q % 2], 16)

            with sp.Fori(0, 2) as a:
                with sp.Fori(0, NG) as g:
                    for Q in range(NQD):
                        load(bass.ds(a * NQD + Q, 1), a * NG + g, Q, (a * NG + g) * NQD + Q)
            for Q in range(2):
                load(slice(Q, Q + 1), 2 * NG, Q, 2 * NG * NQD + Q)
            for n in range(2):
                sp.wait_ge(qkv_in[n], 16 * (NG * NQD + 1))
                sp.wait_ge(o_in[n], 16 * (NG * NQD + 1))

        @block.gpsimd
        def _(pool):
            pool.memset(dv[:, :], 0.0).then_inc(consts, 1)
            pool.memset(pick[:, :], 0.0).then_inc(consts, 1)
            pool.memset(ones[:, :], 1.0).then_inc(consts, 1)
            pool.memset(norm_p[:, :, :], 1.0).then_inc(consts, 1)
            pool.memset(v[:, :, :, :, P:P + 1], 1.0).then_inc(consts, 1)
            pool.wait_ge(consts, 5)
            pool.memset(pick[:, H:H + 1], 1.0).then_inc(consts, 1)
            ln.pool_setup(pool)
            pool.memset(credit[:, :], 0.0).then_inc(w_lo, CREDIT)

            def split(parity, part):
                src = raw[:, parity, part * PART:(part + 1) * PART] if part < 3 else raw_o[:, parity]
                at = slice(part * PART, (part + 1) * PART)
                pool.tensor_tensor(w[:, parity, 1, at], src, w[:, parity, 0, at].bitcast(F32), ALU.subtract)\
                    .then_inc(w_lo, 1)

            for n, (parity, part) in enumerate([(0, 0), (0, 1), (0, 2), (1, 0), (1, 1), (1, 2), (0, 3)]):
                pool.wait_ge(w_hi, n + 1)
                split(parity, part)
            with pool.Fori(0, 2) as a:
                with pool.Fori(0, NG) as g:
                    r = a * NG + g
                    ln.pool_rstd(pool, r)
                    for n in range(H):
                        Q, i = divmod(n, 4)
                        pool.wait_ge(w_hi, r * H + AHEAD + n + 1)
                        split(Q % 2 if i < 3 else (Q + 1) % 2, i)

        @block.scalar
        def _(act):
            def split(parity, part):
                src = raw[:, parity, part * PART:(part + 1) * PART] if part < 3 else raw_o[:, parity]
                act.activation(w[:, parity, 0, part * PART:(part + 1) * PART], src, ACT.Copy).then_inc(w_hi, 1)

            for parity in range(2):
                act.wait_ge(qkv_in[parity], 16)
                for part in range(3):
                    split(parity, part)
            act.wait_ge(o_in[0], 16)
            split(0, 3)
            with act.Fori(0, 2) as a:
                act.wait_ge(done, a * NG + 1)
                act.wait_ge(consts, 6)
                act.dma_start(cols[:, :], flat(d["l2_cols"][bass.ds(a, 1)])).then_inc(params, 16)
                act.dma_start(bo[:, :], d["l2_bo"][bass.ds(a, 1)]).then_inc(params, 16)
                act.dma_start(ek_rows, d["l2_ek"][bass.ds(a, 1)].to_broadcast([P, H * P])).then_inc(params, 16)
                act.dma_start(whole.rearrange("p (q n) -> p q n", q=NQD),
                              qkv_dram[bass.ds(a * NQD, NQD), :, 0:PART].rearrange("q p n -> p q n"))\
                    .then_inc(wq_in, 16)
                act.wait_ge(u_sum, a * NQD + NQD)
                act.wait_ge(consts, 6)
                act.dma_start(whole.rearrange("p (q n) -> p q n", q=NQD),
                              o_dram[bass.ds(a * NQD, NQD)].rearrange("q p n -> p q n")).then_inc(wo_in, 16)
                act.wait_ge(g_sum, a + 1)
                act.activation(big_g[:, :], psW[1][0:H + 1, 0:D], ACT.Copy).then_inc(g_set, 1)
                with act.Fori(0, NG) as g:
                    r = a * NG + g
                    act.wait_ge(done, r + 1)
                    act.dma_start(cT[:, :, :, :].rearrange("p s k n -> p (s k n)").bitcast(F32),
                                  flat(ctxT_dram[bass.ds(g, 1)])).then_inc(ctx_in, 16)
                    ln.act_affine(act, r, psW)

                    def project(n, bank):
                        Q, i = divmod(n, 4)
                        act.wait_ge(q_sum, r * H + n + 1)
                        act.activation(qk[:, n % SLOTS], psW[bank["q", n]][:, :], ACT.Identity,
                                       bias=cols[:, C_BQ + n:C_BQ + n + 1]).then_inc(q_set, 1)
                        act.wait_ge(k_sum, r * H + n + 1)
                        act.activation(qk[:, SLOTS + n % SLOTS], psW[bank["k", n]][:, :], ACT.Identity,
                                       bias=cols[:, C_BK + n:C_BK + n + 1]).then_inc(k_set, 1)

                    def values(n, bank):
                        Q, i = divmod(n, 4)
                        act.wait_ge(v_sum, r * H + n + 1)
                        if Q >= 2:
                            act.wait_ge(pved, r * H + 4 * (Q - 1))
                        act.activation(v[:, Q % 2, i, :, 0:P], psW[bank["v", n]][:, :]
                                       .rearrange("p (h n) -> p h n", h=QH), ACT.Copy).then_inc(v_set, 1)

                    bank = {use: n % 2 for n, use in enumerate(uses())}
                    for n in range(4):
                        project(n, bank)
                        values(n, bank)
                    for n in range(LAST):
                        if 0 <= n - 3 < H:
                            act.wait_ge(a_turned, r * H + n - 2)
                            act.activation(attT[:, 0, (n - 3) % 4], psW[bank["t", n - 3]][:, :], ACT.Copy)\
                                .then_inc(a_hi, 1)
                        if n + 4 < H:
                            project(n + 4, bank)
                        if 0 <= n - 1 < H:
                            c = n - 1
                            act.wait_ge(gapped, r * H + c + 1)
                            act.activation(extra_p[:, c], gap[:, c], ACT.Exp, scale=SCALE).then_inc(extra_exp, 1)
                            act.wait_ge(turned, r * H + c + 1)
                            if c >= 3:
                                act.wait_ge(pved, r * H + c - 2)
                            act.activation(probs[:, c % 3], psT[c % 2][:, :], ACT.Exp, scale=SCALE).then_inc(expd, 1)
                        if n + 4 < H:
                            values(n + 4, bank)
                        if n < H:
                            Q, i = divmod(n, 4)
                            if i < 3:
                                act.wait_ge(qkv_in[Q % 2], r * (NQD // 2 * 16) + 16 * (Q // 2 + 2))
                                split(Q % 2, i)
                            else:
                                act.wait_ge(o_in[(Q + 1) % 2], r * (NQD // 2 * 16) + 16 * ((Q + 1) // 2 + 1))
                                if Q >= 1:
                                    act.wait_ge(outp, r * 2 * NQD + 2 * Q)
                                split((Q + 1) % 2, 3)
                    act.wait_ge(np_turned, r + 1)
                    act.activation(norm_pT[:, :], psT[0][0:H + 1, :], ACT.Copy).then_inc(npT_set, 1)

        @block.vector
        def _(dve):
            dve.wait_ge(consts, 6)
            dve.memset(s_sb[:, 0, 0:1], 0.0).then_inc(done, 1)
            with dve.Fori(0, 2) as a:
                dve.wait_ge(params, a * 48 + 48)
                dve.wait_ge(wq_in, a * 16 + 16)
                for Q in range(NQD):
                    part = whole[:, Q * PART:(Q + 1) * PART].rearrange("p (c n) -> p c n", c=KT)
                    dve.tensor_tensor(part, part, ek_rows[:, Q * QH * P:(Q + 1) * QH * P]
                                      .rearrange("p (a n) -> p a n", a=1).to_broadcast([P, KT, QH * P]), ALU.mult)\
                        .then_inc(u_prod, 1)
                for Q in range(NQD):
                    dve.wait_ge(u_prod, a * NQD + Q + 1)
                    dve.tensor_reduce(u[:, :, Q * QH:(Q + 1) * QH], whole[:, Q * PART:(Q + 1) * PART]
                                      .rearrange("p (c h n) -> p c h n", c=KT, h=QH), AX.X, ALU.add)\
                        .then_inc(u_sum, 1)
                dve.wait_ge(u_sum, a * NQD + NQD)
                dve.tensor_copy(u_parts[:, 0], u[:, :, :]).then_inc(u_hi, 1)
                dve.wait_ge(u_hi, a + 1)
                dve.tensor_tensor(u_parts[:, 1], u[:, :, :], u_parts[:, 0].bitcast(F32), ALU.subtract)\
                    .then_inc(u_set, 1)
                dve.tensor_tensor(c_prod[:, :], cols[:, C_BQ:C_BQ + H], cols[:, C_EK:C_EK + H], ALU.mult)\
                    .then_inc(c_mul, 1)
                dve.tensor_tensor(dv[:, 0:H * (H + 1):H + 2], cols[:, C_EV:C_EV + H], cols[:, C_BV:C_BV + H],
                                  ALU.subtract).then_inc(dv_set, 1)
                dve.tensor_copy(dv[:, H:H * (H + 1):H + 1], cols[:, C_BV:C_BV + H]).then_inc(dv_set, 1)
                dve.wait_ge(c_sum, a + 1)
                dve.tensor_copy(c_row[:, :], psW[0][:, 0:H]).then_inc(c_set, 1)
                with dve.Fori(0, NG) as g:
                    r = a * NG + g
                    dve.wait_ge(done, r + 1)

                    def x(b):
                        return X[:, bass.ds(g * GROUP + b, 1), :].rearrange("p a d -> p (a d)")

                    ln.dve_statistics(dve, r, x)
                    ln.dve_normalise(dve, r, x)
                    ln.dve_lo(dve, r)
                    dve.wait_ge(c_set, a + 1)
                    dve.wait_ge(extra_sum, r + 1)
                    bank = {use: n % 2 for n, use in enumerate(uses())}
                    dve.tensor_tensor(extra[:, :, :], psW[bank["x", 0]][:, 0:GROUP * H]
                                      .rearrange("p (b h) -> p b h", b=GROUP),
                                      c_row[:, :].rearrange("p (a h) -> p a h", a=1).to_broadcast([P, GROUP, H]),
                                      ALU.add).then_inc(extra_set, 1)
                    dve.wait_ge(extra_set, r + 1)

                    def add_output(Q):
                        for m in range(2):
                            xm = X[:, bass.ds(g * GROUP + 2 * m, 2), :]
                            if Q >= 1:
                                dve.wait_ge(added, r * 2 * NQD + 2 * Q)
                            dve.wait_ge(outp, r * 2 * NQD + 2 * Q + m + 1)
                            dve.tensor_tensor(xm, psW[bank["o", 2 * Q + m]][:, :].rearrange("p (b d) -> p b d", b=2),
                                              xm, ALU.add).then_inc(added, 1)

                    for n in range(LAST):
                        if output_at(n) is not None:
                            add_output(output_at(n))
                        c = n - 2
                        if 0 <= c < H:
                            dve.wait_ge(pved, r * H + c + 1)
                            dve.wait_ge(extra_exp, r * H + c + 1)
                            dve.tensor_tensor(den[:, c], psV[:, :, P], extra_p[:, c], ALU.add).then_inc(den_set, 1)
                            dve.wait_ge(den_set, r * H + c + 1)
                            dve.reciprocal(rden[:, c], den[:, c]).then_inc(r_done, 1)
                            dve.wait_ge(r_done, r * H + c + 1)
                            dve.tensor_tensor(norm_p[:, :, c], rden[:, c], extra_p[:, c], ALU.mult).then_inc(np_set, 1)
                            if c >= 2:
                                dve.wait_ge(a_turned, r * H + c - 1)
                            dve.tensor_tensor(att[:, c % 2].rearrange("p (b n) -> p b n", b=GROUP), psV[:, :, 0:P],
                                              rden[:, c].rearrange("p (b a) -> p b a", a=1)
                                              .to_broadcast([P, GROUP, P]), ALU.mult).then_inc(normed, 1)
                        c = n - 3
                        if 0 <= c < H:
                            dve.wait_ge(a_hi, r * H + c + 1)
                            dve.tensor_tensor(attT[:, 1, c % 4], psW[bank["t", c]][:, :],
                                              attT[:, 0, c % 4].bitcast(F32), ALU.subtract).then_inc(a_lo, 1)
                        if n < H:
                            dve.wait_ge(scored, r * H + n + 1)
                            s = psS[n % 2][:, :].rearrange("p (b m) -> p b m", b=GROUP)
                            dve.tensor_reduce(top[:, n], s, AX.X, ALU.max).then_inc(topped, 1)
                            dve.wait_ge(topped, r * H + n + 1)
                            dve.tensor_tensor(peak[:, n], top[:, n], extra[:, :, n], ALU.max).then_inc(peaked, 1)
                            dve.wait_ge(peaked, r * H + n + 1)
                            if n >= 2:
                                dve.wait_ge(turned, r * H + n - 1)
                            dve.tensor_tensor(s_sb[:, n % 2].rearrange("p (b m) -> p b m", b=GROUP), s,
                                              peak[:, n].rearrange("p (b a) -> p b a", a=1)
                                              .to_broadcast([P, GROUP, P]), ALU.subtract).then_inc(eased, 1)
                            dve.tensor_tensor(gap[:, n], extra[:, :, n], peak[:, n], ALU.subtract).then_inc(gapped, 1)
                    add_output(NQD - 1)
                    dve.wait_ge(added, r * 2 * NQD + 2 * NQD)
                    dve.memset(s_sb[:, 0, 0:1], 0.0).then_inc(done, 1)

        @block.tensor
        def _(pe):
            pe.wait_ge(consts, 6)
            with pe.Fori(0, 2) as a:
                pe.wait_ge(done, a * NG + 1)
                pe.wait_ge(c_mul, a + 1)
                pe.matmul(psW[0][:, 0:H], ones[:, :], c_prod[:, :], start=True, stop=True).then_inc(c_sum, 1)
                pe.wait_ge(dv_set, a * 2 + 2)
                pe.wait_ge(wo_in, a * 16 + 16)
                for h in range(H):
                    pe.matmul(psW[1][0:H + 1, 0:D], dv[:, h * (H + 1):(h + 1) * (H + 1)],
                              whole[:, h * D:(h + 1) * D], start=h == 0, stop=False)
                pe.matmul(psW[1][0:H + 1, 0:D], pick[:, :], bo[:, :], start=False, stop=True).then_inc(g_sum, 1)
                pe.wait_ge(c_set, a + 1)
                pe.wait_ge(g_set, a + 1)
                pe.wait_ge(u_set, a + 1)
                pe.sem_inc(gate, 1)
                with pe.Fori(0, NG) as g:
                    r = a * NG + g
                    pe.wait_ge(done, r + 1)
                    order = uses()
                    at = {use: n for n, use in enumerate(order)}
                    freed = {"l": (ln.s_affine, KT), "x": (extra_set, 1), "q": (q_set, H), "k": (k_set, H),
                             "v": (v_set, H), "t": (a_lo, H), "o": (added, 2 * NQD)}

                    def bank(kind, n):
                        i = at[kind, n]
                        if i >= 2:
                            kind0, n0 = order[i - 2]
                            sem, per = freed[kind0]
                            pe.wait_ge(sem, r * per + n0 + 1)
                        return psW[i % 2]

                    def project(n):
                        Q, i = divmod(n, 4)
                        if i == 0:
                            pe.wait_ge(w_lo, r * (4 * NQD) + CREDIT + 4 * Q + 3)
                        for kind, part, src, signal in (("q", 0, ln.hT, q_sum), ("k", 1, cT, k_sum)):
                            ps = bank(kind, n)
                            for c in range(KT):
                                col = part * PART + c * QH * P + i * P
                                ins = mm3(pe, ps[:, :], lambda s: w[:, Q % 2, s, col:col + P], lambda s: src[:, s, c],
                                          c == 0, c == KT - 1)
                            ins.then_inc(signal, 1)

                    def values(n):
                        Q, b = divmod(n, 4)
                        ps = bank("v", n)
                        for c in range(KT):
                            col = 2 * PART + c * QH * P
                            ins = mm3(pe, ps[:, :], lambda s: cT[:, s, c, b * P:(b + 1) * P],
                                      lambda s: w[:, Q % 2, s, col:col + QH * P], c == 0, c == KT - 1)
                        ins.then_inc(v_sum, 1)

                    def output(Q):
                        pe.wait_ge(a_lo, r * H + 4 * Q + 4)
                        pe.wait_ge(w_lo, r * (4 * NQD) + CREDIT + 4 * Q + 7)
                        for m in range(2):
                            ps = bank("o", 2 * Q + m)
                            for e in range(2):
                                tok = slice((2 * m + e) * P, (2 * m + e + 1) * P)
                                out = ps[:, e * D:(e + 1) * D]
                                for i in range(QH):
                                    col = 3 * PART + i * D
                                    ins = mm3(pe, out, lambda s: attT[:, s, i, tok],
                                              lambda s: w[:, Q % 2, s, col:col + D],
                                              i == 0, i == QH - 1 and Q < NQD - 1)
                                if Q == NQD - 1:
                                    ins = pe.matmul(out, norm_pT[:, tok], big_g[:, :], start=False, stop=True)
                            ins.then_inc(outp, 1)

                    ln.pe_turn(pe, r, psW, ident)
                    ln.pe_ready(pe, r)
                    ps = bank("x", 0)
                    for b in range(GROUP):
                        for c in range(KT):
                            ins = mm3(pe, ps[:, b * H:(b + 1) * H], lambda s: ln.hT[:, s, c, b * P:(b + 1) * P],
                                      lambda s: u_parts[:, s, c], c == 0, c == KT - 1)
                    ins.then_inc(extra_sum, 1)
                    pe.wait_ge(ctx_in, r * 16 + 16)
                    for n in range(4):
                        project(n)
                        values(n)
                    for n in range(LAST):
                        if 0 <= n - 2 < H:
                            c = n - 2
                            Q, i = divmod(c, 4)
                            pe.wait_ge(expd, r * H + c + 1)
                            if i == 0:
                                pe.wait_ge(v_set, r * H + 4 * (Q + 1))
                            if c >= 1:
                                pe.wait_ge(normed, r * H + c)
                            for b in range(GROUP):
                                ins = pe.matmul(psV[:, b, 0:P + 1], probs[:, c % 3, b * P:(b + 1) * P],
                                                v[:, Q % 2, b, i, :], start=True, stop=True)
                            ins.then_inc(pved, 1)
                        if output_at(n) is not None:
                            output(output_at(n))
                        if 0 <= n - 3 < H:
                            c = n - 3
                            ps = bank("t", c)
                            pe.wait_ge(normed, r * H + c + 1)
                            for b in range(GROUP):
                                ins = pe.transpose(ps[:, b * P:(b + 1) * P], att[:, c % 2, b * P:(b + 1) * P],
                                                   ident[:, :])
                            ins.then_inc(a_turned, 1)
                        if n < H:
                            Q, i = divmod(n, 4)
                            pe.wait_ge(k_set, r * H + n + 1)
                            if n >= 2:
                                pe.wait_ge(eased, r * H + n - 1)
                            for b in range(GROUP):
                                tok = slice(b * P, (b + 1) * P)
                                ins = pe.matmul(psS[n % 2][:, tok], qk[:, n % SLOTS, tok], qk[:, SLOTS + n % SLOTS, tok],
                                                start=True, stop=True)
                            ins.then_inc(scored, 1)
                        if n + 4 < H:
                            project(n + 4)
                        if 0 <= n - 1 < H:
                            c = n - 1
                            pe.wait_ge(eased, r * H + c + 1)
                            if c >= 2:
                                pe.wait_ge(expd, r * H + c - 1)
                            for b in range(GROUP):
                                ins = pe.transpose(psT[c % 2][:, b * P:(b + 1) * P], s_sb[:, c % 2, b * P:(b + 1) * P],
                                                   ident[:, :])
                            ins.then_inc(turned, 1)
                        if n + 4 < H:
                            values(n + 4)
                    pe.wait_ge(np_set, r * H + H)
                    pe.wait_ge(expd, r * H + H)
                    for b in range(GROUP):
                        ins = pe.transpose(psT[0][0:H + 1, b * P:(b + 1) * P], norm_p[:, b, :], ident[:, :])
                    ins.then_inc(np_turned, 1)
                    pe.wait_ge(npT_set, r + 1)
                    output(NQD - 1)



def _columns(parts):
    import numpy as np
    return np.ascontiguousarray(np.concatenate(parts, axis=1))


def _stack_heads(wT, heads, dh, slot, parts=3):
    import numpy as np
    out = np.zeros((wT.shape[0], len(heads) * slot), wT.dtype)
    for i, h in enumerate(heads):
        for r in range(parts):
            out[:, i * slot + r * dh:i * slot + (r + 1) * dh] = wT[:, h * dh:(h + 1) * dh]
    return out


def _lo_rows(slot, dh, part):
    import numpy as np
    m = np.zeros((P, 1), np.float32)
    for i in range(P // slot):
        m[i * slot + part * dh:i * slot + (part + 1) * dh] = -1.0
    return m


def _layer0_arrays(i):
    import numpy as np
    wq, wk = i["L0_xattn_Wq"].T, i["L0_xattn_Wk"].T
    parts = [_stack_heads(wq, range(4 * n, 4 * n + 4), 8, 32) for n in range(4)]
    parts += [_stack_heads(wk, range(4 * n, 4 * n + 4), 8, 32) for n in range(4)]
    parts += [i["L0_xattn_Wv"].T, i["L0_xattn_Wo"].T]
    cols = [_lo_rows(32, 8, 1), _lo_rows(32, 8, 2), i["L0_xattn_bo"][:, None]]
    return {"l0_w": _columns(parts), "l0_cols": _columns(cols)}


def _tiles(w):
    return w.reshape(-1, P, w.shape[1]).transpose(1, 0, 2)


def _per_tile(v):
    return v.reshape(-1, P).T


def _layer1_arrays(i):
    import numpy as np
    g = {k[9:]: v for k, v in i.items() if k.startswith("L1_xattn_")}
    pairs = [range(2 * n, 2 * n + 2) for n in range(8)]
    w = np.concatenate([_stack_heads(g["q_w"], p, 16, 64) for p in pairs]
                       + [_stack_heads(g["k_w"], p, 16, 64) for p in pairs] + [g["v_w"], g["cproj_w"]], axis=1)
    cols = [_lo_rows(64, 16, 1), _lo_rows(64, 16, 2)]
    cols += [_stack_heads(g["q_b"][None], p, 16, 64).T for p in pairs]
    cols += [_stack_heads(g["k_b"][None], p, 16, 64).T for p in pairs]
    cols += [_per_tile(g["ln1_w"]), _per_tile(g["ln1_b"])]
    rows = [g["v_b"], g["cproj_b"], g["ln1_w"], g["ln1_b"]]
    return {"l1_w": _tiles(w), "l1_cols": _columns(cols), "l1_rows": np.concatenate(rows)[None],
            "l1_mask": i["mask_BxS2_bf1"].view(np.int32).reshape(NG, -1)}


def _mlp_arrays(name, fc_w, fc_b, proj_w, proj_b, gamma, beta):
    w = _columns([_tiles(fc_w).reshape(P, -1), _tiles(proj_w).reshape(P, -1)])
    return {name + "_w": w, name + "_cols": _columns([_per_tile(fc_b), _per_tile(gamma), _per_tile(beta)]),
            name + "_rows": proj_b[None]}


def _layer3_arrays(i):
    import numpy as np
    g = {k[9:]: v for k, v in i.items() if k.startswith("L3_xattn_")}
    quads = [[(4 * kt + s) * 4 + m for s in range(4)] for kt in range(2) for m in range(4)]
    kheads = [range(4 * kt, 4 * kt + 4) for kt in range(2)]
    w = np.concatenate([_stack_heads(g["Wq"], q, 8, 32) for q in quads]
                       + [_stack_heads(g["Wk"], k, 8, 32) for k in kheads] + [g["Wv"], g["Wo"]], axis=1)
    cols = [_lo_rows(32, 8, 1), _lo_rows(32, 8, 2)]
    cols += [_stack_heads(g["bq"][None], q, 8, 32).T for q in quads]
    cols += [_stack_heads(g["bk"][None], k, 8, 32).T for k in kheads]
    cols += [_per_tile(g["gamma"]), _per_tile(g["beta"])]
    rows = [g["bv"], g["bo"], g["gamma"], g["beta"]]
    return {"l3_w": _tiles(w), "l3_cols": _columns(cols), "l3_rows": np.concatenate(rows)[None],
            "l3_mask": i["mask_Bx1xSxS2_ff0"].reshape(BATCH, P, P)}


def _layer2_arrays(i):
    import numpy as np
    g = {k[9:]: v for k, v in i.items() if k.startswith("L2_xattn_")}
    qkv, o, cols, ek, bo = [], [], [], [], []
    for n in "12":
        for Q in range(4):
            at = slice(Q * 512, (Q + 1) * 512)
            qkv.append(np.concatenate([_tiles(g["w" + m + n][:, at]).reshape(P, -1) for m in "qkv"], axis=1))
            o.append(_tiles(g["wo" + n][at]).reshape(P, -1))
        cols.append(_columns([_per_tile(g["bq" + n]), _per_tile(g["bk" + n]), _per_tile(g[f"ln{n}_scale"]),
                              _per_tile(g[f"ln{n}_offset"]), _per_tile(g["bias_k" + n].reshape(-1)),
                              _per_tile(g["bias_v" + n].reshape(-1)), _per_tile(g["bv" + n])]))
        ek.append(g["bias_k" + n].reshape(-1))
        bo.append(g["bo" + n])
    return {"l2_qkv": np.stack(qkv), "l2_o": np.stack(o), "l2_cols": np.stack(cols), "l2_ek": np.stack(ek),
            "l2_bo": np.stack(bo)}


def kernel(**inputs):
    import numpy as _np
    import concourse.bacc as _bacc
    from concourse.bass_utils import run_bass_kernel_spmd as _run
    i = {k: _np.asarray(v) for k, v in inputs.items()}
    nc = _bacc.Bacc("TRN2", target_bir_lowering=False, num_devices=1)
    arrays = {"x": i["x"], "ctx": i["ctx_2048"], **_layer0_arrays(i),
              **_layer1_arrays(i),
              **_mlp_arrays("m1", *[i["L1_xattn_" + n] for n in ("fc_w", "fc_b", "proj_w", "proj_b", "ln2_w", "ln2_b")]),
              **_layer2_arrays(i),
              **_mlp_arrays("m2", *[i["L2_xattn_" + n] for n in ("w_fc1", "b_fc1", "w_fc2", "b_fc2", "ln_mlp_scale",
                                                          "ln_mlp_offset")]),
              **_layer3_arrays(i)}
    d = {}
    for name, a in arrays.items():
        a = arrays[name] = _np.ascontiguousarray(a)
        d[name] = nc.dram_tensor("in_" + name, a.shape, mybir.dt.from_np(a.dtype), kind="ExternalInput").ap()
    out = nc.dram_tensor("out", (BATCH, P, D), F32, kind="ExternalOutput").ap()
    ctxT = nc.dram_tensor("ctxT", (NG, P, 2 * KT * TOK), F32, kind="Internal").ap()
    with ExitStack() as ctx:
        X = ctx.enter_context(nc.sbuf_tensor("X", [P, BATCH, D], F32))
        ident = ctx.enter_context(nc.sbuf_tensor("ident", [P, P], F32))
        identity_phase(nc, ident)
        context_phase(nc, d["ctx"], ctxT, ident)
        layer0_phase(nc, d["x"], d["ctx"], d["l0_w"], d["l0_cols"], X, ident)
        heads_phase(nc, 1, X, ctxT, d["l1_w"], d["l1_cols"], d["l1_rows"], d["l1_mask"], ident)
        mlp_phase(nc, "m1", ACT.Gelu_apprx_tanh, X, d["m1_w"], d["m1_cols"], d["m1_rows"], ident)
        clear_semaphores(nc)
        wide_phase(nc, X, ctxT, d, ident)
        mlp_phase(nc, "m2", ACT.Gelu, X, d["m2_w"], d["m2_cols"], d["m2_rows"], ident)
        heads_phase(nc, 3, X, ctxT, d["l3_w"], d["l3_cols"], d["l3_rows"], d["l3_mask"], ident, out)
    r = _run(nc, [{"in_" + k: a for k, a in arrays.items()}], core_ids=[0])
    return r.results[0]["out"]
```

```python
import concourse.bass as bass
from concourse import mybir
from contextlib import ExitStack

F32 = mybir.dt.float32
F32R = mybir.dt.float32r
U8 = mybir.dt.uint8
I32 = mybir.dt.int32
ALU = mybir.AluOpType
ACT = mybir.ActivationFunctionType
AX = mybir.AxisListType

P = 128
BATCH = 16
D = 256
GROUP = 4
NG = BATCH // GROUP
TOK = GROUP * P
KT = D // P
PASSES = ((0, 0), (0, 1), (1, 0))
F32_LOWEST = 3.4028234663852886e38


def mm3(pe, out, lhs, rhs, first, last, terms=PASSES):
    for n, (a, b) in enumerate(terms):
        ins = pe.matmul(out, lhs(a), rhs(b), start=first and n == 0, stop=last and n == len(terms) - 1)
    return ins


class Buffers:

    def __init__(self, nc, ctx, phase):
        self.nc, self.ctx, self.phase = nc, ctx, phase

    def sb(self, name, shape, dt=F32):
        return self.ctx.enter_context(self.nc.sbuf_tensor(f"{self.phase}_{name}", shape, dt))

    def bank(self, name):
        return self.ctx.enter_context(self.nc.psum_tensor(f"{self.phase}_{name}", [P, 512], F32))

    def sem(self, name):
        return self.ctx.enter_context(self.nc.semaphore(f"{self.phase}_{name}"))


def clear_semaphores(nc):
    with nc.Block() as block:
        @block.gpsimd
        def _(pool):
            pool.sem_clear(range(min(nc.free_semaphores), max(nc.free_semaphores) + 1))


def identity_phase(nc, ident):
    with ExitStack() as ctx:
        t = Buffers(nc, ctx, "id")
        cleared = t.sem("cleared")
        block = ctx.enter_context(nc.Block())

        @block.gpsimd
        def _(pool):
            pool.memset(ident[:, :], 0.0).then_inc(cleared, 1)
            pool.wait_ge(cleared, 1)
            pool.affine_select(out=ident[:, :], in_=ident[:, :], compare_op=ALU.not_equal, fill=1.0,
                               base=0, pattern=[[-1, P]], channel_multiplier=1)


def context_phase(nc, ctx_dram, ctxT_dram, ident):
    with ExitStack() as ctx:
        t = Buffers(nc, ctx, "cx")
        c = t.sb("c", [P, 2, GROUP, D])
        cT = t.sb("cT", [P, 2, 2, KT, TOK], F32R)
        ps = [[t.bank(f"ps{p}{k}") for k in range(KT)] for p in range(2)]
        loaded = [t.sem(f"loaded{p}") for p in range(2)]
        turned, hi_done, lo_done = t.sem("turned"), t.sem("hi_done"), t.sem("lo_done")
        stored = [t.sem(f"stored{p}") for p in range(2)]
        block = ctx.enter_context(nc.Block())

        @block.sync
        def _(sp):
            def load(g):
                if g >= 2:
                    sp.wait_ge(turned, g - 1)
                sp.dma_start(c[:, g % 2], ctx_dram[g * GROUP:(g + 1) * GROUP].rearrange("b p d -> p b d"))\
                    .then_inc(loaded[g % 2], 16)

            load(0)
            load(1)
            for g in range(NG):
                if g + 2 < NG:
                    load(g + 2)
                sp.wait_ge(lo_done, KT * (g + 1))
                sp.wait_ge(hi_done, KT * (g + 1))
                sp.dma_start(ctxT_dram[g], cT[:, g % 2].rearrange("p s k n -> p (s k n)").bitcast(F32))\
                    .then_inc(stored[g % 2], 16)
            for p in range(2):
                sp.wait_ge(stored[p], 16 * (NG // 2))

        @block.tensor
        def _(pe):
            for g in range(NG):
                pe.wait_ge(loaded[g % 2], 16 * (g // 2 + 1))
                if g >= 2:
                    pe.wait_ge(lo_done, KT * (g - 1))
                for k in range(KT):
                    for b in range(GROUP):
                        ins = pe.transpose(ps[g % 2][k][:, b * P:(b + 1) * P], c[:, g % 2, b, k * P:(k + 1) * P],
                                           ident[:, :])
                ins.then_inc(turned, 1)

        @block.scalar
        def _(act):
            for g in range(NG):
                act.wait_ge(turned, g + 1)
                if g >= 2:
                    act.wait_ge(stored[g % 2], 16 * (g // 2))
                for k in range(KT):
                    act.activation(cT[:, g % 2, 0, k], ps[g % 2][k][:, :], ACT.Copy).then_inc(hi_done, 1)

        @block.vector
        def _(dve):
            for g in range(NG):
                if g >= 2:
                    dve.wait_ge(stored[g % 2], 16 * (g // 2))
                for k in range(KT):
                    dve.wait_ge(hi_done, KT * g + k + 1)
                    dve.tensor_tensor(cT[:, g % 2, 1, k], ps[g % 2][k][:, :], cT[:, g % 2, 0, k].bitcast(F32),
                                      ALU.subtract).then_inc(lo_done, 1)


def layer0_phase(nc, x_dram, ctx_dram, w_dram, cols_dram, X, ident):
    H, DH, L = 16, 8, D
    LB = L // P
    SLOT = 32
    NT = H // 4
    NQ, NK, NV = 0, NT * P, 2 * NT * P
    NO = NV + P
    NW = NO + P
    SCALE = float(DH) ** -0.5
    PER = 2 * H
    ITS = BATCH // 2
    USES = ["p0", "p1", "v", "p2", "a", "p3", "o"]
    with ExitStack() as ctx:
        t = Buffers(nc, ctx, "l0")
        w_raw = t.sb("w_raw", [P, NW])
        w = t.sb("w", [P, 2, NW], F32R)
        cols = t.sb("cols", [P, 3])
        c_raw = t.sb("c_raw", [P, 2, L])
        xcs = t.sb("xcs", [P, 2, 2, L], F32R)
        top = t.sb("top", [P, 2, 2, L], F32R)
        qk = t.sb("qk", [P, 2, NT, 2, L], F32R)
        v = t.sb("v", [P, 2, LB, H, 32])
        s_sb = t.sb("s_sb", [P, 2, LB, L])
        peak = t.sb("peak", [P, H, LB])
        probs = t.sb("probs", [P, 8, LB, L])
        o_sb = t.sb("o_sb", [P, 2, L])
        rden = t.sb("rden", [P, NT, LB, 4])
        att = t.sb("att", [P, LB, P])
        attT = t.sb("attT", [P, 2, L], F32R)
        psS = [t.bank(f"psS{i}") for i in range(2)]
        psT = [t.bank(f"psT{i}") for i in range(2)]
        psO, psN = t.bank("psO"), t.bank("psN")
        psW = [t.bank(f"psW{i}") for i in range(2)]
        (weights, x_in, w_hi, w_lo, x_hi, x_lo, proj, rounded, stacked, vproj, v_set, v_ones, scored,
         peaked, eased, turned, expd, pved, o_out, o_turned, r_done, normed, a_turned, a_hi, a_lo, outp, x_set,
         act_eased, gate) = [
            t.sem(n) for n in ("weights x_in w_hi w_lo x_hi x_lo proj rounded stacked vproj v_set v_ones scored "
                               "peaked eased turned expd pved o_out o_turned r_done normed a_turned a_hi a_lo outp "
                               "x_set act_eased gate").split()]
        c_in = [t.sem(f"c_in{i}") for i in range(2)]
        block = ctx.enter_context(nc.Block())

        def pipeline(eng, step):
            for s in range(H):
                step(0, s, False)
            with eng.Fori(0, ITS - 1) as it:
                for s in range(H, H + PER):
                    step(it, s, False)
            for s in range(H, PER + H):
                step(ITS - 1, s, True)

        def ease_count(it, s):
            return act_eased if s % 2 else eased, H * it + s // 2 + 1

        def use_at(it, s, last):
            n = s % H // 2 - 1
            if s % H % 2 or not 0 <= n < len(USES):
                return None, 0, 0
            k = s // H + (-1 if USES[n] in "ao" else 1)
            if last and k >= 2 or isinstance(it, int) and 2 * it + k < 0:
                return None, 0, 0
            return USES[n], k, (s // H * len(USES) + n) % 2

        @block.sync
        def _(sp):
            sp.dma_start(w_raw[:, :], w_dram).then_inc(weights, 16)
            sp.dma_start(cols[:, :], cols_dram).then_inc(weights, 16)

            def load(it, k):
                sp.dma_start(c_raw[:, k % 2], ctx_dram[bass.ds(it * 2 + k, 1)].rearrange("a p l -> p (a l)"))\
                    .then_inc(c_in[k % 2], 16)

            sp.dma_start(X[:, 0:2, :], x_dram[0:2].rearrange("b p l -> p b l")).then_inc(x_in, 16)
            load(0, 0)
            load(0, 1)
            sp.dma_start(X[:, 2:BATCH, :], x_dram[2:BATCH].rearrange("b p l -> p b l")).then_inc(x_in, 16)
            with sp.Fori(0, ITS - 1) as it:
                for k in (2, 3):
                    sp.wait_ge(x_lo, 4 * it + 2 * (k - 1))
                    sp.wait_ge(weights, 32)
                    load(it, k)

        @block.gpsimd
        def _(pool):
            pool.memset(v[:, :, :, :, :], 0.0).then_inc(v_ones, 1)
            pool.wait_ge(v_ones, 1)
            pool.memset(v[:, :, :, :, DH:DH + 1], 1.0).then_inc(v_ones, 1)

            def lo(it, k):
                pool.wait_ge(x_hi, 4 * it + 2 * k + 2)
                pool.sem_inc(gate, 1)
                pool.tensor_tensor(xcs[:, 1, 0], X[:, bass.ds(2 * it + k, 1), :].rearrange("p a l -> p (a l)"),
                                   xcs[:, 0, 0].bitcast(F32), ALU.subtract).then_inc(x_lo, 1)
                pool.tensor_tensor(xcs[:, 1, 1], c_raw[:, k % 2], xcs[:, 0, 1].bitcast(F32),
                                   ALU.subtract).then_inc(x_lo, 1)

            lo(0, 0)
            lo(0, 1)
            with pool.Fori(0, ITS - 1) as it:
                for k in (2, 3):
                    lo(it, k)

        @block.scalar
        def _(act):
            def split(it, k):
                if k >= 1:
                    act.wait_ge(proj, NT * (2 * it + k))
                if k >= 2:
                    act.wait_ge(x_in, 32)
                act.wait_ge(c_in[k % 2], 16 * (it + k // 2 + 1))
                act.activation(xcs[:, 0, 0], X[:, bass.ds(2 * it + k, 1), :].rearrange("p a l -> p (a l)"),
                               ACT.Copy).then_inc(x_hi, 1)
                act.activation(xcs[:, 0, 1], c_raw[:, k % 2], ACT.Copy).then_inc(x_hi, 1)

            def use(it, s, last):
                name, k, n_ps = use_at(it, s - 1, last)
                if name is None:
                    return
                ps = psW[n_ps]
                if name == "v":
                    act.wait_ge(vproj, 2 * it + k + 1)
                    if k >= 2:
                        act.wait_ge(pved, NT * (2 * it + k - 1))
                    act.activation(v[:, k % 2, :, :, 0:DH], ps[:, 0:LB * P]
                                   .rearrange("p (k h d) -> p k h d", k=LB, h=H), ACT.Copy).then_inc(v_set, 1)
                elif name == "a":
                    act.wait_ge(a_turned, 2 * it + k + 1)
                    act.activation(attT[:, 0], ps[:, 0:L], ACT.Copy).then_inc(a_hi, 1)
                elif name != "o":
                    n = int(name[1])
                    act.wait_ge(proj, NT * (2 * it + k) + n + 1)
                    if k > 0 or n >= 2:
                        act.wait_ge(stacked, 2 * (NT * (2 * it + k) + n - 1))
                    act.activation(top[:, n % 2], ps[:, :].rearrange("p (a l) -> p a l", a=2), ACT.Copy)\
                        .then_inc(rounded, 1)

            def step(it, s, last):
                if s % H == 0 and not last:
                    split(it, s // H + 1)
                n, i = divmod(s - 8, 4)
                if i == 0 and n >= 0 and not (last and n >= 2 * NT):
                    act.wait_ge(pved, 2 * NT * it + n + 1)
                    if n >= 2:
                        act.wait_ge(o_turned, 2 * NT * it + n - 1)
                    act.activation(o_sb[:, n % 2], psO[:, 0:L], ACT.Copy).then_inc(o_out, 1)
                use(it, s, last)
                h = s - 2
                if h >= 0 and not (last and h >= PER):
                    act.wait_ge(turned, PER * it + h + 1)
                    if h >= 8:
                        act.wait_ge(pved, 2 * NT * it + h // 4 - 1)
                    act.activation(probs[:, h % 8], psT[h % 2][:, :].rearrange("p (k q) -> p k q", k=LB),
                                   ACT.Exp, scale=-SCALE if h % 2 else SCALE).then_inc(expd, 1)
                if s % 2 and not (last and s >= PER):
                    act.wait_ge(peaked, PER * it + s + 1)
                    if s >= 2:
                        act.wait_ge(turned, PER * it + s - 1)
                    for q in range(LB):
                        ins = act.activation(s_sb[:, s % 2, q], psS[s % 2][:, q * L:(q + 1) * L], ACT.Identity,
                                             bias=peak[:, s % H, q:q + 1], scale=-1.0)
                    ins.then_inc(act_eased, 1)
            act.wait_ge(weights, 32)
            act.activation(w[:, 0], w_raw[:, :], ACT.Copy).then_inc(w_hi, 1)
            act.wait_ge(v_ones, 2)
            act.wait_ge(x_in, 16)
            split(0, 0)
            for s in range(H):
                use(0, s - H, False)
            pipeline(act, step)

        @block.vector
        def _(dve):
            def use(it, s, last):
                name, k, n_ps = use_at(it, s - 1, last)
                if name is None or name == "v":
                    return
                ps = psW[n_ps]
                if name == "a":
                    dve.wait_ge(a_hi, 2 * it + k + 1)
                    dve.tensor_tensor(attT[:, 1], ps[:, 0:L], attT[:, 0].bitcast(F32), ALU.subtract)\
                        .then_inc(a_lo, 1)
                elif name == "o":
                    xb = X[:, bass.ds(2 * it + k, 1), :].rearrange("p a d -> p (a d)")
                    dve.wait_ge(outp, 2 * it + k + 1)
                    dve.scalar_tensor_tensor(xb, ps[:, 0:L], cols[:, 2:3], xb, ALU.add, ALU.add).then_inc(x_set, 1)
                else:
                    n = int(name[1])
                    dve.wait_ge(rounded, NT * (2 * it + k) + n + 1)
                    for j in range(2):
                        dve.scalar_tensor_tensor(qk[:, k % 2, n, j], top[:, n % 2, j].bitcast(F32), cols[:, j:j + 1],
                                                 ps[:, j * L:(j + 1) * L], ALU.mult, ALU.add).then_inc(stacked, 1)

            def step(it, s, last):
                if not (last and s >= PER):
                    dve.wait_ge(scored, PER * it + s + 1)
                    dve.tensor_reduce(peak[:, s % H], psS[s % 2][:, :].rearrange("p (q k) -> p q k", q=LB), AX.X,
                                      ALU.max).then_inc(peaked, 1)
                    if s % 2 == 0:
                        dve.wait_ge(peaked, PER * it + s + 1)
                        if s >= 2:
                            dve.wait_ge(turned, PER * it + s - 1)
                        dve.tensor_tensor(s_sb[:, s % 2], psS[s % 2][:, :].rearrange("p (q k) -> p q k", q=LB),
                                          peak[:, s % H].rearrange("p (q a) -> p q a", a=1).to_broadcast([P, LB, L]),
                                          ALU.subtract).then_inc(eased, 1)
                n, i = divmod(s - 10, 4)
                if i == 0 and n >= 0 and not (last and n >= 2 * NT):
                    dve.wait_ge(o_turned, 2 * NT * it + n + 1)
                    o = psN[:, 0:LB * P].rearrange("p (q i c) -> p q i c", q=LB, i=4)
                    dve.reciprocal(rden[:, n % NT], o[:, :, :, DH]).then_inc(r_done, 1)
                    dve.wait_ge(r_done, 2 * NT * it + n + 1)
                    if n % NT == 0 and n > 0:
                        dve.wait_ge(a_turned, 2 * it + n // NT)
                    dve.tensor_tensor(att[:, :, n % NT * 32:(n % NT + 1) * 32]
                                      .rearrange("p q (i d) -> p q i d", i=4), o[:, :, :, 0:DH],
                                      rden[:, n % NT].rearrange("p q (i a) -> p q i a", a=1)
                                      .to_broadcast([P, LB, 4, DH]), ALU.mult).then_inc(normed, 1)
                use(it, s, last)

            dve.wait_ge(w_hi, 1)
            dve.tensor_tensor(w[:, 1], w_raw[:, :], w[:, 0].bitcast(F32), ALU.subtract).then_inc(w_lo, 1)
            dve.memset(peak[:, :, :], 0.0).then_inc(x_set, 1)
            for s in range(H):
                use(0, s - H, False)
            pipeline(dve, step)

        @block.tensor
        def _(pe):
            def bank_free(it, s, last):
                name, k, _ = use_at(it, s - 4 if s % H >= 6 else s - 6, last)
                if name == "v":
                    pe.wait_ge(v_set, 2 * it + k + 1)
                elif name == "a":
                    pe.wait_ge(a_lo, 2 * it + k + 1)
                elif name == "o":
                    pe.wait_ge(x_set, 2 * it + k + 2)
                elif name is not None:
                    pe.wait_ge(stacked, 2 * (NT * (2 * it + k) + int(name[1]) + 1))

            def use(it, s, last):
                name, k, n_ps = use_at(it, s, last)
                if name is None:
                    return
                bank_free(it, s, last)
                ps = psW[n_ps]
                if name == "v":
                    for j in range(LB):
                        ins = mm3(pe, ps[:, j * P:(j + 1) * P], lambda e: xcs[:, e, 1, j * P:(j + 1) * P],
                                  lambda e: w[:, e, NV:NV + P], True, True)
                    ins.then_inc(vproj, 1)
                elif name == "a":
                    pe.wait_ge(normed, NT * (2 * it + k + 1))
                    for q in range(LB):
                        ins = pe.transpose(ps[:, q * P:(q + 1) * P], att[:, q], ident[:, :])
                    ins.then_inc(a_turned, 1)
                elif name == "o":
                    pe.wait_ge(a_lo, 2 * it + k + 1)
                    mm3(pe, ps[:, 0:L], lambda e: w[:, e, NO:NO + P], lambda e: attT[:, e], True, True)\
                        .then_inc(outp, 1)
                else:
                    n = int(name[1])
                    if n == 0:
                        pe.wait_ge(x_lo, 2 * (2 * it + k) + 2)
                    for j, col in ((0, NQ), (1, NK)):
                        ins = mm3(pe, ps[:, j * L:(j + 1) * L], lambda e: w[:, e, col + n * P:col + (n + 1) * P],
                                  lambda e: xcs[:, e, j], True, True)
                    ins.then_inc(proj, 1)

            def step(it, s, last):
                if not (last and s >= PER):
                    k, h = divmod(s, H)
                    n, i = divmod(h, 4)
                    rows = slice(i * SLOT, (i + 1) * SLOT)
                    if i == 0:
                        pe.wait_ge(stacked, 2 * (NT * (2 * it + k) + n + 1))
                    if s >= 2:
                        pe.wait_ge(*ease_count(it, s - 2))
                    for q in range(LB):
                        ins = pe.matmul(psS[s % 2][:, q * L:(q + 1) * L], qk[rows, k % 2, n, 0, q * P:(q + 1) * P],
                                        qk[rows, k % 2, n, 1, :], start=True, stop=True)
                    ins.then_inc(scored, 1)
                h = s - 2
                if h >= 0 and not (last and h >= PER):
                    pe.wait_ge(*ease_count(it, h))
                    if h >= 2:
                        pe.wait_ge(expd, PER * it + h - 1)
                    for q in range(LB):
                        for j in range(LB):
                            ins = pe.transpose(psT[h % 2][:, j * L + q * P:j * L + (q + 1) * P],
                                               s_sb[:, h % 2, q, j * P:(j + 1) * P], ident[:, :])
                    ins.then_inc(turned, 1)
                n, i = divmod(s - 7, 4)
                if i == 0 and n >= 0 and not (last and n >= 2 * NT):
                    pe.wait_ge(expd, PER * it + 4 * (n + 1))
                    if n % NT == 0:
                        pe.wait_ge(v_set, 2 * it + n // NT + 1)
                    if n >= 1:
                        pe.wait_ge(o_out, 2 * NT * it + n)
                    for j in range(LB):
                        for i in range(4):
                            h = 4 * n + i
                            ins = pe.matmul(psO[32 * i:32 * i + 32, 0:L], v[:, n // NT % 2, j, h % H, :],
                                            probs[:, h % 8, j, :], start=j == 0, stop=j == LB - 1)
                    ins.then_inc(pved, 1)
                n, i = divmod(s - 9, 4)
                if i == 0 and n >= 0 and not (last and n >= 2 * NT):
                    pe.wait_ge(o_out, 2 * NT * it + n + 1)
                    if n >= 1:
                        pe.wait_ge(normed, 2 * NT * it + n)
                    for q in range(LB):
                        ins = pe.transpose(psN[:, q * P:(q + 1) * P], o_sb[:, n % 2, q * P:(q + 1) * P], ident[:, :])
                    ins.then_inc(o_turned, 1)
                use(it, s, last)

            pe.wait_ge(w_lo, 1)
            pe.wait_ge(v_ones, 2)
            for s in range(H):
                use(0, s - H, False)
            pipeline(pe, step)


class TokenNorm:

    def __init__(self, t, eps, gamma=None, beta=None, xn=None, full=None):
        self.eps, self.gamma, self.beta = eps, gamma, beta
        self.stats = t.sb("ln_stats", [P, GROUP, 6])
        self.mean_var = t.sb("ln_mean_var", [P, GROUP, 2])
        self.power = t.sb("ln_power", [P, GROUP])
        self.shifted = t.sb("ln_shifted", [P, GROUP])
        self.rstd = t.sb("ln_rstd", [P, GROUP])
        self.xn = t.sb("ln_xn", [P, GROUP, D]) if xn is None else xn
        self.full = t.sb("ln_full", [P, KT, TOK]) if full is None else full
        self.hT = t.sb("hT", [P, 2, KT, TOK], F32R)
        (self.s_gate, self.s_power_set, self.s_gathered, self.s_aggregated, self.s_shift, self.s_rooted,
         self.s_normed, self.s_turned, self.s_affine, self.s_hi, self.s_lo) = [
            t.sem("ln_" + n) for n in ("gate power_set gathered aggregated shift rooted normed turned affine "
                                       "hi lo").split()]

    def pool_setup(self, pool):
        pool.memset(self.power[:, :], -0.5).then_inc(self.s_power_set, 1)

    def dve_statistics(self, dve, g, x):
        for b in range(GROUP):
            dve.bn_stats(self.stats[:, b], x(b)).then_inc(self.s_gathered, 1)
        for b in range(GROUP):
            dve.wait_ge(self.s_gathered, g * GROUP + b + 1)
            dve.sem_inc(self.s_gate, 1)
            dve.bn_aggr(self.mean_var[:, b], self.stats[:, b]).then_inc(self.s_aggregated, 1)

    def pool_rstd(self, pool, g):
        pool.wait_ge(self.s_aggregated, g * GROUP + GROUP)
        pool.sem_inc(self.s_gate, 1)
        pool.wait_ge(self.s_power_set, 1)
        pool.tensor_scalar(self.shifted[:, :], self.mean_var[:, :, 1], self.eps, 1.0, ALU.add, ALU.mult)\
            .then_inc(self.s_shift, 1)
        pool.wait_ge(self.s_shift, g + 1)
        pool.tensor_tensor(self.rstd[:, :], self.shifted[:, :], self.power[:, :], ALU.pow).then_inc(self.s_rooted, 1)

    def dve_normalise(self, dve, g, x, out=None):
        out = self.xn if out is None else out
        if self.eps is None:
            for b in range(GROUP):
                dve.tensor_copy(out[:, b], x(b)).then_inc(self.s_normed, 1)
            return
        dve.wait_ge(self.s_rooted, g + 1)
        for b in range(GROUP):
            dve.tensor_scalar(out[:, b], x(b), self.mean_var[:, b, 0:1], self.rstd[:, b:b + 1],
                              ALU.subtract, ALU.mult).then_inc(self.s_normed, 1)

    def pe_turn_tile(self, pe, g, k, ps, ident):
        for b in range(GROUP):
            pe.wait_ge(self.s_normed, g * GROUP + b + 1)
            ins = pe.transpose(ps[:, b * P:(b + 1) * P], self.xn[:, b, k * P:(k + 1) * P], ident[:, :])
        ins.then_inc(self.s_turned, 1)

    def pe_turn(self, pe, g, banks, ident):
        for k in range(KT):
            self.pe_turn_tile(pe, g, k, banks[k], ident)

    def act_affine_tile(self, act, k, ps):
        if self.gamma is None:
            act.activation(self.full[:, k], ps[:, :], ACT.Copy).then_inc(self.s_affine, 1)
        else:
            act.activation(self.full[:, k], ps[:, :], ACT.Identity, scale=self.gamma[:, k:k + 1],
                           bias=self.beta[:, k:k + 1]).then_inc(self.s_affine, 1)

    def act_hi_tile(self, act, k):
        act.activation(self.hT[:, 0, k], self.full[:, k], ACT.Copy).then_inc(self.s_hi, 1)

    def act_affine(self, act, g, banks):
        for k in range(KT):
            act.wait_ge(self.s_turned, g * KT + k + 1)
            self.act_affine_tile(act, k, banks[k])
        for k in range(KT):
            act.wait_ge(self.s_affine, g * KT + k + 1)
            self.act_hi_tile(act, k)

    def dve_lo_tile(self, dve, k):
        dve.tensor_tensor(self.hT[:, 1, k], self.full[:, k], self.hT[:, 0, k].bitcast(F32), ALU.subtract)\
            .then_inc(self.s_lo, 1)

    def dve_lo(self, dve, g):
        for k in range(KT):
            dve.wait_ge(self.s_hi, g * KT + k + 1)
            self.dve_lo_tile(dve, k)

    def pe_ready(self, pe, g):
        pe.wait_ge(self.s_lo, g * KT + KT)


def heads_phase(nc, layer, X, ctxT_dram, w_dram, cols_dram, rows_dram, mask_dram, ident, out_dram=None):
    first = layer == 1
    H, DH, SLOT = (16, 16, 64) if first else (32, 8, 32)
    KV = 16 if first else 8
    QT, KTILES = (8, 8) if first else (8, 2)
    NQD = H // 4
    VC = KV * DH
    SCALE = float(DH) ** -0.5
    NQ, NK, NV = 0, QT * P, (QT + KTILES) * P
    NO = NV + VC
    NW = NO + D
    C_MASK, C_BIAS, C_G, C_B = 0, 2, 2 + QT + KTILES, 2 + QT + KTILES + KT
    NC = C_B + KT
    R_V, R_O, R_G, R_B = 0, VC, VC + D, VC + 2 * D
    NR = VC + 3 * D
    TURN = 3
    VALUES, READ, TURN_OUT, NORM = TURN + 5, TURN + 6, TURN + 7, TURN + 8
    T0 = TURN + 9 if first else TURN + 14
    CREDIT = 2
    if first:
        when = {"t0": -3, "t1": -3, "q0": -2, "k0": -2, "q1": -1, "k1": -1}
        for u in range(2, QT):
            when[f"q{u}"] = when[f"k{u}"] = 2 * u - 3
    else:
        when = {"t0": -6, "t1": -6, "q0": -4, "k0": -3, "k1": 11}
        for u in range(1, QT):
            when[f"q{u}"] = 4 * u - 3
    when.update({"v0": 4, "v1": 4, "v2": 5, "v3": 6, "a0": H + TURN + 5, "a1": H + TURN + 5, "o0": H + TURN + 7,
                 "o1": H + TURN + 7})
    cycle = sorted(when, key=lambda name: when[name] % H)
    tiles = [name for name in sorted(when, key=lambda name: when[name]) if name[0] in "qk"]

    def place(c):
        n, i = c // 4, c % 4
        return (c // 2, SLOT * (c % 2), c // 2, c) if first else (n, SLOT * i, n // 4, 4 * (n // 4) + i)

    def real(it, k):
        return not isinstance(it, int) or 0 <= it + k < NG

    def uses_at(it, s):
        out = []
        for pos, name in enumerate(cycle):
            k, r = divmod(s - when[name], H)
            if r == 0 and real(it, k):
                out.append((name[0], int(name[1]), k, pos % 2))
        return out

    def pipeline(eng, step):
        for s in range(-H, T0):
            step(0, s)
        with eng.Fori(0, NG - 1) as it:
            for s in range(T0, T0 + H):
                step(it, s)
        for s in range(T0, 2 * H):
            step(NG - 1, s)

    with ExitStack() as ctx:
        t = Buffers(nc, ctx, f"l{layer}")
        cols = t.sb("cols", [P, NC])
        rows = t.sb("rows", [P, NR])
        w = t.sb("w", [P, 2, KT, NW], F32R)
        w_raw = t.sb("w_raw", [P, KT, NW])
        cT = t.sb("cT", [P, 2, KT, TOK], F32R)
        mask = t.sb("mask", [P, TOK])
        mask_raw = t.sb("mask_raw", [P, TOK // 4], I32) if first else t.sb("mask_raw", [P, TOK])
        full = t.sb("full", [P, 2, TOK])
        top = t.sb("top", [P, 2, TOK], F32R)
        qk = t.sb("qk", [P, QT + KTILES, TOK], F32R)
        vt = t.sb("vt", [P, 2, VC])
        v = t.sb("v", [P, GROUP, KV, 32])
        s_sb = t.sb("s_sb", [P, 4, TOK])
        peak = t.sb("peak", [P, H, GROUP])
        probs = t.sb("probs", [P, 8, TOK])
        o_sb = t.sb("o_sb", [P, 2, TOK])
        rden = t.sb("rden", [P, NQD, GROUP, 4])
        att = t.sb("att", [P, GROUP, D])
        attT = t.sb("attT", [P, 2, KT, TOK], F32R)
        xb = t.sb("xb", [P, GROUP, D])
        y, yn = (None, None) if first else (t.sb("y", [P, GROUP, D]), t.sb("yn", [P, GROUP, D]))
        ln = TokenNorm(t, 1e-5 if first else None, cols[:, C_G:C_G + KT] if first else None,
                       cols[:, C_B:C_B + KT] if first else None)
        psS = [t.bank(f"psS{i}") for i in range(2)]
        psT = [t.bank(f"psT{i}") for i in range(2)]
        psO, psN = t.bank("psO"), t.bank("psN")
        psW = [t.bank(f"psW{i}") for i in range(2)]
        (rows_in, w_hi, w_lo, w_lo_pool, loaded, mask_in, mask_set, q_sum, k_sum, v_sum, biased, topped,
         stacked, v_read, v_set, v_ones, scored, masked, peaked, eased, turned, expd, pved, o_out, o_turned, r_done,
         normed, a_turned, a_hi, a_lo, outp, x_biased, added, y_stats, y_mean, y_shift, y_rstd, y_normed, y_scaled,
         y_set, y_left, stored) = [
            t.sem(n) for n in ("rows_in w_hi w_lo w_lo_pool loaded mask_in mask_set q_sum k_sum v_sum biased "
                               "topped stacked v_read v_set v_ones scored masked peaked eased turned expd pved o_out "
                               "o_turned r_done normed a_turned a_hi a_lo outp x_biased added y_stats y_mean y_shift "
                               "y_rstd y_normed y_scaled y_set y_left stored").split()]
        w_in = [t.sem(f"w_in{k}") for k in range(KT)]
        block = ctx.enter_context(nc.Block())

        def tile_count(it, k, name):
            return (it + k) * len(tiles) + tiles.index(name) + 1

        @block.sync
        def _(sp):
            for k in range(KT):
                sp.dma_start(w_raw[:, k], w_dram[:, k]).then_inc(w_in[k], 16)
            sp.dma_start(cols[:, :], cols_dram).then_inc(rows_in, 16)
            sp.dma_start(rows[:, :], rows_dram.to_broadcast([P, NR])).then_inc(rows_in, 16)

            def load(g):
                sp.dma_start(cT[:, :, :, :].rearrange("p s k n -> p (s k n)").bitcast(F32),
                             ctxT_dram[bass.ds(g, 1)].rearrange("a p n -> p (a n)")).then_inc(loaded, 16)

            def load_mask(g):
                if first:
                    sp.dma_start(mask_raw[:, :], mask_dram[bass.ds(g, 1)].to_broadcast([P, TOK // 4]))\
                        .then_inc(mask_in, 16)
                else:
                    sp.dma_start(mask_raw[:, :].rearrange("p (b k) -> p b k", b=GROUP),
                                 mask_dram[bass.ds(g * GROUP, GROUP)].rearrange("b q k -> q b k")).then_inc(mask_in, 16)

            def store(g):
                if not first:
                    sp.wait_ge(y_set, g + 1)
                    sp.wait_ge(rows_in, 32)
                    sp.dma_start(out_dram[bass.ds(g * GROUP, GROUP)].rearrange("b q d -> q b d"), y[:, :, :])\
                        .then_inc(stored, 16)
                    sp.wait_ge(stored, 16 * (g + 1))
                    sp.sem_inc(y_left, 1)

            load(0)
            load_mask(0)
            sp.sem_inc(y_left, 1)
            with sp.Fori(0, NG - 1) as it:
                sp.wait_ge(mask_set, it + 1)
                sp.wait_ge(rows_in, 32)
                load_mask(it + 1)
                sp.wait_ge(v_sum, it * GROUP + GROUP)
                sp.wait_ge(rows_in, 32)
                sp.wait_ge(k_sum, it * KTILES + KTILES)
                sp.wait_ge(rows_in, 32)
                load(it + 1)
                store(it)
            store(NG - 1)
        @block.gpsimd
        def _(pool):
            def step(it, s):
                k, r = divmod(s, H)
                if not first and r == TURN + 10 and real(it, k - 1):
                    pool.wait_ge(y_mean, (it + k) * GROUP)
                    pool.sem_inc(ln.s_gate, 1)
                    pool.tensor_scalar(ln.shifted[:, :], ln.mean_var[:, :, 1], 1e-6, 1.0, ALU.add, ALU.mult)\
                        .then_inc(y_shift, 1)
                    pool.wait_ge(y_shift, it + k)
                    pool.tensor_tensor(ln.rstd[:, :], ln.shifted[:, :], ln.power[:, :], ALU.pow).then_inc(y_rstd, 1)
                if not first and r == TURN + 12 and real(it, k - 1):
                    pool.wait_ge(y_normed, (it + k) * GROUP)
                    pool.tensor_tensor(yn[:, :, :], yn[:, :, :],
                                       rows[:, R_G:R_G + D].rearrange("p (a d) -> p a d", a=1)
                                       .to_broadcast([P, GROUP, D]), ALU.mult).then_inc(y_scaled, 1)
                if not first and r == TURN + 13 and real(it, k - 1):
                    pool.wait_ge(y_scaled, it + k)
                    pool.wait_ge(y_left, it + k)
                    pool.tensor_tensor(y[:, :, :], yn[:, :, :],
                                       rows[:, R_B:R_B + D].rearrange("p (a d) -> p a d", a=1)
                                       .to_broadcast([P, GROUP, D]), ALU.add).then_inc(y_set, 1)
                if 0 <= s and real(it, k):
                    pool.wait_ge(peaked, it * H + s + 1)
                    sc = s_sb[:, s % 4].rearrange("p (b k) -> p b k", b=GROUP)
                    pool.tensor_tensor(sc, sc, peak[:, r].rearrange("p (b a) -> p b a", a=1)
                                       .to_broadcast([P, GROUP, P]), ALU.subtract).then_inc(eased, 1)
                if first and r == T0 and real(it, k + 1):
                    ln.pool_rstd(pool, it + k + 1)
                if r == (H - 1 if first else T0 + 4) and real(it, k) and s >= 0:
                    pool.tensor_tensor(xb[:, :, :], X[:, bass.ds((it + k) * GROUP, GROUP), :],
                                       rows[:, R_O:R_O + D].rearrange("p (a d) -> p a d", a=1)
                                       .to_broadcast([P, GROUP, D]), ALU.add).then_inc(x_biased, 1)

            pool.memset(v[:, :, :, :], 0.0).then_inc(v_ones, 1)
            pool.wait_ge(v_ones, 1)
            pool.memset(v[:, :, :, DH:DH + 1], 1.0).then_inc(v_ones, 1)
            ln.pool_setup(pool)
            pool.wait_ge(w_hi, 2)
            pool.tensor_tensor(w[:, 1, 1], w_raw[:, 1], w[:, 0, 1].bitcast(F32), ALU.subtract).then_inc(w_lo_pool, 1)
            pool.wait_ge(rows_in, 32)
            pipeline(pool, step)

        @block.scalar
        def _(act):
            def use(it, kind, n, k, bank):
                G, ps = it + k, psW[bank]
                if kind == "t":
                    act.wait_ge(ln.s_turned, G * KT + n + 1)
                    if not isinstance(G, int) or G > 0:
                        act.wait_ge(ln.s_lo, G * KT - KT + n + 1)
                    ln.act_affine_tile(act, n, ps)
                    act.wait_ge(ln.s_affine, G * KT + n + 1)
                    if not isinstance(G, int) or G > 0:
                        act.wait_ge(q_sum, G * QT)
                    ln.act_hi_tile(act, n)
                elif kind in "qk":
                    act.wait_ge(q_sum if kind == "q" else k_sum, G * (QT if kind == "q" else KTILES) + n + 1)
                    at = tiles.index(f"{kind}{n}")
                    if not isinstance(G, int) or G * len(tiles) + at >= 2:
                        act.wait_ge(stacked, G * len(tiles) + at - 1)
                    col = C_BIAS + n + (0 if kind == "q" else QT)
                    act.activation(full[:, at % 2], ps[:, :], ACT.Identity, bias=cols[:, col:col + 1])\
                        .then_inc(biased, 1)
                elif kind == "v":
                    act.wait_ge(v_sum, G * GROUP + n + 1)
                    if not isinstance(G, int) or G * GROUP + n >= 2:
                        act.wait_ge(v_set, G * GROUP + n - 1)
                    act.activation(vt[:, n % 2], ps[:, 0:VC], ACT.Copy).then_inc(v_read, 1)
                elif kind == "a":
                    act.wait_ge(a_turned, G * KT + n + 1)
                    act.activation(attT[:, 0, n], ps[:, :], ACT.Copy).then_inc(a_hi, 1)

            def step(it, s):
                n, i = divmod(s - READ, 4)
                if i == 0 and n >= 0 and real(it, n // NQD):
                    act.wait_ge(pved, it * NQD + n + 1)
                    if n >= 2:
                        act.wait_ge(o_turned, it * NQD + n - 1)
                    act.activation(o_sb[:, n % 2], psO[:, :], ACT.Copy).then_inc(o_out, 1)
                for args in uses_at(it, s - 1):
                    use(it, *args)
                c = s - TURN
                if c >= 0 and real(it, c // H):
                    act.wait_ge(turned, it * H + c + 1)
                    if c >= 8:
                        act.wait_ge(pved, it * NQD + c // 4 - 1)
                    act.activation(probs[:, c % 8], psT[c % 2][:, :], ACT.Exp).then_inc(expd, 1)

            for k in range(KT):
                act.wait_ge(w_in[k], 16)
                act.activation(w[:, 0, k], w_raw[:, k], ACT.Copy).then_inc(w_hi, 1)
            act.wait_ge(rows_in, 32)
            pipeline(act, step)

        @block.vector
        def _(dve):
            def x(G, b):
                return X[:, bass.ds(G * GROUP + b, 1), :].rearrange("p a d -> p (a d)")

            def use(it, kind, n, k, bank):
                G, ps = it + k, psW[bank]
                if kind == "t":
                    dve.wait_ge(ln.s_hi, G * KT + n + 1)
                    ln.dve_lo_tile(dve, n)
                elif kind in "qk":
                    at = tiles.index(f"{kind}{n}")
                    dve.wait_ge(biased, tile_count(it, k, f"{kind}{n}"))
                    dve.tensor_copy(top[:, at % 2], full[:, at % 2]).then_inc(topped, 1)
                    dve.wait_ge(topped, tile_count(it, k, f"{kind}{n}"))
                    j, u = (0, n) if kind == "q" else (1, QT + n)
                    dve.scalar_tensor_tensor(qk[:, u], top[:, at % 2].bitcast(F32), cols[:, C_MASK + j:C_MASK + j + 1],
                                             full[:, at % 2], ALU.mult, ALU.add).then_inc(stacked, 1)
                elif kind == "v":
                    dve.wait_ge(v_read, G * GROUP + n + 1)
                    if not isinstance(G, int) or G > 0:
                        dve.wait_ge(pved, G * NQD)
                    dve.tensor_tensor(v[:, n, :, 0:DH], vt[:, n % 2].rearrange("p (h d) -> p h d", h=KV),
                                      rows[:, R_V:R_V + VC].rearrange("p (h d) -> p h d", h=KV), ALU.add)\
                        .then_inc(v_set, 1)
                elif kind == "a":
                    dve.wait_ge(a_hi, G * KT + n + 1)
                    dve.tensor_tensor(attT[:, 1, n], ps[:, :], attT[:, 0, n].bitcast(F32), ALU.subtract)\
                        .then_inc(a_lo, 1)
                else:
                    dve.wait_ge(outp, G * 2 + n + 1)
                    dve.wait_ge(x_biased, G + 1)
                    o = ps[:, :].rearrange("p (b d) -> p b d", b=2)
                    dst = X[:, bass.ds(G * GROUP + 2 * n, 2), :] if first else xb[:, 2 * n:2 * n + 2]
                    dve.tensor_tensor(dst, o, xb[:, 2 * n:2 * n + 2], ALU.add).then_inc(added, 1)

            def norm(it, n):
                dve.wait_ge(o_turned, it * NQD + n + 1)
                o = psN[:, :].rearrange("p (b i c) -> p b i c", b=GROUP, i=4)
                q = n % NQD
                dve.reciprocal(rden[:, q], o[:, :, :, DH]).then_inc(r_done, 1)
                dve.wait_ge(r_done, it * NQD + n + 1)
                if q == 0 and n > 0:
                    dve.wait_ge(a_turned, (it + n // NQD) * KT)
                if first:
                    dst = att[:, :, q * 64:(q + 1) * 64].rearrange("p b (i d) -> p b i d", i=4)
                else:
                    dst = att[:, :, (q // 4) * P:(q // 4 + 1) * P]\
                        .rearrange("p b (i m d) -> p b i m d", i=4, m=4)[:, :, :, q % 4, :]
                dve.tensor_tensor(dst, o[:, :, :, 0:DH],
                                  rden[:, q].rearrange("p b (i a) -> p b i a", a=1)
                                  .to_broadcast([P, GROUP, 4, DH]), ALU.mult).then_inc(normed, 1)

            def step(it, s):
                k, r = divmod(s, H)
                for args in uses_at(it, s - 1):
                    use(it, *args)
                G = it + k
                if r == 0 and real(it, k) and s >= 0:
                    dve.wait_ge(mask_in, G * 16 + 16)
                    if first:
                        dve.tensor_scalar(mask[:, :], mask_raw[:, :].bitcast(U8), -1.0, F32_LOWEST, ALU.add, ALU.mult)\
                            .then_inc(mask_set, 1)
                    else:
                        dve.tensor_copy(mask[:, :], mask_raw[:, :]).then_inc(mask_set, 1)
                    dve.wait_ge(mask_set, G + 1)
                if first and r == T0 and real(it, k + 1):
                    ln.dve_statistics(dve, G + 1, lambda b: x(G + 1, b))
                if r == (T0 + 1 if first else T0 + 4) and real(it, k + 1):
                    if not isinstance(G, int) or G >= 0:
                        dve.wait_ge(ln.s_turned, (G + 1) * KT)
                    ln.dve_normalise(dve, G + 1, lambda b: x(G + 1, b))
                if 0 <= s and real(it, k):
                    dve.wait_ge(scored, it * H + s + 1)
                    if s >= 4:
                        dve.wait_ge(turned, it * H + s - 3)
                    dve.scalar_tensor_tensor(s_sb[:, s % 4], psS[s % 2][:, :], SCALE, mask[:, :], ALU.mult, ALU.add)\
                        .then_inc(masked, 1)
                    dve.wait_ge(masked, it * H + s + 1)
                    dve.tensor_reduce(peak[:, r], s_sb[:, s % 4].rearrange("p (b k) -> p b k", b=GROUP), AX.X,
                                      ALU.max).then_inc(peaked, 1)
                n, i = divmod(s - NORM, 4)
                if i == 0 and n >= 0 and real(it, n // NQD):
                    norm(it, n)
                if not first and r == TURN + 9 and real(it, k - 1):
                    dve.wait_ge(added, CREDIT + G * 2)
                    for b in range(GROUP):
                        dve.bn_stats(ln.stats[:, b], xb[:, b]).then_inc(y_stats, 1)
                    for b in range(GROUP):
                        dve.wait_ge(y_stats, (G - 1) * GROUP + b + 1)
                        dve.sem_inc(ln.s_gate, 1)
                        dve.bn_aggr(ln.mean_var[:, b], ln.stats[:, b]).then_inc(y_mean, 1)
                if not first and r == TURN + 11 and real(it, k - 1):
                    dve.wait_ge(y_rstd, G)
                    for b in range(GROUP):
                        dve.tensor_scalar(yn[:, b], xb[:, b], ln.mean_var[:, b, 0:1], ln.rstd[:, b:b + 1],
                                          ALU.subtract, ALU.mult).then_inc(y_normed, 1)

            dve.wait_ge(w_hi, 1)
            dve.tensor_tensor(w[:, 1, 0], w_raw[:, 0], w[:, 0, 0].bitcast(F32), ALU.subtract).then_inc(w_lo, 1)
            dve.wait_ge(v_ones, 2)
            dve.memset(peak[:, :, :], 0.0).then_inc(added, CREDIT)
            dve.wait_ge(rows_in, 32)
            pipeline(dve, step)

        @block.tensor
        def _(pe):
            def bank_free(it, s, kind, n):
                pos = cycle.index(f"{kind}{n}") + s // H * len(cycle)
                for pos in range(pos - 2, pos - 2 - len(cycle), -2):
                    name = cycle[pos % len(cycle)]
                    k = (pos // len(cycle) * H + when[name] % H - when[name]) // H
                    if not real(it, k):
                        continue
                    G, n = it + k, int(name[1])
                    if name[0] in "qk":
                        pe.wait_ge(biased, tile_count(it, k, name))
                    elif name[0] == "v":
                        pe.wait_ge(v_read, G * GROUP + n + 1)
                    elif name[0] == "t":
                        pe.wait_ge(ln.s_affine, G * KT + n + 1)
                    elif name[0] == "a":
                        pe.wait_ge(a_lo, G * KT + n + 1)
                    else:
                        pe.wait_ge(added, CREDIT + G * 2 + n + 1)
                    if k >= 0:
                        return

            def use(it, s, kind, n, k, bank):
                G, ps = it + k, psW[bank]
                bank_free(it, s, kind, n)
                if kind == "t":
                    ln.pe_turn_tile(pe, G, n, ps, ident)
                elif kind in "qk":
                    if n == 0:
                        if kind == "q":
                            ln.pe_ready(pe, G)
                        else:
                            pe.wait_ge(loaded, G * 16 + 16)
                    src, at, signal = (ln.hT, NQ, q_sum) if kind == "q" else (cT, NK, k_sum)
                    at += n * P
                    for c in range(KT):
                        ins = mm3(pe, ps[:, :], lambda e: w[:, e, c, at:at + P], lambda e: src[:, e, c],
                                  c == 0, c == KT - 1)
                    ins.then_inc(signal, 1)
                elif kind == "v":
                    for c in range(KT):
                        ins = mm3(pe, ps[:, 0:VC], lambda e: cT[:, e, c, n * P:(n + 1) * P],
                                  lambda e: w[:, e, c, NV:NV + VC], c == 0, c == KT - 1)
                    ins.then_inc(v_sum, 1)
                elif kind == "a":
                    if n == 0:
                        pe.wait_ge(normed, G * NQD + NQD)
                    for b in range(GROUP):
                        ins = pe.transpose(ps[:, b * P:(b + 1) * P], att[:, b, n * P:(n + 1) * P], ident[:, :])
                    ins.then_inc(a_turned, 1)
                else:
                    if n == 0:
                        pe.wait_ge(a_lo, G * KT + KT)
                    for b in (2 * n, 2 * n + 1):
                        for c in range(KT):
                            ins = mm3(pe, ps[:, (b % 2) * D:(b % 2 + 1) * D],
                                      lambda e: attT[:, e, c, b * P:(b + 1) * P], lambda e: w[:, e, c, NO:NO + D],
                                      c == 0, c == KT - 1)
                    ins.then_inc(outp, 1)

            def step(it, s):
                k, c = divmod(s, H)
                if s >= 0 and real(it, k):
                    qt, row, kt, _ = place(c)
                    if s >= 2:
                        pe.wait_ge(masked, it * H + s - 1)
                    pe.wait_ge(stacked, max((tile_count(0, 0, f"q{qt}"), tile_count(0, 0, f"k{kt}")))
                               + (it + k) * len(tiles))
                    for b in range(GROUP):
                        at = slice(b * P, (b + 1) * P)
                        ins = pe.matmul(psS[s % 2][:, at], qk[row:row + SLOT, qt, at], qk[row:row + SLOT, QT + kt, at],
                                        start=True, stop=True)
                    ins.then_inc(scored, 1)
                c = s - TURN
                if c >= 0 and real(it, c // H):
                    pe.wait_ge(eased, it * H + c + 1)
                    if c >= 2:
                        pe.wait_ge(expd, it * H + c - 1)
                    for b in range(GROUP):
                        at = slice(b * P, (b + 1) * P)
                        ins = pe.transpose(psT[c % 2][:, at], s_sb[:, c % 4, at], ident[:, :])
                    ins.then_inc(turned, 1)
                n, i = divmod(s - VALUES, 4)
                if i == 0 and n >= 0 and real(it, n // NQD):
                    pe.wait_ge(expd, it * H + 4 * (n + 1))
                    if n >= 1:
                        pe.wait_ge(o_out, it * NQD + n)
                    if n % NQD == 0:
                        pe.wait_ge(v_set, (it + n // NQD) * GROUP + GROUP)
                    for b in range(GROUP):
                        at = slice(b * P, (b + 1) * P)
                        for i in range(4):
                            c = 4 * n + i
                            ins = pe.matmul(psO[32 * i:32 * i + 32, at], v[:, b, place(c % H)[3], :],
                                            probs[:, c % 8, at], start=True, stop=True)
                    ins.then_inc(pved, 1)
                n, i = divmod(s - TURN_OUT, 4)
                if i == 0 and n >= 0 and real(it, n // NQD):
                    pe.wait_ge(o_out, it * NQD + n + 1)
                    if n >= 1:
                        pe.wait_ge(normed, it * NQD + n)
                    for b in range(GROUP):
                        at = slice(b * P, (b + 1) * P)
                        ins = pe.transpose(psN[:, at], o_sb[:, n % 2, at], ident[:, :])
                    ins.then_inc(o_turned, 1)
                for args in uses_at(it, s):
                    use(it, s, *args)

            pe.wait_ge(w_lo, 1)
            pe.wait_ge(w_lo_pool, 1)
            pipeline(pe, step)


def mlp_phase(nc, name, gelu, X, w_dram, cols_dram, rows_dram, ident):
    F = 4 * D
    FT = F // P
    NF, NP_ = 0, KT * F
    NW = NP_ + FT * D
    C_B, C_G, C_O = 0, FT, FT + KT
    NC = C_O + KT
    with ExitStack() as ctx:
        t = Buffers(nc, ctx, name)
        cols = t.sb("cols", [P, NC])
        rows = t.sb("rows", [P, D])
        w = t.sb("w", [P, 2, NW], F32R)
        w_raw = t.sb("w_raw", [P, NW])
        ln = TokenNorm(t, 1e-5, cols[:, C_G:C_G + KT], cols[:, C_O:C_O + KT])
        act_out = t.sb("act_out", [P, 2, TOK])
        y = t.sb("y", [P, 2, FT, TOK], F32R)
        xb = t.sb("xb", [P, GROUP, D])
        psW = [t.bank(f"psW{i}") for i in range(2)]
        psH = [t.bank(f"psH{i}") for i in range(2)]
        psO = [t.bank(f"psO{i}") for i in range(2)]
        (weights, w_hi, w_lo, fc, gelued, y_hi, y_lo, outp, x_biased, done) = [
            t.sem(n) for n in "weights w_hi w_lo fc gelued y_hi y_lo outp x_biased done".split()]
        block = ctx.enter_context(nc.Block())

        @block.sync
        def _(sp):
            sp.dma_start(w_raw[:, :], w_dram).then_inc(weights, 16)
            sp.dma_start(cols[:, :], cols_dram).then_inc(weights, 16)
            sp.dma_start(rows[:, :], rows_dram.to_broadcast([P, D])).then_inc(weights, 16)

        @block.gpsimd
        def _(pool):
            ln.pool_setup(pool)
            pool.wait_ge(weights, 48)
            with pool.Fori(0, NG) as g:
                pool.wait_ge(done, g + 1)
                ln.pool_rstd(pool, g)
                pool.tensor_tensor(xb[:, :, :], X[:, bass.ds(g * GROUP, GROUP), :],
                                   rows[:, :].rearrange("p (a d) -> p a d", a=1).to_broadcast([P, GROUP, D]),
                                   ALU.add).then_inc(x_biased, 1)

        @block.scalar
        def _(act):
            act.wait_ge(weights, 48)
            act.activation(w[:, 0], w_raw[:, :], ACT.Copy).then_inc(w_hi, 1)
            with act.Fori(0, NG) as g:
                act.wait_ge(done, g + 1)
                ln.act_affine(act, g, psW)
                for n in range(FT):
                    act.wait_ge(fc, g * FT + n + 1)
                    if n >= 2:
                        act.wait_ge(y_lo, g * FT + n - 1)
                    act.activation(act_out[:, n % 2], psH[n % 2][:, :], gelu, bias=cols[:, C_B + n:C_B + n + 1])\
                        .then_inc(gelued, 1)

        @block.vector
        def _(dve):
            dve.wait_ge(w_hi, 1)
            dve.tensor_tensor(w[:, 1], w_raw[:, :], w[:, 0].bitcast(F32), ALU.subtract).then_inc(w_lo, 1)
            dve.wait_ge(w_lo, 1)
            dve.memset(act_out[:, 0, 0:1], 0.0).then_inc(done, 1)
            with dve.Fori(0, NG) as g:
                dve.wait_ge(done, g + 1)

                def x(b):
                    return X[:, bass.ds(g * GROUP + b, 1), :].rearrange("p a d -> p (a d)")

                ln.dve_statistics(dve, g, x)
                ln.dve_normalise(dve, g, x)
                ln.dve_lo(dve, g)
                for n in range(FT):
                    dve.wait_ge(gelued, g * FT + n + 1)
                    dve.tensor_copy(y[:, 0, n], act_out[:, n % 2]).then_inc(y_hi, 1)
                    dve.wait_ge(y_hi, g * FT + n + 1)
                    dve.tensor_tensor(y[:, 1, n], act_out[:, n % 2], y[:, 0, n].bitcast(F32), ALU.subtract)\
                        .then_inc(y_lo, 1)
                dve.wait_ge(x_biased, g + 1)
                for m in range(2):
                    dve.wait_ge(outp, g * 2 + m + 1)
                    ins = dve.tensor_tensor(X[:, bass.ds(g * GROUP + 2 * m, 2), :],
                                            psO[m][:, :].rearrange("p (b d) -> p b d", b=2), xb[:, 2 * m:2 * m + 2],
                                            ALU.add)
                    if m == 1:
                        ins.then_inc(done, 1)

        @block.tensor
        def _(pe):
            pe.wait_ge(w_lo, 1)
            with pe.Fori(0, NG) as g:
                pe.wait_ge(done, g + 1)
                ln.pe_turn(pe, g, psW, ident)
                ln.pe_ready(pe, g)
                for n in range(FT):
                    if n >= 2:
                        pe.wait_ge(gelued, g * FT + n - 1)
                    for k in range(KT):
                        at = NF + k * F + n * P
                        ins = mm3(pe, psH[n % 2][:, :], lambda s: w[:, s, at:at + P], lambda s: ln.hT[:, s, k],
                                  k == 0, k == KT - 1)
                    ins.then_inc(fc, 1)
                pe.wait_ge(y_lo, g * FT + FT)
                for b in range(GROUP):
                    for n in range(FT):
                        at = NP_ + n * D
                        ins = mm3(pe, psO[b // 2][:, (b % 2) * D:(b % 2 + 1) * D],
                                  lambda s: y[:, s, n, b * P:(b + 1) * P], lambda s: w[:, s, at:at + D],
                                  n == 0, n == FT - 1)
                    if b % 2:
                        ins.then_inc(outp, 1)


def wide_phase(nc, X, ctxT_dram, d, ident):
    H, QH = 16, 4
    NQD = H // QH
    SCALE = float(P) ** -0.5
    PART = KT * QH * P
    C_BQ, C_BK, C_G, C_B, C_EK, C_EV, C_BV = 0, 16, 32, 34, 36, 52, 68
    NC = 84
    AHEAD = 7
    CREDIT = 8
    SLOTS = 6
    LAST = H + 3
    with ExitStack() as ctx:
        t = Buffers(nc, ctx, "l2")
        cols = t.sb("cols", [P, NC])
        bo = t.sb("bo", [1, D])
        raw = t.sb("raw", [P, 2, 3 * PART])
        raw_o = t.sb("raw_o", [P, 2, PART])
        w = t.sb("w", [P, 2, 2, 4 * PART], F32R)
        qk = t.sb("qk", [P, 2 * SLOTS, TOK])
        v = t.sb("v", [P, 2, GROUP, QH, P + 1])
        cT = t.sb("cT", [P, 2, KT, TOK], F32R)
        s_sb = t.sb("s_sb", [P, 2, TOK])
        probs = t.sb("probs", [P, 3, TOK])
        att = t.sb("att", [P, 2, TOK])
        attT = t.sb("attT", [P, 2, QH, TOK], F32R)
        extra = t.sb("extra", [P, GROUP, H])
        top = t.sb("top", [P, H, GROUP])
        peak = t.sb("peak", [P, H, GROUP])
        gap = t.sb("gap", [P, H, GROUP])
        extra_p = t.sb("extra_p", [P, H, GROUP])
        den = t.sb("den", [P, H, GROUP])
        rden = t.sb("rden", [P, H, GROUP])
        norm_p = t.sb("norm_p", [P, GROUP, H + 1])
        norm_pT = t.sb("norm_pT", [H + 1, TOK])
        u = t.sb("u", [P, KT, H])
        u_parts = t.sb("u_parts", [P, 2, KT, H], F32R)
        ones = t.sb("ones", [P, P])
        c_prod = t.sb("c_prod", [P, H])
        c_row = t.sb("c_row", [P, H])
        dv = t.sb("dv", [P, H * (H + 1)])
        pick = t.sb("pick", [1, H + 1])
        credit = t.sb("credit", [P, 1])
        big_g = t.sb("big_g", [H + 1, D])
        ln = TokenNorm(t, 1e-5, cols[:, C_G:C_G + KT], cols[:, C_B:C_B + KT],
                       att[:, :, :].rearrange("p a (b d) -> p (a b) d", b=2), s_sb)
        psS = [t.bank(f"psS{n}") for n in range(2)]
        psT = [t.bank(f"psT{n}") for n in range(2)]
        psV = ctx.enter_context(nc.psum_tensor("l2_psV", [P, GROUP, 256], F32))
        psW = [t.bank(f"psW{n}") for n in range(2)]
        whole = qk[:, 0:2 * QH].rearrange("p h n -> p (h n)")
        ek_rows = qk[:, 2 * QH:3 * QH].rearrange("p h n -> p (h n)")
        (consts, params, wq_in, wo_in, u_prod, u_sum, u_hi, u_set, c_mul, c_sum, c_set, dv_set, g_sum,
         g_set, w_hi, w_lo, ctx_in, extra_sum, extra_set, q_sum, q_set, k_sum, k_set, v_sum, v_set, scored,
         topped, peaked, eased, gapped, extra_exp, turned, expd, pved, den_set, r_done, np_set, normed, a_turned,
         a_hi, a_lo, outp, added, np_turned, npT_set, done, gate) = [
            t.sem(n) for n in ("consts params wq_in wo_in u_prod u_sum u_hi u_set c_mul c_sum c_set dv_set "
                               "g_sum g_set w_hi w_lo ctx_in extra_sum extra_set q_sum q_set k_sum k_set "
                               "v_sum v_set scored topped peaked eased gapped extra_exp turned expd pved den_set "
                               "r_done np_set normed a_turned a_hi a_lo outp added np_turned npT_set done gate").split()]
        qkv_in = [t.sem(f"qkv_in{n}") for n in range(2)]
        o_in = [t.sem(f"o_in{n}") for n in range(2)]
        block = ctx.enter_context(nc.Block())
        qkv_dram, o_dram = d["l2_qkv"], d["l2_o"]

        def uses():
            order = [("l", 0), ("l", 1), ("x", 0)]
            for n in range(4):
                order += [("q", n), ("k", n), ("v", n)]
            for n in range(LAST):
                if output_at(n) is not None:
                    order += [("o", 2 * output_at(n)), ("o", 2 * output_at(n) + 1)]
                if 0 <= n - 3 < H:
                    order += [("t", n - 3)]
                if n + 4 < H:
                    order += [("q", n + 4), ("k", n + 4), ("v", n + 4)]
            return order + [("o", 2 * NQD - 2), ("o", 2 * NQD - 1)]

        def output_at(n):
            Q, i = divmod(n - 7, 4)
            return Q if i == 0 and 0 <= Q < NQD - 1 else None

        def flat(ap):
            return ap.rearrange("a p n -> p (a n)")

        @block.sync
        def _(sp):
            def load(index, r, Q, stream):
                sp.wait_ge(w_lo, stream * 4 + 3)
                sp.dma_start(raw[:, Q % 2], flat(qkv_dram[index])).then_inc(qkv_in[Q % 2], 16)
                sp.wait_ge(w_lo, stream * 4 + 7)
                sp.dma_start(raw_o[:, Q % 2], flat(o_dram[index])).then_inc(o_in[Q % 2], 16)

            with sp.Fori(0, 2) as a:
                with sp.Fori(0, NG) as g:
                    for Q in range(NQD):
                        load(bass.ds(a * NQD + Q, 1), a * NG + g, Q, (a * NG + g) * NQD + Q)
            for Q in range(2):
                load(slice(Q, Q + 1), 2 * NG, Q, 2 * NG * NQD + Q)
            for n in range(2):
                sp.wait_ge(qkv_in[n], 16 * (NG * NQD + 1))
                sp.wait_ge(o_in[n], 16 * (NG * NQD + 1))

        @block.gpsimd
        def _(pool):
            pool.memset(dv[:, :], 0.0).then_inc(consts, 1)
            pool.memset(pick[:, :], 0.0).then_inc(consts, 1)
            pool.memset(ones[:, :], 1.0).then_inc(consts, 1)
            pool.memset(norm_p[:, :, :], 1.0).then_inc(consts, 1)
            pool.memset(v[:, :, :, :, P:P + 1], 1.0).then_inc(consts, 1)
            pool.wait_ge(consts, 5)
            pool.memset(pick[:, H:H + 1], 1.0).then_inc(consts, 1)
            ln.pool_setup(pool)
            pool.memset(credit[:, :], 0.0).then_inc(w_lo, CREDIT)

            def split(parity, part):
                src = raw[:, parity, part * PART:(part + 1) * PART] if part < 3 else raw_o[:, parity]
                at = slice(part * PART, (part + 1) * PART)
                pool.tensor_tensor(w[:, parity, 1, at], src, w[:, parity, 0, at].bitcast(F32), ALU.subtract)\
                    .then_inc(w_lo, 1)

            for n, (parity, part) in enumerate([(0, 0), (0, 1), (0, 2), (1, 0), (1, 1), (1, 2), (0, 3)]):
                pool.wait_ge(w_hi, n + 1)
                split(parity, part)
            with pool.Fori(0, 2) as a:
                with pool.Fori(0, NG) as g:
                    r = a * NG + g
                    ln.pool_rstd(pool, r)
                    for n in range(H):
                        Q, i = divmod(n, 4)
                        pool.wait_ge(w_hi, r * H + AHEAD + n + 1)
                        split(Q % 2 if i < 3 else (Q + 1) % 2, i)

        @block.scalar
        def _(act):
            def split(parity, part):
                src = raw[:, parity, part * PART:(part + 1) * PART] if part < 3 else raw_o[:, parity]
                act.activation(w[:, parity, 0, part * PART:(part + 1) * PART], src, ACT.Copy).then_inc(w_hi, 1)

            for parity in range(2):
                act.wait_ge(qkv_in[parity], 16)
                for part in range(3):
                    split(parity, part)
            act.wait_ge(o_in[0], 16)
            split(0, 3)
            with act.Fori(0, 2) as a:
                act.wait_ge(done, a * NG + 1)
                act.wait_ge(consts, 6)
                act.dma_start(cols[:, :], flat(d["l2_cols"][bass.ds(a, 1)])).then_inc(params, 16)
                act.dma_start(bo[:, :], d["l2_bo"][bass.ds(a, 1)]).then_inc(params, 16)
                act.dma_start(ek_rows, d["l2_ek"][bass.ds(a, 1)].to_broadcast([P, H * P])).then_inc(params, 16)
                act.dma_start(whole.rearrange("p (q n) -> p q n", q=NQD),
                              qkv_dram[bass.ds(a * NQD, NQD), :, 0:PART].rearrange("q p n -> p q n"))\
                    .then_inc(wq_in, 16)
                act.wait_ge(u_sum, a * NQD + NQD)
                act.wait_ge(consts, 6)
                act.dma_start(whole.rearrange("p (q n) -> p q n", q=NQD),
                              o_dram[bass.ds(a * NQD, NQD)].rearrange("q p n -> p q n")).then_inc(wo_in, 16)
                act.wait_ge(g_sum, a + 1)
                act.activation(big_g[:, :], psW[1][0:H + 1, 0:D], ACT.Copy).then_inc(g_set, 1)
                with act.Fori(0, NG) as g:
                    r = a * NG + g
                    act.wait_ge(done, r + 1)
                    act.dma_start(cT[:, :, :, :].rearrange("p s k n -> p (s k n)").bitcast(F32),
                                  flat(ctxT_dram[bass.ds(g, 1)])).then_inc(ctx_in, 16)
                    ln.act_affine(act, r, psW)

                    def project(n, bank):
                        Q, i = divmod(n, 4)
                        act.wait_ge(q_sum, r * H + n + 1)
                        act.activation(qk[:, n % SLOTS], psW[bank["q", n]][:, :], ACT.Identity,
                                       bias=cols[:, C_BQ + n:C_BQ + n + 1]).then_inc(q_set, 1)
                        act.wait_ge(k_sum, r * H + n + 1)
                        act.activation(qk[:, SLOTS + n % SLOTS], psW[bank["k", n]][:, :], ACT.Identity,
                                       bias=cols[:, C_BK + n:C_BK + n + 1]).then_inc(k_set, 1)

                    def values(n, bank):
                        Q, i = divmod(n, 4)
                        act.wait_ge(v_sum, r * H + n + 1)
                        if Q >= 2:
                            act.wait_ge(pved, r * H + 4 * (Q - 1))
                        act.activation(v[:, Q % 2, i, :, 0:P], psW[bank["v", n]][:, :]
                                       .rearrange("p (h n) -> p h n", h=QH), ACT.Copy).then_inc(v_set, 1)

                    bank = {use: n % 2 for n, use in enumerate(uses())}
                    for n in range(4):
                        project(n, bank)
                        values(n, bank)
                    for n in range(LAST):
                        if 0 <= n - 3 < H:
                            act.wait_ge(a_turned, r * H + n - 2)
                            act.activation(attT[:, 0, (n - 3) % 4], psW[bank["t", n - 3]][:, :], ACT.Copy)\
                                .then_inc(a_hi, 1)
                        if n + 4 < H:
                            project(n + 4, bank)
                        if 0 <= n - 1 < H:
                            c = n - 1
                            act.wait_ge(gapped, r * H + c + 1)
                            act.activation(extra_p[:, c], gap[:, c], ACT.Exp, scale=SCALE).then_inc(extra_exp, 1)
                            act.wait_ge(turned, r * H + c + 1)
                            if c >= 3:
                                act.wait_ge(pved, r * H + c - 2)
                            act.activation(probs[:, c % 3], psT[c % 2][:, :], ACT.Exp, scale=SCALE).then_inc(expd, 1)
                        if n + 4 < H:
                            values(n + 4, bank)
                        if n < H:
                            Q, i = divmod(n, 4)
                            if i < 3:
                                act.wait_ge(qkv_in[Q % 2], r * (NQD // 2 * 16) + 16 * (Q // 2 + 2))
                                split(Q % 2, i)
                            else:
                                act.wait_ge(o_in[(Q + 1) % 2], r * (NQD // 2 * 16) + 16 * ((Q + 1) // 2 + 1))
                                if Q >= 1:
                                    act.wait_ge(outp, r * 2 * NQD + 2 * Q)
                                split((Q + 1) % 2, 3)
                    act.wait_ge(np_turned, r + 1)
                    act.activation(norm_pT[:, :], psT[0][0:H + 1, :], ACT.Copy).then_inc(npT_set, 1)

        @block.vector
        def _(dve):
            dve.wait_ge(consts, 6)
            dve.memset(s_sb[:, 0, 0:1], 0.0).then_inc(done, 1)
            with dve.Fori(0, 2) as a:
                dve.wait_ge(params, a * 48 + 48)
                dve.wait_ge(wq_in, a * 16 + 16)
                for Q in range(NQD):
                    part = whole[:, Q * PART:(Q + 1) * PART].rearrange("p (c n) -> p c n", c=KT)
                    dve.tensor_tensor(part, part, ek_rows[:, Q * QH * P:(Q + 1) * QH * P]
                                      .rearrange("p (a n) -> p a n", a=1).to_broadcast([P, KT, QH * P]), ALU.mult)\
                        .then_inc(u_prod, 1)
                for Q in range(NQD):
                    dve.wait_ge(u_prod, a * NQD + Q + 1)
                    dve.tensor_reduce(u[:, :, Q * QH:(Q + 1) * QH], whole[:, Q * PART:(Q + 1) * PART]
                                      .rearrange("p (c h n) -> p c h n", c=KT, h=QH), AX.X, ALU.add)\
                        .then_inc(u_sum, 1)
                dve.wait_ge(u_sum, a * NQD + NQD)
                dve.tensor_copy(u_parts[:, 0], u[:, :, :]).then_inc(u_hi, 1)
                dve.wait_ge(u_hi, a + 1)
                dve.tensor_tensor(u_parts[:, 1], u[:, :, :], u_parts[:, 0].bitcast(F32), ALU.subtract)\
                    .then_inc(u_set, 1)
                dve.tensor_tensor(c_prod[:, :], cols[:, C_BQ:C_BQ + H], cols[:, C_EK:C_EK + H], ALU.mult)\
                    .then_inc(c_mul, 1)
                dve.tensor_tensor(dv[:, 0:H * (H + 1):H + 2], cols[:, C_EV:C_EV + H], cols[:, C_BV:C_BV + H],
                                  ALU.subtract).then_inc(dv_set, 1)
                dve.tensor_copy(dv[:, H:H * (H + 1):H + 1], cols[:, C_BV:C_BV + H]).then_inc(dv_set, 1)
                dve.wait_ge(c_sum, a + 1)
                dve.tensor_copy(c_row[:, :], psW[0][:, 0:H]).then_inc(c_set, 1)
                with dve.Fori(0, NG) as g:
                    r = a * NG + g
                    dve.wait_ge(done, r + 1)

                    def x(b):
                        return X[:, bass.ds(g * GROUP + b, 1), :].rearrange("p a d -> p (a d)")

                    ln.dve_statistics(dve, r, x)
                    ln.dve_normalise(dve, r, x)
                    ln.dve_lo(dve, r)
                    dve.wait_ge(c_set, a + 1)
                    dve.wait_ge(extra_sum, r + 1)
                    bank = {use: n % 2 for n, use in enumerate(uses())}
                    dve.tensor_tensor(extra[:, :, :], psW[bank["x", 0]][:, 0:GROUP * H]
                                      .rearrange("p (b h) -> p b h", b=GROUP),
                                      c_row[:, :].rearrange("p (a h) -> p a h", a=1).to_broadcast([P, GROUP, H]),
                                      ALU.add).then_inc(extra_set, 1)
                    dve.wait_ge(extra_set, r + 1)

                    def add_output(Q):
                        for m in range(2):
                            xm = X[:, bass.ds(g * GROUP + 2 * m, 2), :]
                            if Q >= 1:
                                dve.wait_ge(added, r * 2 * NQD + 2 * Q)
                            dve.wait_ge(outp, r * 2 * NQD + 2 * Q + m + 1)
                            dve.tensor_tensor(xm, psW[bank["o", 2 * Q + m]][:, :].rearrange("p (b d) -> p b d", b=2),
                                              xm, ALU.add).then_inc(added, 1)

                    for n in range(LAST):
                        if output_at(n) is not None:
                            add_output(output_at(n))
                        c = n - 2
                        if 0 <= c < H:
                            dve.wait_ge(pved, r * H + c + 1)
                            dve.wait_ge(extra_exp, r * H + c + 1)
                            dve.tensor_tensor(den[:, c], psV[:, :, P], extra_p[:, c], ALU.add).then_inc(den_set, 1)
                            dve.wait_ge(den_set, r * H + c + 1)
                            dve.reciprocal(rden[:, c], den[:, c]).then_inc(r_done, 1)
                            dve.wait_ge(r_done, r * H + c + 1)
                            dve.tensor_tensor(norm_p[:, :, c], rden[:, c], extra_p[:, c], ALU.mult).then_inc(np_set, 1)
                            if c >= 2:
                                dve.wait_ge(a_turned, r * H + c - 1)
                            dve.tensor_tensor(att[:, c % 2].rearrange("p (b n) -> p b n", b=GROUP), psV[:, :, 0:P],
                                              rden[:, c].rearrange("p (b a) -> p b a", a=1)
                                              .to_broadcast([P, GROUP, P]), ALU.mult).then_inc(normed, 1)
                        c = n - 3
                        if 0 <= c < H:
                            dve.wait_ge(a_hi, r * H + c + 1)
                            dve.tensor_tensor(attT[:, 1, c % 4], psW[bank["t", c]][:, :],
                                              attT[:, 0, c % 4].bitcast(F32), ALU.subtract).then_inc(a_lo, 1)
                        if n < H:
                            dve.wait_ge(scored, r * H + n + 1)
                            s = psS[n % 2][:, :].rearrange("p (b m) -> p b m", b=GROUP)
                            dve.tensor_reduce(top[:, n], s, AX.X, ALU.max).then_inc(topped, 1)
                            dve.wait_ge(topped, r * H + n + 1)
                            dve.tensor_tensor(peak[:, n], top[:, n], extra[:, :, n], ALU.max).then_inc(peaked, 1)
                            dve.wait_ge(peaked, r * H + n + 1)
                            if n >= 2:
                                dve.wait_ge(turned, r * H + n - 1)
                            dve.tensor_tensor(s_sb[:, n % 2].rearrange("p (b m) -> p b m", b=GROUP), s,
                                              peak[:, n].rearrange("p (b a) -> p b a", a=1)
                                              .to_broadcast([P, GROUP, P]), ALU.subtract).then_inc(eased, 1)
                            dve.tensor_tensor(gap[:, n], extra[:, :, n], peak[:, n], ALU.subtract).then_inc(gapped, 1)
                    add_output(NQD - 1)
                    dve.wait_ge(added, r * 2 * NQD + 2 * NQD)
                    dve.memset(s_sb[:, 0, 0:1], 0.0).then_inc(done, 1)

        @block.tensor
        def _(pe):
            pe.wait_ge(consts, 6)
            with pe.Fori(0, 2) as a:
                pe.wait_ge(done, a * NG + 1)
                pe.wait_ge(c_mul, a + 1)
                pe.matmul(psW[0][:, 0:H], ones[:, :], c_prod[:, :], start=True, stop=True).then_inc(c_sum, 1)
                pe.wait_ge(dv_set, a * 2 + 2)
                pe.wait_ge(wo_in, a * 16 + 16)
                for h in range(H):
                    pe.matmul(psW[1][0:H + 1, 0:D], dv[:, h * (H + 1):(h + 1) * (H + 1)],
                              whole[:, h * D:(h + 1) * D], start=h == 0, stop=False)
                pe.matmul(psW[1][0:H + 1, 0:D], pick[:, :], bo[:, :], start=False, stop=True).then_inc(g_sum, 1)
                pe.wait_ge(c_set, a + 1)
                pe.wait_ge(g_set, a + 1)
                pe.wait_ge(u_set, a + 1)
                pe.sem_inc(gate, 1)
                with pe.Fori(0, NG) as g:
                    r = a * NG + g
                    pe.wait_ge(done, r + 1)
                    order = uses()
                    at = {use: n for n, use in enumerate(order)}
                    freed = {"l": (ln.s_affine, KT), "x": (extra_set, 1), "q": (q_set, H), "k": (k_set, H),
                             "v": (v_set, H), "t": (a_lo, H), "o": (added, 2 * NQD)}

                    def bank(kind, n):
                        i = at[kind, n]
                        if i >= 2:
                            kind0, n0 = order[i - 2]
                            sem, per = freed[kind0]
                            pe.wait_ge(sem, r * per + n0 + 1)
                        return psW[i % 2]

                    def project(n):
                        Q, i = divmod(n, 4)
                        if i == 0:
                            pe.wait_ge(w_lo, r * (4 * NQD) + CREDIT + 4 * Q + 3)
                        for kind, part, src, signal in (("q", 0, ln.hT, q_sum), ("k", 1, cT, k_sum)):
                            ps = bank(kind, n)
                            for c in range(KT):
                                col = part * PART + c * QH * P + i * P
                                ins = mm3(pe, ps[:, :], lambda s: w[:, Q % 2, s, col:col + P], lambda s: src[:, s, c],
                                          c == 0, c == KT - 1)
                            ins.then_inc(signal, 1)

                    def values(n):
                        Q, b = divmod(n, 4)
                        ps = bank("v", n)
                        for c in range(KT):
                            col = 2 * PART + c * QH * P
                            ins = mm3(pe, ps[:, :], lambda s: cT[:, s, c, b * P:(b + 1) * P],
                                      lambda s: w[:, Q % 2, s, col:col + QH * P], c == 0, c == KT - 1)
                        ins.then_inc(v_sum, 1)

                    def output(Q):
                        pe.wait_ge(a_lo, r * H + 4 * Q + 4)
                        pe.wait_ge(w_lo, r * (4 * NQD) + CREDIT + 4 * Q + 7)
                        for m in range(2):
                            ps = bank("o", 2 * Q + m)
                            for e in range(2):
                                tok = slice((2 * m + e) * P, (2 * m + e + 1) * P)
                                out = ps[:, e * D:(e + 1) * D]
                                for i in range(QH):
                                    col = 3 * PART + i * D
                                    ins = mm3(pe, out, lambda s: attT[:, s, i, tok],
                                              lambda s: w[:, Q % 2, s, col:col + D],
                                              i == 0, i == QH - 1 and Q < NQD - 1)
                                if Q == NQD - 1:
                                    ins = pe.matmul(out, norm_pT[:, tok], big_g[:, :], start=False, stop=True)
                            ins.then_inc(outp, 1)

                    ln.pe_turn(pe, r, psW, ident)
                    ln.pe_ready(pe, r)
                    ps = bank("x", 0)
                    for b in range(GROUP):
                        for c in range(KT):
                            ins = mm3(pe, ps[:, b * H:(b + 1) * H], lambda s: ln.hT[:, s, c, b * P:(b + 1) * P],
                                      lambda s: u_parts[:, s, c], c == 0, c == KT - 1)
                    ins.then_inc(extra_sum, 1)
                    pe.wait_ge(ctx_in, r * 16 + 16)
                    for n in range(4):
                        project(n)
                        values(n)
                    for n in range(LAST):
                        if 0 <= n - 2 < H:
                            c = n - 2
                            Q, i = divmod(c, 4)
                            pe.wait_ge(expd, r * H + c + 1)
                            if i == 0:
                                pe.wait_ge(v_set, r * H + 4 * (Q + 1))
                            if c >= 1:
                                pe.wait_ge(normed, r * H + c)
                            for b in range(GROUP):
                                ins = pe.matmul(psV[:, b, 0:P + 1], probs[:, c % 3, b * P:(b + 1) * P],
                                                v[:, Q % 2, b, i, :], start=True, stop=True)
                            ins.then_inc(pved, 1)
                        if output_at(n) is not None:
                            output(output_at(n))
                        if 0 <= n - 3 < H:
                            c = n - 3
                            ps = bank("t", c)
                            pe.wait_ge(normed, r * H + c + 1)
                            for b in range(GROUP):
                                ins = pe.transpose(ps[:, b * P:(b + 1) * P], att[:, c % 2, b * P:(b + 1) * P],
                                                   ident[:, :])
                            ins.then_inc(a_turned, 1)
                        if n < H:
                            Q, i = divmod(n, 4)
                            pe.wait_ge(k_set, r * H + n + 1)
                            if n >= 2:
                                pe.wait_ge(eased, r * H + n - 1)
                            for b in range(GROUP):
                                tok = slice(b * P, (b + 1) * P)
                                ins = pe.matmul(psS[n % 2][:, tok], qk[:, n % SLOTS, tok], qk[:, SLOTS + n % SLOTS, tok],
                                                start=True, stop=True)
                            ins.then_inc(scored, 1)
                        if n + 4 < H:
                            project(n + 4)
                        if 0 <= n - 1 < H:
                            c = n - 1
                            pe.wait_ge(eased, r * H + c + 1)
                            if c >= 2:
                                pe.wait_ge(expd, r * H + c - 1)
                            for b in range(GROUP):
                                ins = pe.transpose(psT[c % 2][:, b * P:(b + 1) * P], s_sb[:, c % 2, b * P:(b + 1) * P],
                                                   ident[:, :])
                            ins.then_inc(turned, 1)
                        if n + 4 < H:
                            values(n + 4)
                    pe.wait_ge(np_set, r * H + H)
                    pe.wait_ge(expd, r * H + H)
                    for b in range(GROUP):
                        ins = pe.transpose(psT[0][0:H + 1, b * P:(b + 1) * P], norm_p[:, b, :], ident[:, :])
                    ins.then_inc(np_turned, 1)
                    pe.wait_ge(npT_set, r + 1)
                    output(NQD - 1)



def _columns(parts):
    import numpy as np
    return np.ascontiguousarray(np.concatenate(parts, axis=1))


def _stack_heads(wT, heads, dh, slot, parts=3):
    import numpy as np
    out = np.zeros((wT.shape[0], len(heads) * slot), wT.dtype)
    for i, h in enumerate(heads):
        for r in range(parts):
            out[:, i * slot + r * dh:i * slot + (r + 1) * dh] = wT[:, h * dh:(h + 1) * dh]
    return out


def _lo_rows(slot, dh, part):
    import numpy as np
    m = np.zeros((P, 1), np.float32)
    for i in range(P // slot):
        m[i * slot + part * dh:i * slot + (part + 1) * dh] = -1.0
    return m


def _layer0_arrays(i):
    import numpy as np
    wq, wk = i["L0_xattn_Wq"].T, i["L0_xattn_Wk"].T
    parts = [_stack_heads(wq, range(4 * n, 4 * n + 4), 8, 32) for n in range(4)]
    parts += [_stack_heads(wk, range(4 * n, 4 * n + 4), 8, 32) for n in range(4)]
    parts += [i["L0_xattn_Wv"].T, i["L0_xattn_Wo"].T]
    cols = [_lo_rows(32, 8, 1), _lo_rows(32, 8, 2), i["L0_xattn_bo"][:, None]]
    return {"l0_w": _columns(parts), "l0_cols": _columns(cols)}


def _tiles(w):
    return w.reshape(-1, P, w.shape[1]).transpose(1, 0, 2)


def _per_tile(v):
    return v.reshape(-1, P).T


def _layer1_arrays(i):
    import numpy as np
    g = {k[9:]: v for k, v in i.items() if k.startswith("L1_xattn_")}
    pairs = [range(2 * n, 2 * n + 2) for n in range(8)]
    w = np.concatenate([_stack_heads(g["q_w"], p, 16, 64) for p in pairs]
                       + [_stack_heads(g["k_w"], p, 16, 64) for p in pairs] + [g["v_w"], g["cproj_w"]], axis=1)
    cols = [_lo_rows(64, 16, 1), _lo_rows(64, 16, 2)]
    cols += [_stack_heads(g["q_b"][None], p, 16, 64).T for p in pairs]
    cols += [_stack_heads(g["k_b"][None], p, 16, 64).T for p in pairs]
    cols += [_per_tile(g["ln1_w"]), _per_tile(g["ln1_b"])]
    rows = [g["v_b"], g["cproj_b"], g["ln1_w"], g["ln1_b"]]
    return {"l1_w": _tiles(w), "l1_cols": _columns(cols), "l1_rows": np.concatenate(rows)[None],
            "l1_mask": i["mask_BxS2_bf1"].view(np.int32).reshape(NG, -1)}


def _mlp_arrays(name, fc_w, fc_b, proj_w, proj_b, gamma, beta):
    w = _columns([_tiles(fc_w).reshape(P, -1), _tiles(proj_w).reshape(P, -1)])
    return {name + "_w": w, name + "_cols": _columns([_per_tile(fc_b), _per_tile(gamma), _per_tile(beta)]),
            name + "_rows": proj_b[None]}


def _layer3_arrays(i):
    import numpy as np
    g = {k[9:]: v for k, v in i.items() if k.startswith("L3_xattn_")}
    quads = [[(4 * kt + s) * 4 + m for s in range(4)] for kt in range(2) for m in range(4)]
    kheads = [range(4 * kt, 4 * kt + 4) for kt in range(2)]
    w = np.concatenate([_stack_heads(g["Wq"], q, 8, 32) for q in quads]
                       + [_stack_heads(g["Wk"], k, 8, 32) for k in kheads] + [g["Wv"], g["Wo"]], axis=1)
    cols = [_lo_rows(32, 8, 1), _lo_rows(32, 8, 2)]
    cols += [_stack_heads(g["bq"][None], q, 8, 32).T for q in quads]
    cols += [_stack_heads(g["bk"][None], k, 8, 32).T for k in kheads]
    cols += [_per_tile(g["gamma"]), _per_tile(g["beta"])]
    rows = [g["bv"], g["bo"], g["gamma"], g["beta"]]
    return {"l3_w": _tiles(w), "l3_cols": _columns(cols), "l3_rows": np.concatenate(rows)[None],
            "l3_mask": i["mask_Bx1xSxS2_ff0"].reshape(BATCH, P, P)}


def _layer2_arrays(i):
    import numpy as np
    g = {k[9:]: v for k, v in i.items() if k.startswith("L2_xattn_")}
    qkv, o, cols, ek, bo = [], [], [], [], []
    for n in "12":
        for Q in range(4):
            at = slice(Q * 512, (Q + 1) * 512)
            qkv.append(np.concatenate([_tiles(g["w" + m + n][:, at]).reshape(P, -1) for m in "qkv"], axis=1))
            o.append(_tiles(g["wo" + n][at]).reshape(P, -1))
        cols.append(_columns([_per_tile(g["bq" + n]), _per_tile(g["bk" + n]), _per_tile(g[f"ln{n}_scale"]),
                              _per_tile(g[f"ln{n}_offset"]), _per_tile(g["bias_k" + n].reshape(-1)),
                              _per_tile(g["bias_v" + n].reshape(-1)), _per_tile(g["bv" + n])]))
        ek.append(g["bias_k" + n].reshape(-1))
        bo.append(g["bo" + n])
    return {"l2_qkv": np.stack(qkv), "l2_o": np.stack(o), "l2_cols": np.stack(cols), "l2_ek": np.stack(ek),
            "l2_bo": np.stack(bo)}


def kernel(**inputs):
    import numpy as _np
    import concourse.bacc as _bacc
    from concourse.bass_utils import run_bass_kernel_spmd as _run
    i = {k: _np.asarray(v) for k, v in inputs.items()}
    nc = _bacc.Bacc("TRN2", target_bir_lowering=False, num_devices=1)
    arrays = {"x": i["x"], "ctx": i["ctx_2048"], **_layer0_arrays(i),
              **_layer1_arrays(i),
              **_mlp_arrays("m1", *[i["L1_xattn_" + n] for n in ("fc_w", "fc_b", "proj_w", "proj_b", "ln2_w", "ln2_b")]),
              **_layer2_arrays(i),
              **_mlp_arrays("m2", *[i["L2_xattn_" + n] for n in ("w_fc1", "b_fc1", "w_fc2", "b_fc2", "ln_mlp_scale",
                                                          "ln_mlp_offset")]),
              **_layer3_arrays(i)}
    d = {}
    for name, a in arrays.items():
        a = arrays[name] = _np.ascontiguousarray(a)
        d[name] = nc.dram_tensor("in_" + name, a.shape, mybir.dt.from_np(a.dtype), kind="ExternalInput").ap()
    out = nc.dram_tensor("out", (BATCH, P, D), F32, kind="ExternalOutput").ap()
    ctxT = nc.dram_tensor("ctxT", (NG, P, 2 * KT * TOK), F32, kind="Internal").ap()
    with ExitStack() as ctx:
        X = ctx.enter_context(nc.sbuf_tensor("X", [P, BATCH, D], F32))
        ident = ctx.enter_context(nc.sbuf_tensor("ident", [P, P], F32))
        identity_phase(nc, ident)
        context_phase(nc, d["ctx"], ctxT, ident)
        layer0_phase(nc, d["x"], d["ctx"], d["l0_w"], d["l0_cols"], X, ident)
        heads_phase(nc, 1, X, ctxT, d["l1_w"], d["l1_cols"], d["l1_rows"], d["l1_mask"], ident)
        mlp_phase(nc, "m1", ACT.Gelu_apprx_tanh, X, d["m1_w"], d["m1_cols"], d["m1_rows"], ident)
        clear_semaphores(nc)
        wide_phase(nc, X, ctxT, d, ident)
        mlp_phase(nc, "m2", ACT.Gelu, X, d["m2_w"], d["m2_cols"], d["m2_rows"], ident)
        heads_phase(nc, 3, X, ctxT, d["l3_w"], d["l3_cols"], d["l3_rows"], d["l3_mask"], ident, out)
    r = _run(nc, [{"in_" + k: a for k, a in arrays.items()}], core_ids=[0])
    return r.results[0]["out"]
```

```python
import concourse.bass as bass
from concourse import mybir
from contextlib import ExitStack

F32 = mybir.dt.float32
F32R = mybir.dt.float32r
U8 = mybir.dt.uint8
I32 = mybir.dt.int32
ALU = mybir.AluOpType
ACT = mybir.ActivationFunctionType
AX = mybir.AxisListType

P = 128
BATCH = 16
D = 256
GROUP = 4
NG = BATCH // GROUP
TOK = GROUP * P
KT = D // P
PASSES = ((0, 0), (0, 1), (1, 0))
F32_LOWEST = 3.4028234663852886e38


def mm3(pe, out, lhs, rhs, first, last, terms=PASSES):
    for n, (a, b) in enumerate(terms):
        ins = pe.matmul(out, lhs(a), rhs(b), start=first and n == 0, stop=last and n == len(terms) - 1)
    return ins


class Buffers:

    def __init__(self, nc, ctx, phase):
        self.nc, self.ctx, self.phase = nc, ctx, phase

    def sb(self, name, shape, dt=F32):
        return self.ctx.enter_context(self.nc.sbuf_tensor(f"{self.phase}_{name}", shape, dt))

    def bank(self, name):
        return self.ctx.enter_context(self.nc.psum_tensor(f"{self.phase}_{name}", [P, 512], F32))

    def sem(self, name):
        return self.ctx.enter_context(self.nc.semaphore(f"{self.phase}_{name}"))


class Stage:

    def __init__(self, nc, ctx, d):
        self.d = d
        self.raw = ctx.enter_context(nc.sbuf_tensor("stage", [P, 2 * 3 * KT * 4 * P], F32))
        self.arrived = {name: [ctx.enter_context(nc.semaphore(f"{name}_arrived{n}")) for n in range(2)]
                        for name in ("l1", "m1", "l2", "m2", "l3")}

    def load(self, eng, name):
        if name == "l2":
            parts = [self.d["l2_qkv"][Q] for Q in range(2)]
        elif name in ("m1", "m2"):
            w, half = self.d[name + "_w"], KT * 4 * D
            parts = [w[:, 0:half], w[:, half:w.shape[1]]]
        else:
            parts = [self.d[name + "_w"][:, k] for k in range(KT)]
        at = 0
        for part, sem in zip(parts, self.arrived[name]):
            eng.dma_start(self.raw[:, at:at + part.shape[1]], part).then_inc(sem, 16)
            at += part.shape[1]


def clear_semaphores(nc):
    with nc.Block() as block:
        @block.gpsimd
        def _(pool):
            pool.sem_clear(range(min(nc.free_semaphores), max(nc.free_semaphores) + 1))


def identity_phase(nc, ident):
    with ExitStack() as ctx:
        t = Buffers(nc, ctx, "id")
        cleared = t.sem("cleared")
        block = ctx.enter_context(nc.Block())

        @block.gpsimd
        def _(pool):
            pool.memset(ident[:, :], 0.0).then_inc(cleared, 1)
            pool.wait_ge(cleared, 1)
            pool.affine_select(out=ident[:, :], in_=ident[:, :], compare_op=ALU.not_equal, fill=1.0,
                               base=0, pattern=[[-1, P]], channel_multiplier=1)


def load_context(eng, cT, ctxT_dram, g):
    return eng.dma_start(cT[:, :, :, :, :].rearrange("p b s k n -> p b (s k n)").bitcast(F32),
                         ctxT_dram[bass.ds(g * GROUP, GROUP)].rearrange("b p n -> p b n"))


def layer0_phase(nc, x_dram, ctx_dram, w_dram, cols_dram, X, ctxT_dram, ident, stage, ahead):
    H, DH, L = 16, 8, D
    LB = L // P
    SLOT = 32
    NT = H // 4
    NQ, NK, NV = 0, NT * P, 2 * NT * P
    NO = NV + P
    NW = NO + P
    SCALE = float(DH) ** -0.5
    PER = 2 * H
    ITS = BATCH // 2
    USES = ["c", "p0", "p1", "v", "p2", "a", "p3", "o"]
    with ExitStack() as ctx:
        t = Buffers(nc, ctx, "l0")
        w_raw = t.sb("w_raw", [P, NW])
        w = t.sb("w", [P, 2, NW], F32R)
        cols = t.sb("cols", [P, 3])
        c_raw = t.sb("c_raw", [P, 2, L])
        xcs = t.sb("xcs", [P, 2, 2, L], F32R)
        top = t.sb("top", [P, 2, 2, L], F32R)
        qk = t.sb("qk", [P, 2, NT, 2, L], F32R)
        v = t.sb("v", [P, 2, LB, H, 32])
        s_sb = t.sb("s_sb", [P, 2, LB, L])
        peak = t.sb("peak", [P, H, LB])
        probs = t.sb("probs", [P, 8, LB, L])
        o_sb = t.sb("o_sb", [P, 2, L])
        rden = t.sb("rden", [P, NT, LB, 4])
        att = t.sb("att", [P, LB, P])
        attT = t.sb("attT", [P, 2, L], F32R)
        cT = t.sb("cT", [P, 2, 2, L], F32R)
        psS = [t.bank(f"psS{i}") for i in range(2)]
        psT = [t.bank(f"psT{i}") for i in range(2)]
        psO, psN = t.bank("psO"), t.bank("psN")
        psW = [t.bank(f"psW{i}") for i in range(2)]
        (weights, x_in, w_hi, w_lo, x_hi, x_lo, proj, rounded, stacked, vproj, v_set, v_ones, scored,
         peaked, eased, turned, expd, pved, o_out, o_turned, r_done, normed, a_turned, a_hi, a_lo, outp, x_set,
         act_eased, c_turned, c_hi, c_lo, gate) = [
            t.sem(n) for n in ("weights x_in w_hi w_lo x_hi x_lo proj rounded stacked vproj v_set v_ones scored "
                               "peaked eased turned expd pved o_out o_turned r_done normed a_turned a_hi a_lo outp "
                               "x_set act_eased c_turned c_hi c_lo gate").split()]
        c_in = [t.sem(f"c_in{i}") for i in range(2)]
        c_stored = [t.sem(f"c_stored{i}") for i in range(2)]
        block = ctx.enter_context(nc.Block())

        def pipeline(eng, step):
            for s in range(H):
                step(0, s, False)
            with eng.Fori(0, ITS - 1) as it:
                for s in range(H, H + PER):
                    step(it, s, False)
            for s in range(H, PER + H):
                step(ITS - 1, s, True)

        def ease_count(it, s):
            return act_eased if s % 2 else eased, H * it + s // 2 + 1

        def use_at(it, s, last):
            n = s % H // 2
            if s % H % 2:
                return None, 0, 0
            k = s // H + (-1 if USES[n] in "ao" else 1)
            if last and k >= 2 or isinstance(it, int) and 2 * it + k < 0:
                return None, 0, 0
            return USES[n], k, (s // H * len(USES) + n) % 2

        @block.sync
        def _(sp):
            sp.dma_start(w_raw[:, :], w_dram).then_inc(weights, 16)
            sp.dma_start(cols[:, :], cols_dram).then_inc(weights, 16)

            def load(it, k):
                sp.dma_start(c_raw[:, k % 2], ctx_dram[bass.ds(it * 2 + k, 1)].rearrange("a p l -> p (a l)"))\
                    .then_inc(c_in[k % 2], 16)

            sp.dma_start(X[:, 0:2, :], x_dram[0:2].rearrange("b p l -> p b l")).then_inc(x_in, 16)
            load(0, 0)
            load(0, 1)
            sp.dma_start(X[:, 2:BATCH, :], x_dram[2:BATCH].rearrange("b p l -> p b l")).then_inc(x_in, 16)
            if ahead:
                stage.load(sp, ahead)

            def store(it, k):
                sp.wait_ge(c_lo, 2 * it + k + 1)
                sp.wait_ge(weights, 32)
                sp.dma_start(ctxT_dram[bass.ds(it * 2 + k, 1)].rearrange("a p n -> p (a n)"),
                             cT[:, k % 2].rearrange("p s n -> p (s n)").bitcast(F32)).then_inc(c_stored[k % 2], 16)

            store(0, 0)
            with sp.Fori(0, ITS - 1) as it:
                for k in (2, 3):
                    sp.wait_ge(x_lo, 4 * it + 2 * (k - 1))
                    sp.wait_ge(weights, 32)
                    sp.wait_ge(c_turned, 2 * it + k - 1)
                    sp.wait_ge(weights, 32)
                    load(it, k)
                    store(it, k - 1)
            store(ITS - 1, 1)
            for sem in c_stored:
                sp.wait_ge(sem, 16 * ITS)

        @block.gpsimd
        def _(pool):
            pool.memset(v[:, :, :, :, :], 0.0).then_inc(v_ones, 1)
            pool.wait_ge(v_ones, 1)
            pool.memset(v[:, :, :, :, DH:DH + 1], 1.0).then_inc(v_ones, 1)

            def lo(it, k):
                pool.wait_ge(x_hi, 4 * it + 2 * k + 2)
                pool.sem_inc(gate, 1)
                pool.tensor_tensor(xcs[:, 1, 0], X[:, bass.ds(2 * it + k, 1), :].rearrange("p a l -> p (a l)"),
                                   xcs[:, 0, 0].bitcast(F32), ALU.subtract).then_inc(x_lo, 1)
                pool.tensor_tensor(xcs[:, 1, 1], c_raw[:, k % 2], xcs[:, 0, 1].bitcast(F32),
                                   ALU.subtract).then_inc(x_lo, 1)

            lo(0, 0)
            lo(0, 1)
            with pool.Fori(0, ITS - 1) as it:
                for k in (2, 3):
                    lo(it, k)

        @block.scalar
        def _(act):
            def split(it, k):
                if k >= 1:
                    act.wait_ge(proj, NT * (2 * it + k))
                if k >= 2:
                    act.wait_ge(x_in, 32)
                act.wait_ge(c_in[k % 2], 16 * (it + k // 2 + 1))
                act.activation(xcs[:, 0, 0], X[:, bass.ds(2 * it + k, 1), :].rearrange("p a l -> p (a l)"),
                               ACT.Copy).then_inc(x_hi, 1)
                act.activation(xcs[:, 0, 1], c_raw[:, k % 2], ACT.Copy).then_inc(x_hi, 1)

            def use(it, s, last):
                name, k, n_ps = use_at(it, s - 1, last)
                if name is None:
                    return
                ps = psW[n_ps]
                if name == "c":
                    act.wait_ge(c_turned, 2 * it + k + 1)
                    if k >= 2:
                        act.wait_ge(c_stored[k % 2], 16 * (it + k // 2))
                    act.activation(cT[:, k % 2, 0], ps[:, 0:L], ACT.Copy).then_inc(c_hi, 1)
                elif name == "v":
                    act.wait_ge(vproj, 2 * it + k + 1)
                    if k >= 2:
                        act.wait_ge(pved, NT * (2 * it + k - 1))
                    act.activation(v[:, k % 2, :, :, 0:DH], ps[:, 0:LB * P]
                                   .rearrange("p (k h d) -> p k h d", k=LB, h=H), ACT.Copy).then_inc(v_set, 1)
                elif name == "a":
                    act.wait_ge(a_turned, 2 * it + k + 1)
                    act.activation(attT[:, 0], ps[:, 0:L], ACT.Copy).then_inc(a_hi, 1)
                elif name != "o":
                    n = int(name[1])
                    act.wait_ge(proj, NT * (2 * it + k) + n + 1)
                    if k > 0 or n >= 2:
                        act.wait_ge(stacked, 2 * (NT * (2 * it + k) + n - 1))
                    act.activation(top[:, n % 2], ps[:, :].rearrange("p (a l) -> p a l", a=2), ACT.Copy)\
                        .then_inc(rounded, 1)

            def step(it, s, last):
                if s % H == 0 and not last:
                    split(it, s // H + 1)
                n, i = divmod(s - 9, 4)
                if i == 0 and n >= 0 and not (last and n >= 2 * NT):
                    act.wait_ge(pved, 2 * NT * it + n + 1)
                    if n >= 2:
                        act.wait_ge(o_turned, 2 * NT * it + n - 1)
                    act.activation(o_sb[:, n % 2], psO[:, 0:L], ACT.Copy).then_inc(o_out, 1)
                use(it, s, last)
                h = s - 2
                if h >= 0 and not (last and h >= PER):
                    act.wait_ge(turned, PER * it + h + 1)
                    if h >= 8:
                        act.wait_ge(pved, 2 * NT * it + h // 4 - 1)
                    act.activation(probs[:, h % 8], psT[h % 2][:, :].rearrange("p (k q) -> p k q", k=LB),
                                   ACT.Exp, scale=-SCALE if h % 2 else SCALE).then_inc(expd, 1)
                if s % 2 and not (last and s >= PER):
                    act.wait_ge(peaked, PER * it + s + 1)
                    if s >= 2:
                        act.wait_ge(turned, PER * it + s - 1)
                    for q in range(LB):
                        ins = act.activation(s_sb[:, s % 2, q], psS[s % 2][:, q * L:(q + 1) * L], ACT.Identity,
                                             bias=peak[:, s % H, q:q + 1], scale=-1.0)
                    ins.then_inc(act_eased, 1)
            act.wait_ge(weights, 32)
            act.activation(w[:, 0], w_raw[:, :], ACT.Copy).then_inc(w_hi, 1)
            act.wait_ge(v_ones, 2)
            act.wait_ge(x_in, 16)
            split(0, 0)
            for s in range(H):
                use(0, s - H, False)
            pipeline(act, step)

        @block.vector
        def _(dve):
            def use(it, s, last):
                name, k, n_ps = use_at(it, s - 1, last)
                if name is None or name == "v":
                    return
                ps = psW[n_ps]
                if name == "c":
                    dve.wait_ge(c_hi, 2 * it + k + 1)
                    dve.tensor_tensor(cT[:, k % 2, 1], ps[:, 0:L], cT[:, k % 2, 0].bitcast(F32), ALU.subtract)\
                        .then_inc(c_lo, 1)
                elif name == "a":
                    dve.wait_ge(a_hi, 2 * it + k + 1)
                    dve.tensor_tensor(attT[:, 1], ps[:, 0:L], attT[:, 0].bitcast(F32), ALU.subtract)\
                        .then_inc(a_lo, 1)
                elif name == "o":
                    xb = X[:, bass.ds(2 * it + k, 1), :].rearrange("p a d -> p (a d)")
                    dve.wait_ge(outp, 2 * it + k + 1)
                    dve.scalar_tensor_tensor(xb, ps[:, 0:L], cols[:, 2:3], xb, ALU.add, ALU.add).then_inc(x_set, 1)
                else:
                    n = int(name[1])
                    dve.wait_ge(rounded, NT * (2 * it + k) + n + 1)
                    for j in range(2):
                        dve.scalar_tensor_tensor(qk[:, k % 2, n, j], top[:, n % 2, j].bitcast(F32), cols[:, j:j + 1],
                                                 ps[:, j * L:(j + 1) * L], ALU.mult, ALU.add).then_inc(stacked, 1)

            def step(it, s, last):
                if not (last and s >= PER):
                    dve.wait_ge(scored, PER * it + s + 1)
                    dve.tensor_reduce(peak[:, s % H], psS[s % 2][:, :].rearrange("p (q k) -> p q k", q=LB), AX.X,
                                      ALU.max).then_inc(peaked, 1)
                    if s % 2 == 0:
                        dve.wait_ge(peaked, PER * it + s + 1)
                        if s >= 2:
                            dve.wait_ge(turned, PER * it + s - 1)
                        dve.tensor_tensor(s_sb[:, s % 2], psS[s % 2][:, :].rearrange("p (q k) -> p q k", q=LB),
                                          peak[:, s % H].rearrange("p (q a) -> p q a", a=1).to_broadcast([P, LB, L]),
                                          ALU.subtract).then_inc(eased, 1)
                n, i = divmod(s - 11, 4)
                if i == 0 and n >= 0 and not (last and n >= 2 * NT):
                    dve.wait_ge(o_turned, 2 * NT * it + n + 1)
                    o = psN[:, 0:LB * P].rearrange("p (q i c) -> p q i c", q=LB, i=4)
                    dve.reciprocal(rden[:, n % NT], o[:, :, :, DH]).then_inc(r_done, 1)
                    dve.wait_ge(r_done, 2 * NT * it + n + 1)
                    if n % NT == 0 and n > 0:
                        dve.wait_ge(a_turned, 2 * it + n // NT)
                    dve.tensor_tensor(att[:, :, n % NT * 32:(n % NT + 1) * 32]
                                      .rearrange("p q (i d) -> p q i d", i=4), o[:, :, :, 0:DH],
                                      rden[:, n % NT].rearrange("p q (i a) -> p q i a", a=1)
                                      .to_broadcast([P, LB, 4, DH]), ALU.mult).then_inc(normed, 1)
                use(it, s, last)

            dve.wait_ge(w_hi, 1)
            dve.tensor_tensor(w[:, 1], w_raw[:, :], w[:, 0].bitcast(F32), ALU.subtract).then_inc(w_lo, 1)
            dve.memset(peak[:, :, :], 0.0).then_inc(x_set, 1)
            for s in range(H):
                use(0, s - H, False)
            pipeline(dve, step)

        @block.tensor
        def _(pe):
            def bank_free(it, s, last):
                name, k, _ = use_at(it, s - 4, last)
                if name == "c":
                    pe.wait_ge(c_lo, 2 * it + k + 1)
                elif name == "v":
                    pe.wait_ge(v_set, 2 * it + k + 1)
                elif name == "a":
                    pe.wait_ge(a_lo, 2 * it + k + 1)
                elif name == "o":
                    pe.wait_ge(x_set, 2 * it + k + 2)
                elif name is not None:
                    pe.wait_ge(stacked, 2 * (NT * (2 * it + k) + int(name[1]) + 1))

            def use(it, s, last):
                name, k, n_ps = use_at(it, s, last)
                if name is None:
                    return
                bank_free(it, s, last)
                ps = psW[n_ps]
                if name == "c":
                    pe.wait_ge(c_in[k % 2], 16 * (it + k // 2 + 1))
                    for j in range(KT):
                        ins = pe.transpose(ps[:, j * P:(j + 1) * P], c_raw[:, k % 2, j * P:(j + 1) * P], ident[:, :])
                    ins.then_inc(c_turned, 1)
                elif name == "v":
                    for j in range(LB):
                        ins = mm3(pe, ps[:, j * P:(j + 1) * P], lambda e: xcs[:, e, 1, j * P:(j + 1) * P],
                                  lambda e: w[:, e, NV:NV + P], True, True)
                    ins.then_inc(vproj, 1)
                elif name == "a":
                    pe.wait_ge(normed, NT * (2 * it + k + 1))
                    for q in range(LB):
                        ins = pe.transpose(ps[:, q * P:(q + 1) * P], att[:, q], ident[:, :])
                    ins.then_inc(a_turned, 1)
                elif name == "o":
                    pe.wait_ge(a_lo, 2 * it + k + 1)
                    mm3(pe, ps[:, 0:L], lambda e: w[:, e, NO:NO + P], lambda e: attT[:, e], True, True)\
                        .then_inc(outp, 1)
                else:
                    n = int(name[1])
                    if n == 0:
                        pe.wait_ge(x_lo, 2 * (2 * it + k) + 2)
                    for j, col in ((0, NQ), (1, NK)):
                        ins = mm3(pe, ps[:, j * L:(j + 1) * L], lambda e: w[:, e, col + n * P:col + (n + 1) * P],
                                  lambda e: xcs[:, e, j], True, True)
                    ins.then_inc(proj, 1)

            def step(it, s, last):
                if not (last and s >= PER):
                    k, h = divmod(s, H)
                    n, i = divmod(h, 4)
                    rows = slice(i * SLOT, (i + 1) * SLOT)
                    if i == 0:
                        pe.wait_ge(stacked, 2 * (NT * (2 * it + k) + n + 1))
                    if s >= 2:
                        pe.wait_ge(*ease_count(it, s - 2))
                    for q in range(LB):
                        ins = pe.matmul(psS[s % 2][:, q * L:(q + 1) * L], qk[rows, k % 2, n, 0, q * P:(q + 1) * P],
                                        qk[rows, k % 2, n, 1, :], start=True, stop=True)
                    ins.then_inc(scored, 1)
                h = s - 2
                if h >= 0 and not (last and h >= PER):
                    pe.wait_ge(*ease_count(it, h))
                    if h >= 2:
                        pe.wait_ge(expd, PER * it + h - 1)
                    for q in range(LB):
                        for j in range(LB):
                            ins = pe.transpose(psT[h % 2][:, j * L + q * P:j * L + (q + 1) * P],
                                               s_sb[:, h % 2, q, j * P:(j + 1) * P], ident[:, :])
                    ins.then_inc(turned, 1)
                n, i = divmod(s - 7, 4)
                if i < LB and n >= 0 and not (last and n >= 2 * NT):
                    if i == 0:
                        pe.wait_ge(expd, PER * it + 4 * (n + 1))
                        if n % NT == 0:
                            pe.wait_ge(v_set, 2 * it + n // NT + 1)
                        if n >= 1:
                            pe.wait_ge(o_out, 2 * NT * it + n)
                    for m in range(4):
                        h = 4 * n + m
                        ins = pe.matmul(psO[32 * m:32 * m + 32, 0:L], v[:, n // NT % 2, i, h % H, :],
                                        probs[:, h % 8, i, :], start=i == 0, stop=i == LB - 1)
                    if i == LB - 1:
                        ins.then_inc(pved, 1)
                n, i = divmod(s - 10, 4)
                if i == 0 and n >= 0 and not (last and n >= 2 * NT):
                    pe.wait_ge(o_out, 2 * NT * it + n + 1)
                    if n >= 1:
                        pe.wait_ge(normed, 2 * NT * it + n)
                    for q in range(LB):
                        ins = pe.transpose(psN[:, q * P:(q + 1) * P], o_sb[:, n % 2, q * P:(q + 1) * P], ident[:, :])
                    ins.then_inc(o_turned, 1)
                use(it, s, last)

            pe.wait_ge(w_lo, 1)
            pe.wait_ge(v_ones, 2)
            for s in range(H):
                use(0, s - H, False)
            pipeline(pe, step)


class TokenNorm:

    def __init__(self, t, eps, gamma=None, beta=None, xn=None, full=None):
        self.eps, self.gamma, self.beta = eps, gamma, beta
        self.stats = t.sb("ln_stats", [P, GROUP, 6])
        self.mean_var = t.sb("ln_mean_var", [P, GROUP, 2])
        self.power = t.sb("ln_power", [P, GROUP])
        self.shifted = t.sb("ln_shifted", [P, GROUP])
        self.rstd = t.sb("ln_rstd", [P, GROUP])
        self.xn = t.sb("ln_xn", [P, GROUP, D]) if xn is None else xn
        self.full = t.sb("ln_full", [P, KT, TOK]) if full is None else full
        self.hT = t.sb("hT", [P, 2, KT, TOK], F32R)
        (self.s_gate, self.s_power_set, self.s_gathered, self.s_aggregated, self.s_shift, self.s_rooted,
         self.s_normed, self.s_turned, self.s_affine, self.s_hi, self.s_lo) = [
            t.sem("ln_" + n) for n in ("gate power_set gathered aggregated shift rooted normed turned affine "
                                       "hi lo").split()]

    def pool_setup(self, pool):
        pool.memset(self.power[:, :], -0.5).then_inc(self.s_power_set, 1)

    def dve_statistics(self, dve, g, x):
        for b in range(GROUP):
            dve.bn_stats(self.stats[:, b], x(b)).then_inc(self.s_gathered, 1)
        for b in range(GROUP):
            dve.wait_ge(self.s_gathered, g * GROUP + b + 1)
            dve.sem_inc(self.s_gate, 1)
            dve.bn_aggr(self.mean_var[:, b], self.stats[:, b]).then_inc(self.s_aggregated, 1)

    def pool_rstd(self, pool, g):
        pool.wait_ge(self.s_aggregated, g * GROUP + GROUP)
        pool.sem_inc(self.s_gate, 1)
        pool.wait_ge(self.s_power_set, 1)
        pool.tensor_scalar(self.shifted[:, :], self.mean_var[:, :, 1], self.eps, 1.0, ALU.add, ALU.mult)\
            .then_inc(self.s_shift, 1)
        pool.wait_ge(self.s_shift, g + 1)
        pool.tensor_tensor(self.rstd[:, :], self.shifted[:, :], self.power[:, :], ALU.pow).then_inc(self.s_rooted, 1)

    def dve_normalise(self, dve, g, x, out=None):
        out = self.xn if out is None else out
        if self.eps is None:
            for b in range(GROUP):
                dve.tensor_copy(out[:, b], x(b)).then_inc(self.s_normed, 1)
            return
        dve.wait_ge(self.s_rooted, g + 1)
        for b in range(GROUP):
            dve.tensor_scalar(out[:, b], x(b), self.mean_var[:, b, 0:1], self.rstd[:, b:b + 1],
                              ALU.subtract, ALU.mult).then_inc(self.s_normed, 1)

    def pe_turn_tile(self, pe, g, k, ps, ident):
        for b in range(GROUP):
            pe.wait_ge(self.s_normed, g * GROUP + b + 1)
            ins = pe.transpose(ps[:, b * P:(b + 1) * P], self.xn[:, b, k * P:(k + 1) * P], ident[:, :])
        ins.then_inc(self.s_turned, 1)

    def pe_turn(self, pe, g, banks, ident):
        for k in range(KT):
            self.pe_turn_tile(pe, g, k, banks[k], ident)

    def act_affine_tile(self, act, k, ps):
        if self.gamma is None:
            act.activation(self.full[:, k], ps[:, :], ACT.Copy).then_inc(self.s_affine, 1)
        else:
            act.activation(self.full[:, k], ps[:, :], ACT.Identity, scale=self.gamma[:, k:k + 1],
                           bias=self.beta[:, k:k + 1]).then_inc(self.s_affine, 1)

    def act_hi_tile(self, act, k):
        act.activation(self.hT[:, 0, k], self.full[:, k], ACT.Copy).then_inc(self.s_hi, 1)

    def act_affine(self, act, g, banks):
        for k in range(KT):
            act.wait_ge(self.s_turned, g * KT + k + 1)
            self.act_affine_tile(act, k, banks[k])
        for k in range(KT):
            act.wait_ge(self.s_affine, g * KT + k + 1)
            self.act_hi_tile(act, k)

    def dve_lo_tile(self, dve, k):
        dve.tensor_tensor(self.hT[:, 1, k], self.full[:, k], self.hT[:, 0, k].bitcast(F32), ALU.subtract)\
            .then_inc(self.s_lo, 1)

    def dve_lo(self, dve, g):
        for k in range(KT):
            dve.wait_ge(self.s_hi, g * KT + k + 1)
            self.dve_lo_tile(dve, k)

    def pe_ready(self, pe, g):
        pe.wait_ge(self.s_lo, g * KT + KT)


def heads_phase(nc, layer, X, ctxT_dram, cols_dram, rows_dram, mask_dram, ident, stage, ahead=None, out_dram=None):
    first = layer == 1
    H, DH, SLOT = (16, 16, 64) if first else (32, 8, 32)
    KV = 16 if first else 8
    QT, KTILES = (8, 8) if first else (8, 2)
    NQD = H // 4
    VC = KV * DH
    SCALE = float(DH) ** -0.5
    NQ, NK, NV = 0, QT * P, (QT + KTILES) * P
    NO = NV + VC
    NW = NO + D
    C_MASK, C_BIAS, C_G, C_B = 0, 2, 2 + QT + KTILES, 2 + QT + KTILES + KT
    NC = C_B + KT
    R_V, R_O, R_G, R_B = 0, VC, VC + D, VC + 2 * D
    NR = VC + 3 * D
    TURN = 3
    SPREAD = 0 if first else 1
    VALUES = TURN + 5 if first else TURN + 4
    SLOTS = 8
    READ = VALUES + SPREAD + 1
    TURN_OUT, NORM = READ + 1, READ + 2
    T0 = NORM + 1 if first else NORM + 6
    CREDIT = 2
    if first:
        when = {"t0": -3, "t1": -3, "q0": -2, "k0": -2, "q1": -1, "k1": -1}
        for u in range(2, QT):
            when[f"q{u}"] = when[f"k{u}"] = 2 * u - 3
    else:
        when = {"t0": -6, "t1": -6, "q0": -4, "k0": -3, "k1": 11}
        for u in range(1, QT):
            when[f"q{u}"] = 4 * u - 3
    when.update({"v0": 4, "v1": 4, "v2": 5, "v3": 6, "a0": H + NORM - 3, "a1": H + NORM - 3, "o0": H + NORM - 1,
                 "o1": H + NORM - 1})
    cycle = sorted(when, key=lambda name: when[name] % H)
    tiles = [name for name in sorted(when, key=lambda name: when[name]) if name[0] in "qk"]

    def place(c):
        n, i = c // 4, c % 4
        return (c // 2, SLOT * (c % 2), c // 2, c) if first else (n, SLOT * i, n // 4, 4 * (n // 4) + i)

    def real(it, k):
        return not isinstance(it, int) or 0 <= it + k < NG

    def uses_at(it, s):
        out = []
        for pos, name in enumerate(cycle):
            k, r = divmod(s - when[name], H)
            if r == 0 and real(it, k):
                out.append((name[0], int(name[1]), k, pos % 2))
        return out

    def pipeline(eng, step):
        for s in range(-H, T0):
            step(0, s)
        with eng.Fori(0, NG - 1) as it:
            for s in range(T0, T0 + H):
                step(it, s)
        for s in range(T0, 2 * H):
            step(NG - 1, s)

    with ExitStack() as ctx:
        t = Buffers(nc, ctx, f"l{layer}")
        cols = t.sb("cols", [P, NC])
        rows = t.sb("rows", [P, NR])
        w = t.sb("w", [P, 2, KT, NW], F32R)
        w_raw = stage.raw[:, 0:KT * NW].rearrange("p (k n) -> p k n", k=KT)
        cT = t.sb("cT", [P, GROUP, 2, KT, P], F32R)
        mask = t.sb("mask", [P, TOK])
        mask_raw = t.sb("mask_raw", [P, TOK // 4], I32) if first else t.sb("mask_raw", [P, TOK])
        full = t.sb("full", [P, 2, TOK])
        top = t.sb("top", [P, 2, TOK], F32R)
        qk = t.sb("qk", [P, QT + KTILES, TOK], F32R)
        vt = t.sb("vt", [P, 2, VC])
        v = t.sb("v", [P, GROUP, KV, 32])
        s_sb = t.sb("s_sb", [P, 4, TOK])
        peak = t.sb("peak", [P, H, GROUP])
        probs = t.sb("probs", [P, SLOTS, TOK])
        o_sb = t.sb("o_sb", [P, 2, TOK])
        rden = t.sb("rden", [P, NQD, GROUP, 4])
        att = t.sb("att", [P, GROUP, D])
        attT = t.sb("attT", [P, 2, KT, TOK], F32R)
        xb = t.sb("xb", [P, GROUP, D])
        y, yn = (None, None) if first else (t.sb("y", [P, GROUP, D]), t.sb("yn", [P, GROUP, D]))
        ln = TokenNorm(t, 1e-5 if first else None, cols[:, C_G:C_G + KT] if first else None,
                       cols[:, C_B:C_B + KT] if first else None)
        psS = [t.bank(f"psS{i}") for i in range(2)]
        psT = [t.bank(f"psT{i}") for i in range(2)]
        psO, psN = t.bank("psO"), t.bank("psN")
        psW = [t.bank(f"psW{i}") for i in range(2)]
        (rows_in, w_hi, w_lo, w_lo_pool, loaded, mask_in, mask_set, q_sum, k_sum, v_sum, biased, topped,
         stacked, v_read, v_set, v_ones, scored, masked, peaked, eased, turned, expd, pved, o_out, o_turned, r_done,
         normed, a_turned, a_hi, a_lo, outp, x_biased, added, y_stats, y_mean, y_shift, y_rstd, y_normed, y_scaled,
         y_set, y_left, stored) = [
            t.sem(n) for n in ("rows_in w_hi w_lo w_lo_pool loaded mask_in mask_set q_sum k_sum v_sum biased "
                               "topped stacked v_read v_set v_ones scored masked peaked eased turned expd pved o_out "
                               "o_turned r_done normed a_turned a_hi a_lo outp x_biased added y_stats y_mean y_shift "
                               "y_rstd y_normed y_scaled y_set y_left stored").split()]
        w_in = stage.arrived[f"l{layer}"]
        block = ctx.enter_context(nc.Block())

        def tile_count(it, k, name):
            return (it + k) * len(tiles) + tiles.index(name) + 1

        @block.sync
        def _(sp):
            sp.dma_start(cols[:, :], cols_dram).then_inc(rows_in, 16)
            sp.dma_start(rows[:, :], rows_dram.to_broadcast([P, NR])).then_inc(rows_in, 16)

            def load(g):
                load_context(sp, cT, ctxT_dram, g).then_inc(loaded, 16)

            def load_mask(g):
                if first:
                    sp.dma_start(mask_raw[:, :], mask_dram[bass.ds(g, 1)].to_broadcast([P, TOK // 4]))\
                        .then_inc(mask_in, 16)
                else:
                    sp.dma_start(mask_raw[:, :].rearrange("p (b k) -> p b k", b=GROUP),
                                 mask_dram[bass.ds(g * GROUP, GROUP)].rearrange("b q k -> q b k")).then_inc(mask_in, 16)

            def store(g):
                if not first:
                    sp.wait_ge(y_set, g + 1)
                    sp.wait_ge(rows_in, 32)
                    sp.dma_start(out_dram[bass.ds(g * GROUP, GROUP)].rearrange("b q d -> q b d"), y[:, :, :])\
                        .then_inc(stored, 16)
                    sp.wait_ge(stored, 16 * (g + 1))
                    sp.sem_inc(y_left, 1)

            load(0)
            load_mask(0)
            if ahead:
                for sem in (w_lo, w_lo_pool):
                    sp.wait_ge(sem, 1)
                stage.load(sp, ahead)
            sp.sem_inc(y_left, 1)
            with sp.Fori(0, NG - 1) as it:
                sp.wait_ge(mask_set, it + 1)
                sp.wait_ge(rows_in, 32)
                load_mask(it + 1)
                sp.wait_ge(v_sum, it * GROUP + GROUP)
                sp.wait_ge(rows_in, 32)
                sp.wait_ge(k_sum, it * KTILES + KTILES)
                sp.wait_ge(rows_in, 32)
                load(it + 1)
                store(it)
            store(NG - 1)
        @block.gpsimd
        def _(pool):
            def step(it, s):
                k, r = divmod(s, H)
                if not first and r == NORM + 2 and real(it, k - 1):
                    pool.wait_ge(y_mean, (it + k) * GROUP)
                    pool.sem_inc(ln.s_gate, 1)
                    pool.tensor_scalar(ln.shifted[:, :], ln.mean_var[:, :, 1], 1e-6, 1.0, ALU.add, ALU.mult)\
                        .then_inc(y_shift, 1)
                    pool.wait_ge(y_shift, it + k)
                    pool.tensor_tensor(ln.rstd[:, :], ln.shifted[:, :], ln.power[:, :], ALU.pow).then_inc(y_rstd, 1)
                if not first and r == NORM + 4 and real(it, k - 1):
                    pool.wait_ge(y_normed, (it + k) * GROUP)
                    pool.tensor_tensor(yn[:, :, :], yn[:, :, :],
                                       rows[:, R_G:R_G + D].rearrange("p (a d) -> p a d", a=1)
                                       .to_broadcast([P, GROUP, D]), ALU.mult).then_inc(y_scaled, 1)
                if not first and r == NORM + 5 and real(it, k - 1):
                    pool.wait_ge(y_scaled, it + k)
                    pool.wait_ge(y_left, it + k)
                    pool.tensor_tensor(y[:, :, :], yn[:, :, :],
                                       rows[:, R_B:R_B + D].rearrange("p (a d) -> p a d", a=1)
                                       .to_broadcast([P, GROUP, D]), ALU.add).then_inc(y_set, 1)
                if 0 <= s and real(it, k):
                    pool.wait_ge(peaked, it * H + s + 1)
                    sc = s_sb[:, s % 4].rearrange("p (b k) -> p b k", b=GROUP)
                    pool.tensor_tensor(sc, sc, peak[:, r].rearrange("p (b a) -> p b a", a=1)
                                       .to_broadcast([P, GROUP, P]), ALU.subtract).then_inc(eased, 1)
                if first and r == T0 and real(it, k + 1):
                    ln.pool_rstd(pool, it + k + 1)
                if r == (H - 1 if first else T0 + 4) and real(it, k) and s >= 0:
                    pool.tensor_tensor(xb[:, :, :], X[:, bass.ds((it + k) * GROUP, GROUP), :],
                                       rows[:, R_O:R_O + D].rearrange("p (a d) -> p a d", a=1)
                                       .to_broadcast([P, GROUP, D]), ALU.add).then_inc(x_biased, 1)

            pool.memset(v[:, :, :, :], 0.0).then_inc(v_ones, 1)
            pool.wait_ge(v_ones, 1)
            pool.memset(v[:, :, :, DH:DH + 1], 1.0).then_inc(v_ones, 1)
            ln.pool_setup(pool)
            pool.wait_ge(w_hi, 2)
            pool.tensor_tensor(w[:, 1, 1], w_raw[:, 1], w[:, 0, 1].bitcast(F32), ALU.subtract).then_inc(w_lo_pool, 1)
            pool.wait_ge(rows_in, 32)
            pipeline(pool, step)

        @block.scalar
        def _(act):
            def use(it, kind, n, k, bank):
                G, ps = it + k, psW[bank]
                if kind == "t":
                    act.wait_ge(ln.s_turned, G * KT + n + 1)
                    if not isinstance(G, int) or G > 0:
                        act.wait_ge(ln.s_lo, G * KT - KT + n + 1)
                    ln.act_affine_tile(act, n, ps)
                    act.wait_ge(ln.s_affine, G * KT + n + 1)
                    if not isinstance(G, int) or G > 0:
                        act.wait_ge(q_sum, G * QT)
                    ln.act_hi_tile(act, n)
                elif kind in "qk":
                    act.wait_ge(q_sum if kind == "q" else k_sum, G * (QT if kind == "q" else KTILES) + n + 1)
                    at = tiles.index(f"{kind}{n}")
                    if not isinstance(G, int) or G * len(tiles) + at >= 2:
                        act.wait_ge(stacked, G * len(tiles) + at - 1)
                    col = C_BIAS + n + (0 if kind == "q" else QT)
                    act.activation(full[:, at % 2], ps[:, :], ACT.Identity, bias=cols[:, col:col + 1])\
                        .then_inc(biased, 1)
                elif kind == "v":
                    act.wait_ge(v_sum, G * GROUP + n + 1)
                    if not isinstance(G, int) or G * GROUP + n >= 2:
                        act.wait_ge(v_set, G * GROUP + n - 1)
                    act.activation(vt[:, n % 2], ps[:, 0:VC], ACT.Copy).then_inc(v_read, 1)
                elif kind == "a":
                    act.wait_ge(a_turned, G * KT + n + 1)
                    act.activation(attT[:, 0, n], ps[:, :], ACT.Copy).then_inc(a_hi, 1)

            def step(it, s):
                n, i = divmod(s - READ, 4)
                if i == 0 and n >= 0 and real(it, n // NQD):
                    act.wait_ge(pved, it * NQD + n + 1)
                    if n >= 2:
                        act.wait_ge(o_turned, it * NQD + n - 1)
                    act.activation(o_sb[:, n % 2], psO[:, :], ACT.Copy).then_inc(o_out, 1)
                for args in uses_at(it, s - 1):
                    use(it, *args)
                c = s - TURN
                if c >= 0 and real(it, c // H):
                    act.wait_ge(turned, it * H + c + 1)
                    if c >= SLOTS:
                        act.wait_ge(pved, it * NQD + (c - SLOTS) // 4 + 1)
                    act.activation(probs[:, c % SLOTS], psT[c % 2][:, :], ACT.Exp).then_inc(expd, 1)

            for k in range(KT):
                act.wait_ge(w_in[k], 16)
                act.activation(w[:, 0, k], w_raw[:, k], ACT.Copy).then_inc(w_hi, 1)
            act.wait_ge(rows_in, 32)
            pipeline(act, step)

        @block.vector
        def _(dve):
            def x(G, b):
                return X[:, bass.ds(G * GROUP + b, 1), :].rearrange("p a d -> p (a d)")

            def use(it, kind, n, k, bank):
                G, ps = it + k, psW[bank]
                if kind == "t":
                    dve.wait_ge(ln.s_hi, G * KT + n + 1)
                    ln.dve_lo_tile(dve, n)
                elif kind in "qk":
                    at = tiles.index(f"{kind}{n}")
                    dve.wait_ge(biased, tile_count(it, k, f"{kind}{n}"))
                    dve.tensor_copy(top[:, at % 2], full[:, at % 2]).then_inc(topped, 1)
                    dve.wait_ge(topped, tile_count(it, k, f"{kind}{n}"))
                    j, u = (0, n) if kind == "q" else (1, QT + n)
                    dve.scalar_tensor_tensor(qk[:, u], top[:, at % 2].bitcast(F32), cols[:, C_MASK + j:C_MASK + j + 1],
                                             full[:, at % 2], ALU.mult, ALU.add).then_inc(stacked, 1)
                elif kind == "v":
                    dve.wait_ge(v_read, G * GROUP + n + 1)
                    if not isinstance(G, int) or G > 0:
                        dve.wait_ge(pved, G * NQD)
                    dve.tensor_tensor(v[:, n, :, 0:DH], vt[:, n % 2].rearrange("p (h d) -> p h d", h=KV),
                                      rows[:, R_V:R_V + VC].rearrange("p (h d) -> p h d", h=KV), ALU.add)\
                        .then_inc(v_set, 1)
                elif kind == "a":
                    dve.wait_ge(a_hi, G * KT + n + 1)
                    dve.tensor_tensor(attT[:, 1, n], ps[:, :], attT[:, 0, n].bitcast(F32), ALU.subtract)\
                        .then_inc(a_lo, 1)
                else:
                    dve.wait_ge(outp, G * 2 + n + 1)
                    dve.wait_ge(x_biased, G + 1)
                    o = ps[:, :].rearrange("p (b d) -> p b d", b=2)
                    dst = X[:, bass.ds(G * GROUP + 2 * n, 2), :] if first else xb[:, 2 * n:2 * n + 2]
                    dve.tensor_tensor(dst, o, xb[:, 2 * n:2 * n + 2], ALU.add).then_inc(added, 1)

            def norm(it, n):
                dve.wait_ge(o_turned, it * NQD + n + 1)
                o = psN[:, :].rearrange("p (b i c) -> p b i c", b=GROUP, i=4)
                q = n % NQD
                dve.reciprocal(rden[:, q], o[:, :, :, DH]).then_inc(r_done, 1)
                dve.wait_ge(r_done, it * NQD + n + 1)
                if q == 0 and n > 0:
                    dve.wait_ge(a_turned, (it + n // NQD) * KT)
                if first:
                    dst = att[:, :, q * 64:(q + 1) * 64].rearrange("p b (i d) -> p b i d", i=4)
                else:
                    dst = att[:, :, (q // 4) * P:(q // 4 + 1) * P]\
                        .rearrange("p b (i m d) -> p b i m d", i=4, m=4)[:, :, :, q % 4, :]
                dve.tensor_tensor(dst, o[:, :, :, 0:DH],
                                  rden[:, q].rearrange("p b (i a) -> p b i a", a=1)
                                  .to_broadcast([P, GROUP, 4, DH]), ALU.mult).then_inc(normed, 1)

            def step(it, s):
                k, r = divmod(s, H)
                for args in uses_at(it, s - 1):
                    use(it, *args)
                G = it + k
                if r == 0 and real(it, k) and s >= 0:
                    dve.wait_ge(mask_in, G * 16 + 16)
                    if first:
                        dve.tensor_scalar(mask[:, :], mask_raw[:, :].bitcast(U8), -1.0, F32_LOWEST, ALU.add, ALU.mult)\
                            .then_inc(mask_set, 1)
                    else:
                        dve.tensor_copy(mask[:, :], mask_raw[:, :]).then_inc(mask_set, 1)
                    dve.wait_ge(mask_set, G + 1)
                if first and r == T0 and real(it, k + 1):
                    ln.dve_statistics(dve, G + 1, lambda b: x(G + 1, b))
                if r == (T0 + 1 if first else T0 + 4) and real(it, k + 1):
                    if not isinstance(G, int) or G >= 0:
                        dve.wait_ge(ln.s_turned, (G + 1) * KT)
                    ln.dve_normalise(dve, G + 1, lambda b: x(G + 1, b))
                if 0 <= s and real(it, k):
                    dve.wait_ge(scored, it * H + s + 1)
                    if s >= 4:
                        dve.wait_ge(turned, it * H + s - 3)
                    dve.scalar_tensor_tensor(s_sb[:, s % 4], psS[s % 2][:, :], SCALE, mask[:, :], ALU.mult, ALU.add)\
                        .then_inc(masked, 1)
                    dve.wait_ge(masked, it * H + s + 1)
                    dve.tensor_reduce(peak[:, r], s_sb[:, s % 4].rearrange("p (b k) -> p b k", b=GROUP), AX.X,
                                      ALU.max).then_inc(peaked, 1)
                n, i = divmod(s - NORM, 4)
                if i == 0 and n >= 0 and real(it, n // NQD):
                    norm(it, n)
                if not first and r == NORM + 1 and real(it, k - 1):
                    dve.wait_ge(added, CREDIT + G * 2)
                    for b in range(GROUP):
                        dve.bn_stats(ln.stats[:, b], xb[:, b]).then_inc(y_stats, 1)
                    for b in range(GROUP):
                        dve.wait_ge(y_stats, (G - 1) * GROUP + b + 1)
                        dve.sem_inc(ln.s_gate, 1)
                        dve.bn_aggr(ln.mean_var[:, b], ln.stats[:, b]).then_inc(y_mean, 1)
                if not first and r == NORM + 3 and real(it, k - 1):
                    dve.wait_ge(y_rstd, G)
                    for b in range(GROUP):
                        dve.tensor_scalar(yn[:, b], xb[:, b], ln.mean_var[:, b, 0:1], ln.rstd[:, b:b + 1],
                                          ALU.subtract, ALU.mult).then_inc(y_normed, 1)

            dve.wait_ge(w_hi, 1)
            dve.tensor_tensor(w[:, 1, 0], w_raw[:, 0], w[:, 0, 0].bitcast(F32), ALU.subtract).then_inc(w_lo, 1)
            dve.wait_ge(v_ones, 2)
            dve.memset(peak[:, :, :], 0.0).then_inc(added, CREDIT)
            dve.wait_ge(rows_in, 32)
            pipeline(dve, step)

        @block.tensor
        def _(pe):
            def bank_free(it, s, kind, n):
                pos = cycle.index(f"{kind}{n}") + s // H * len(cycle)
                for pos in range(pos - 2, pos - 2 - len(cycle), -2):
                    name = cycle[pos % len(cycle)]
                    k = (pos // len(cycle) * H + when[name] % H - when[name]) // H
                    if not real(it, k):
                        continue
                    G, n = it + k, int(name[1])
                    if name[0] in "qk":
                        pe.wait_ge(biased, tile_count(it, k, name))
                    elif name[0] == "v":
                        pe.wait_ge(v_read, G * GROUP + n + 1)
                    elif name[0] == "t":
                        pe.wait_ge(ln.s_affine, G * KT + n + 1)
                    elif name[0] == "a":
                        pe.wait_ge(a_lo, G * KT + n + 1)
                    else:
                        pe.wait_ge(added, CREDIT + G * 2 + n + 1)
                    if k >= 0:
                        return

            def use(it, s, kind, n, k, bank):
                G, ps = it + k, psW[bank]
                bank_free(it, s, kind, n)
                if kind == "t":
                    ln.pe_turn_tile(pe, G, n, ps, ident)
                elif kind in "qk":
                    if n == 0:
                        if kind == "q":
                            ln.pe_ready(pe, G)
                        else:
                            pe.wait_ge(loaded, G * 16 + 16)
                    at, signal = (NQ + n * P, q_sum) if kind == "q" else (NK + n * P, k_sum)
                    for c in range(KT):
                        ins = mm3(pe, ps[:, :], lambda e: w[:, e, c, at:at + P],
                                  lambda e: ln.hT[:, e, c] if kind == "q" else cT[:, :, e, c], c == 0, c == KT - 1)
                    ins.then_inc(signal, 1)
                elif kind == "v":
                    for c in range(KT):
                        ins = mm3(pe, ps[:, 0:VC], lambda e: cT[:, n, e, c],
                                  lambda e: w[:, e, c, NV:NV + VC], c == 0, c == KT - 1)
                    ins.then_inc(v_sum, 1)
                elif kind == "a":
                    if n == 0:
                        pe.wait_ge(normed, G * NQD + NQD)
                    for b in range(GROUP):
                        ins = pe.transpose(ps[:, b * P:(b + 1) * P], att[:, b, n * P:(n + 1) * P], ident[:, :])
                    ins.then_inc(a_turned, 1)
                else:
                    if n == 0:
                        pe.wait_ge(a_lo, G * KT + KT)
                    for b in (2 * n, 2 * n + 1):
                        for c in range(KT):
                            ins = mm3(pe, ps[:, (b % 2) * D:(b % 2 + 1) * D],
                                      lambda e: attT[:, e, c, b * P:(b + 1) * P], lambda e: w[:, e, c, NO:NO + D],
                                      c == 0, c == KT - 1)
                    ins.then_inc(outp, 1)

            def step(it, s):
                k, c = divmod(s, H)
                if s >= 0 and real(it, k):
                    qt, row, kt, _ = place(c)
                    if s >= 2:
                        pe.wait_ge(masked, it * H + s - 1)
                    pe.wait_ge(stacked, max((tile_count(0, 0, f"q{qt}"), tile_count(0, 0, f"k{kt}")))
                               + (it + k) * len(tiles))
                    for b in range(GROUP):
                        at = slice(b * P, (b + 1) * P)
                        ins = pe.matmul(psS[s % 2][:, at], qk[row:row + SLOT, qt, at], qk[row:row + SLOT, QT + kt, at],
                                        start=True, stop=True)
                    ins.then_inc(scored, 1)
                c = s - TURN
                if c >= 0 and real(it, c // H):
                    pe.wait_ge(eased, it * H + c + 1)
                    if c >= 2:
                        pe.wait_ge(expd, it * H + c - 1)
                    for b in range(GROUP):
                        at = slice(b * P, (b + 1) * P)
                        ins = pe.transpose(psT[c % 2][:, at], s_sb[:, c % 4, at], ident[:, :])
                    ins.then_inc(turned, 1)
                n, i = divmod(s - VALUES, 4)
                if i in (0, SPREAD) and n >= 0 and real(it, n // NQD):
                    if i == 0:
                        pe.wait_ge(expd, it * H + 4 * (n + 1))
                        if n >= 1:
                            pe.wait_ge(o_out, it * NQD + n)
                        if n % NQD == 0:
                            pe.wait_ge(v_set, (it + n // NQD) * GROUP + GROUP)
                    half = GROUP // 2 if SPREAD else GROUP
                    for b in range(half if i else 0, GROUP if i else half):
                        at = slice(b * P, (b + 1) * P)
                        for m in range(4):
                            c = 4 * n + m
                            ins = pe.matmul(psO[32 * m:32 * m + 32, at], v[:, b, place(c % H)[3], :],
                                            probs[:, c % SLOTS, at], start=True, stop=True)
                    if i == SPREAD:
                        ins.then_inc(pved, 1)
                n, i = divmod(s - TURN_OUT, 4)
                if i == 0 and n >= 0 and real(it, n // NQD):
                    pe.wait_ge(o_out, it * NQD + n + 1)
                    if n >= 1:
                        pe.wait_ge(normed, it * NQD + n)
                    for b in range(GROUP):
                        at = slice(b * P, (b + 1) * P)
                        ins = pe.transpose(psN[:, at], o_sb[:, n % 2, at], ident[:, :])
                    ins.then_inc(o_turned, 1)
                for args in uses_at(it, s):
                    use(it, s, *args)

            pe.wait_ge(w_lo, 1)
            pe.wait_ge(w_lo_pool, 1)
            pipeline(pe, step)


def mlp_phase(nc, name, gelu, X, cols_dram, rows_dram, ident, stage, ahead):
    F = 4 * D
    FT = F // P
    NF, NP_ = 0, KT * F
    NW = NP_ + FT * D
    C_B, C_G, C_O = 0, FT, FT + KT
    NC = C_O + KT
    with ExitStack() as ctx:
        t = Buffers(nc, ctx, name)
        cols = t.sb("cols", [P, NC])
        rows = t.sb("rows", [P, D])
        w = t.sb("w", [P, 2, NW], F32R)
        w_raw = stage.raw[:, 0:NW]
        fc_in, proj_in = stage.arrived[name]
        ln = TokenNorm(t, 1e-5, cols[:, C_G:C_G + KT], cols[:, C_O:C_O + KT])
        act_out = t.sb("act_out", [P, 2, TOK])
        y = t.sb("y", [P, 2, FT, TOK], F32R)
        xb = t.sb("xb", [P, GROUP, D])
        psW = [t.bank(f"psW{i}") for i in range(2)]
        psH = [t.bank(f"psH{i}") for i in range(2)]
        psO = [t.bank(f"psO{i}") for i in range(2)]
        (cols_in, w_hi, w_lo, w_lo_pool, fc, gelued, y_hi, y_lo, outp, x_biased, done) = [
            t.sem(n) for n in "cols_in w_hi w_lo w_lo_pool fc gelued y_hi y_lo outp x_biased done".split()]
        block = ctx.enter_context(nc.Block())

        def each_group(eng, group):
            with eng.Fori(0, NG - 1) as g:
                group(g, False)
            group(NG - 1, True)

        @block.sync
        def _(sp):
            sp.dma_start(cols[:, :], cols_dram).then_inc(cols_in, 16)
            sp.dma_start(rows[:, :], rows_dram.to_broadcast([P, D])).then_inc(cols_in, 16)
            if ahead:
                for sem in (w_lo, w_lo_pool):
                    sp.wait_ge(sem, 1)
                stage.load(sp, ahead)

        @block.gpsimd
        def _(pool):
            ln.pool_setup(pool)
            ln.pool_rstd(pool, 0)
            pool.wait_ge(w_hi, 2)
            pool.tensor_tensor(w[:, 1, NP_:NW], w_raw[:, NP_:NW], w[:, 0, NP_:NW].bitcast(F32), ALU.subtract)\
                .then_inc(w_lo_pool, 1)
            pool.wait_ge(cols_in, 32)

            def group(g, last):
                if not last:
                    ln.pool_rstd(pool, g + 1)
                pool.wait_ge(done, g + 1)
                pool.sem_inc(ln.s_gate, 1)
                pool.tensor_tensor(xb[:, :, :], X[:, bass.ds(g * GROUP, GROUP), :],
                                   rows[:, :].rearrange("p (a d) -> p a d", a=1).to_broadcast([P, GROUP, D]),
                                   ALU.add).then_inc(x_biased, 1)

            each_group(pool, group)

        @block.scalar
        def _(act):
            act.wait_ge(fc_in, 16)
            act.activation(w[:, 0, 0:NP_], w_raw[:, 0:NP_], ACT.Copy).then_inc(w_hi, 1)
            act.wait_ge(cols_in, 32)
            ln.act_affine(act, 0, psW)
            act.wait_ge(proj_in, 16)
            act.activation(w[:, 0, NP_:NW], w_raw[:, NP_:NW], ACT.Copy).then_inc(w_hi, 1)

            def group(g, last):
                for n in range(FT):
                    act.wait_ge(fc, g * FT + n + 1)
                    if n >= 2:
                        act.wait_ge(y_lo, g * FT + n - 1)
                    act.activation(act_out[:, n % 2], psH[n % 2][:, :], gelu, bias=cols[:, C_B + n:C_B + n + 1])\
                        .then_inc(gelued, 1)
                if not last:
                    ln.act_affine(act, g + 1, psW)

            each_group(act, group)

        @block.vector
        def _(dve):
            def x(g, b):
                return X[:, bass.ds(g * GROUP + b, 1), :].rearrange("p a d -> p (a d)")

            ln.dve_statistics(dve, 0, lambda b: x(0, b))
            ln.dve_normalise(dve, 0, lambda b: x(0, b))
            dve.wait_ge(w_hi, 1)
            dve.tensor_tensor(w[:, 1, 0:NP_], w_raw[:, 0:NP_], w[:, 0, 0:NP_].bitcast(F32), ALU.subtract)\
                .then_inc(w_lo, 1)
            ln.dve_lo(dve, 0)
            dve.sem_inc(done, 1)

            def group(g, last):
                if not last:
                    ln.dve_statistics(dve, g + 1, lambda b: x(g + 1, b))
                for n in range(FT):
                    dve.wait_ge(gelued, g * FT + n + 1)
                    dve.tensor_copy(y[:, 0, n], act_out[:, n % 2]).then_inc(y_hi, 1)
                    dve.wait_ge(y_hi, g * FT + n + 1)
                    dve.tensor_tensor(y[:, 1, n], act_out[:, n % 2], y[:, 0, n].bitcast(F32), ALU.subtract)\
                        .then_inc(y_lo, 1)
                    if n == 3 and not last:
                        ln.dve_normalise(dve, g + 1, lambda b: x(g + 1, b))
                if not last:
                    ln.dve_lo(dve, g + 1)
                dve.wait_ge(x_biased, g + 1)
                for m in range(2):
                    dve.wait_ge(outp, g * 2 + m + 1)
                    ins = dve.tensor_tensor(X[:, bass.ds(g * GROUP + 2 * m, 2), :],
                                            psO[m][:, :].rearrange("p (b d) -> p b d", b=2), xb[:, 2 * m:2 * m + 2],
                                            ALU.add)
                    if m == 1:
                        ins.then_inc(done, 1)

            each_group(dve, group)

        @block.tensor
        def _(pe):
            ln.pe_turn(pe, 0, psW, ident)
            pe.wait_ge(w_lo, 1)

            def group(g, last):
                ln.pe_ready(pe, g)
                for n in range(FT):
                    if n >= 2:
                        pe.wait_ge(gelued, g * FT + n - 1)
                    for k in range(KT):
                        at = NF + k * F + n * P
                        ins = mm3(pe, psH[n % 2][:, :], lambda s: w[:, s, at:at + P], lambda s: ln.hT[:, s, k],
                                  k == 0, k == KT - 1)
                    ins.then_inc(fc, 1)
                if not last:
                    ln.pe_turn(pe, g + 1, psW, ident)
                pe.wait_ge(w_lo_pool, 1)
                pe.wait_ge(done, g + 1)
                pe.wait_ge(y_lo, g * FT + FT)
                for b in range(GROUP):
                    for n in range(FT):
                        at = NP_ + n * D
                        ins = mm3(pe, psO[b // 2][:, (b % 2) * D:(b % 2 + 1) * D],
                                  lambda s: y[:, s, n, b * P:(b + 1) * P], lambda s: w[:, s, at:at + D],
                                  n == 0, n == FT - 1)
                    if b % 2:
                        ins.then_inc(outp, 1)

            each_group(pe, group)


def wide_phase(nc, X, ctxT_dram, d, ident, stage, ahead):
    H, QH = 16, 4
    NQD = H // QH
    SCALE = float(P) ** -0.5
    PART = KT * QH * P
    C_BQ, C_BK, C_G, C_B, C_EK, C_EV, C_BV = 0, 16, 32, 34, 36, 52, 68
    NC = 84
    AHEAD = 7
    CREDIT = 8
    SLOTS = 4
    LEAD = 3
    T0 = 8

    cycle = []
    for n in range(H):
        if n == 2:
            cycle.append(("n", 0, -1))
        k, j = divmod(n - 7, H)
        if j % 4 == 0:
            cycle += [("o", j // 2, k), ("o", j // 2 + 1, k)]
        k, c = divmod(n - 3, H)
        cycle.append(("t", c, k))
        k, h = divmod(n + LEAD, H)
        cycle += [("q", h, k), ("k", h, k), ("v", h, k)]
        if n == 12:
            cycle += [("l", 0, 1), ("l", 1, 1)]
        if n == 15:
            cycle.append(("x", 0, 1))
    order = {(kind, n): pos for pos, (kind, n, _) in enumerate(cycle)}

    def real(it, k):
        return not isinstance(it, int) or 0 <= it + k < NG

    with ExitStack() as ctx:
        t = Buffers(nc, ctx, "l2")
        cols = t.sb("cols", [P, NC])
        bo = t.sb("bo", [1, D])
        raw = stage.raw[:, :].rearrange("p (a n) -> p a n", a=2)
        raw_o = t.sb("raw_o", [P, 2, PART])
        w = t.sb("w", [P, 2, 2, 4 * PART], F32R)
        qk = t.sb("qk", [P, 2 * SLOTS, TOK])
        v = t.sb("v", [P, 2, GROUP, QH, P + 1])
        cT = t.sb("cT", [P, GROUP, 2, KT, P], F32R)
        s_sb = t.sb("s_sb", [P, 2, TOK])
        probs = t.sb("probs", [P, 2, TOK])
        att = t.sb("att", [P, 2, TOK])
        attT = t.sb("attT", [P, 2, QH, TOK], F32R)
        extra = t.sb("extra", [P, GROUP, H])
        top = t.sb("top", [P, H, GROUP])
        peak = t.sb("peak", [P, H, GROUP])
        gap = t.sb("gap", [P, H, GROUP])
        extra_p = t.sb("extra_p", [P, H, GROUP])
        den = t.sb("den", [P, H, GROUP])
        rden = t.sb("rden", [P, H, GROUP])
        norm_p = t.sb("norm_p", [P, GROUP, H + 1])
        norm_pT = t.sb("norm_pT", [H + 1, TOK])
        u = t.sb("u", [P, KT, H])
        u_parts = t.sb("u_parts", [P, 2, KT, H], F32R)
        ones = t.sb("ones", [P, P])
        c_prod = t.sb("c_prod", [P, H])
        c_row = t.sb("c_row", [P, H])
        dv = t.sb("dv", [P, H * (H + 1)])
        pick = t.sb("pick", [1, H + 1])
        credit = t.sb("credit", [P, 1])
        big_g = t.sb("big_g", [H + 1, D])
        ln = TokenNorm(t, 1e-5, cols[:, C_G:C_G + KT], cols[:, C_B:C_B + KT])
        psS = [t.bank(f"psS{n}") for n in range(2)]
        psT = [t.bank(f"psT{n}") for n in range(2)]
        psV = ctx.enter_context(nc.psum_tensor("l2_psV", [P, GROUP, 256], F32))
        psW = [t.bank(f"psW{n}") for n in range(2)]
        whole_q = v[:, :, :, :, :].rearrange("p a b h n -> p (a b h n)")[:, 0:NQD * PART]
        whole_o = qk[:, :, :].rearrange("p h n -> p (h n)")
        ek_rows = [s_sb[:, 0], s_sb[:, 1], probs[:, 0], probs[:, 1]]
        (consts, params, ek_in, wq_in, wo_in, u_prod, u_sum, u_hi, u_set, c_mul, c_sum, c_set, dv_set, g_sum,
         g_set, w_hi, w_lo, ctx_in, extra_sum, extra_set, q_sum, q_set, k_sum, k_set, v_sum, v_set, scored,
         topped, peaked, eased, gapped, extra_exp, turned, expd, pved, den_set, r_done, np_set, normed, a_turned,
         a_hi, a_lo, outp, added, np_turned, npT_set, done, v_ones, gate) = [
            t.sem(n) for n in ("consts params ek_in wq_in wo_in u_prod u_sum u_hi u_set c_mul c_sum c_set dv_set "
                               "g_sum g_set w_hi w_lo ctx_in extra_sum extra_set q_sum q_set k_sum k_set "
                               "v_sum v_set scored topped peaked eased gapped extra_exp turned expd pved den_set "
                               "r_done np_set normed a_turned a_hi a_lo outp added np_turned npT_set done v_ones gate").split()]
        qkv_in = stage.arrived["l2"]
        o_in = [t.sem(f"o_in{n}") for n in range(2)]
        block = ctx.enter_context(nc.Block())
        qkv_dram, o_dram = d["l2_qkv"], d["l2_o"]

        psum = {(kind, n): psW[pos % 2] for (kind, n), pos in order.items()}

        def pipeline(eng, step):
            for s in range(-H, T0):
                step(0, s)
            with eng.Fori(0, NG - 1) as it:
                for s in range(T0, T0 + H):
                    step(it, s)
            for s in range(T0, 2 * H):
                step(NG - 1, s)

        def flat(ap):
            return ap.rearrange("a p n -> p (a n)")

        @block.sync
        def _(sp):
            def load_qkv(index, Q, stream):
                sp.wait_ge(w_lo, stream * 4 + 3)
                sp.dma_start(raw[:, Q % 2], flat(qkv_dram[index])).then_inc(qkv_in[Q % 2], 16)

            def load_o(index, Q, stream):
                sp.wait_ge(w_lo, stream * 4 + 7)
                sp.dma_start(raw_o[:, Q % 2], flat(o_dram[index])).then_inc(o_in[Q % 2], 16)

            for a in range(2):
                for Q in range(NQD):
                    if a > 0 or Q >= 2:
                        load_qkv(slice(a * NQD + Q, a * NQD + Q + 1), Q, a * NG * NQD + Q)
                    load_o(slice(a * NQD + Q, a * NQD + Q + 1), Q, a * NG * NQD + Q)
                with sp.Fori(0, NG - 1) as it:
                    for Q in range(NQD):
                        stream = (a * NG + 1) * NQD + it * NQD + Q
                        load_qkv(slice(a * NQD + Q, a * NQD + Q + 1), Q, stream)
                        load_o(slice(a * NQD + Q, a * NQD + Q + 1), Q, stream)
            for Q in range(2):
                load_qkv(slice(Q, Q + 1), Q, 2 * NG * NQD + Q)
                load_o(slice(Q, Q + 1), Q, 2 * NG * NQD + Q)
            for n in range(2):
                sp.wait_ge(o_in[n], 16 * (NG * NQD + 1))
            if ahead:
                sp.wait_ge(w_lo, CREDIT + AHEAD + 2 * NG * H)
                stage.load(sp, ahead)

        @block.gpsimd
        def _(pool):
            pool.memset(dv[:, :], 0.0).then_inc(consts, 1)
            pool.memset(pick[:, :], 0.0).then_inc(consts, 1)
            pool.memset(ones[:, :], 1.0).then_inc(consts, 1)
            pool.memset(norm_p[:, :, :], 1.0).then_inc(consts, 1)
            pool.wait_ge(consts, 4)
            pool.memset(pick[:, H:H + 1], 1.0).then_inc(consts, 1)
            ln.pool_setup(pool)
            pool.memset(credit[:, :], 0.0).then_inc(w_lo, CREDIT)

            def split(parity, part):
                src = raw[:, parity, part * PART:(part + 1) * PART] if part < 3 else raw_o[:, parity]
                at = slice(part * PART, (part + 1) * PART)
                pool.tensor_tensor(w[:, parity, 1, at], src, w[:, parity, 0, at].bitcast(F32), ALU.subtract)\
                    .then_inc(w_lo, 1)

            for n, (parity, part) in enumerate([(0, 0), (0, 1), (0, 2), (1, 0), (1, 1), (1, 2), (0, 3)]):
                pool.wait_ge(w_hi, n + 1)
                split(parity, part)
            with pool.Fori(0, 2) as a:
                def step(it, s):
                    r, (k, n) = a * NG + it, divmod(s, H)
                    if s >= 0 and real(it, k):
                        Q, i = divmod(n, 4)
                        pool.wait_ge(w_hi, r * H + AHEAD + s + 1)
                        split(Q % 2 if i < 3 else (Q + 1) % 2, i)
                    if n == 10 and real(it, k + 1):
                        ln.pool_rstd(pool, r + k + 1)
                        if s < 0:
                            pool.wait_ge(u_sum, a * NQD + NQD)
                            pool.sem_inc(gate, 1)
                            pool.memset(v[:, :, :, :, P:P + 1], 1.0).then_inc(v_ones, 1)

                pipeline(pool, step)

        @block.scalar
        def _(act):
            def split(parity, part):
                src = raw[:, parity, part * PART:(part + 1) * PART] if part < 3 else raw_o[:, parity]
                act.activation(w[:, parity, 0, part * PART:(part + 1) * PART], src, ACT.Copy).then_inc(w_hi, 1)

            for parity in range(2):
                act.wait_ge(qkv_in[parity], 16)
                for part in range(3):
                    split(parity, part)
            act.wait_ge(o_in[0], 16)
            split(0, 3)
            with act.Fori(0, 2) as a:
                act.wait_ge(done, a + 1)
                act.wait_ge(consts, 5)
                act.dma_start(cols[:, :], flat(d["l2_cols"][bass.ds(a, 1)])).then_inc(params, 16)
                act.dma_start(bo[:, :], d["l2_bo"][bass.ds(a, 1)]).then_inc(params, 16)
                act.dma_start(whole_o.rearrange("p (q n) -> p q n", q=NQD),
                              o_dram[bass.ds(a * NQD, NQD)].rearrange("q p n -> p q n")).then_inc(wo_in, 16)
                for half, place in enumerate((s_sb, probs)):
                    act.dma_start(place[:, :, :].rearrange("p a n -> p (a n)"),
                                  d["l2_ek"][bass.ds(a, 1), half * 2 * TOK:(half + 1) * 2 * TOK]
                                  .to_broadcast([P, 2 * TOK])).then_inc(ek_in, 16)
                act.dma_start(whole_q.rearrange("p (q n) -> p q n", q=NQD),
                              qkv_dram[bass.ds(a * NQD, NQD), :, 0:PART].rearrange("q p n -> p q n"))\
                    .then_inc(wq_in, 16)
                act.wait_ge(params, a * 32 + 32)
                act.wait_ge(g_sum, a + 1)
                act.activation(big_g[:, :], psW[1][0:H + 1, 0:D], ACT.Copy).then_inc(g_set, 1)

                def step(it, s):
                    r, (k, n) = a * NG + it, divmod(s, H)
                    if n == 2 and real(it, k - 1):
                        act.wait_ge(np_turned, r + k)
                        act.activation(norm_pT[:, :], psum["n", 0][0:H + 1, :], ACT.Copy).then_inc(npT_set, 1)
                    if n == 13 and real(it, k + 1):
                        ln.act_affine(act, r + k + 1, [psum["l", c] for c in range(KT)])
                    c = s - 3
                    if c >= 0 and real(it, c // H):
                        act.wait_ge(a_turned, r * H + c + 1)
                        act.activation(attT[:, 0, c % 4], psum["t", c % H][:, :], ACT.Copy).then_inc(a_hi, 1)
                    h = s + LEAD
                    if h >= 0 and real(it, h // H):
                        m = h % H
                        act.wait_ge(q_sum, r * H + h + 1)
                        act.activation(qk[:, m % SLOTS], psum["q", m][:, :], ACT.Identity,
                                       bias=cols[:, C_BQ + m:C_BQ + m + 1]).then_inc(q_set, 1)
                        act.wait_ge(k_sum, r * H + h + 1)
                        act.activation(qk[:, SLOTS + m % SLOTS], psum["k", m][:, :], ACT.Identity,
                                       bias=cols[:, C_BK + m:C_BK + m + 1]).then_inc(k_set, 1)
                    c = s - 1
                    if c >= 0 and real(it, c // H):
                        act.wait_ge(gapped, r * H + c + 1)
                        act.activation(extra_p[:, c % H], gap[:, c % H], ACT.Exp, scale=SCALE).then_inc(extra_exp, 1)
                        act.wait_ge(turned, r * H + c + 1)
                        if c >= 2:
                            act.wait_ge(pved, r * H + c - 1)
                        act.activation(probs[:, c % 2], psT[c % 2][:, :], ACT.Exp, scale=SCALE).then_inc(expd, 1)
                    if h >= 0 and real(it, h // H):
                        Q, i = divmod(h, 4)
                        if h == 0:
                            act.wait_ge(v_ones, a + 1)
                        act.wait_ge(v_sum, r * H + h + 1)
                        if Q >= 2:
                            act.wait_ge(pved, r * H + 4 * (Q - 1))
                        act.activation(v[:, Q % 2, i, :, 0:P], psum["v", h % H][:, :]
                                       .rearrange("p (h n) -> p h n", h=QH), ACT.Copy).then_inc(v_set, 1)
                    if n == 12 and real(it, k + 1):
                        load_context(act, cT, ctxT_dram, it + (k + 1)).then_inc(ctx_in, 16)
                    if s >= 0 and real(it, k):
                        Q, i = divmod(n, 4)
                        if i < 3:
                            act.wait_ge(qkv_in[Q % 2], (r + k) * (NQD // 2 * 16) + 16 * (Q // 2 + 2))
                            split(Q % 2, i)
                        else:
                            act.wait_ge(o_in[(Q + 1) % 2], (r + k) * (NQD // 2 * 16) + 16 * ((Q + 1) // 2 + 1))
                            if s // 4 >= 1:
                                act.wait_ge(outp, r * 2 * NQD + 2 * (s // 4))
                            split((Q + 1) % 2, 3)

                pipeline(act, step)

        @block.vector
        def _(dve):
            dve.wait_ge(consts, 5)
            dve.memset(s_sb[:, 0, 0:1], 0.0).then_inc(done, 1)
            with dve.Fori(0, 2) as a:
                dve.wait_ge(params, a * 32 + 32)
                dve.tensor_tensor(c_prod[:, :], cols[:, C_BQ:C_BQ + H], cols[:, C_EK:C_EK + H], ALU.mult)\
                    .then_inc(c_mul, 1)
                dve.tensor_tensor(dv[:, 0:H * (H + 1):H + 2], cols[:, C_EV:C_EV + H], cols[:, C_BV:C_BV + H],
                                  ALU.subtract).then_inc(dv_set, 1)
                dve.tensor_copy(dv[:, H:H * (H + 1):H + 1], cols[:, C_BV:C_BV + H]).then_inc(dv_set, 1)
                dve.wait_ge(c_sum, a + 1)
                dve.tensor_copy(c_row[:, :], psW[0][:, 0:H]).then_inc(c_set, 1)

                def extra_key_weights():
                    dve.wait_ge(wq_in, a * 16 + 16)
                    dve.wait_ge(ek_in, a * 32 + 32)
                    for Q in range(NQD):
                        part = whole_q[:, Q * PART:(Q + 1) * PART].rearrange("p (c n) -> p c n", c=KT)
                        dve.tensor_tensor(part, part, ek_rows[Q].rearrange("p (a n) -> p a n", a=1)
                                          .to_broadcast([P, KT, QH * P]), ALU.mult).then_inc(u_prod, 1)
                    for Q in range(NQD):
                        dve.wait_ge(u_prod, a * NQD + Q + 1)
                        dve.tensor_reduce(u[:, :, Q * QH:(Q + 1) * QH], whole_q[:, Q * PART:(Q + 1) * PART]
                                          .rearrange("p (c h n) -> p c h n", c=KT, h=QH), AX.X, ALU.add)\
                            .then_inc(u_sum, 1)
                    dve.wait_ge(u_sum, a * NQD + NQD)
                    dve.tensor_copy(u_parts[:, 0], u[:, :, :]).then_inc(u_hi, 1)
                    dve.wait_ge(u_hi, a + 1)
                    dve.tensor_tensor(u_parts[:, 1], u[:, :, :], u_parts[:, 0].bitcast(F32), ALU.subtract)\
                        .then_inc(u_set, 1)

                def x(g, b):
                    return X[:, bass.ds(g * GROUP + b, 1), :].rearrange("p a d -> p (a d)")

                def step(it, s):
                    r, (k, n) = a * NG + it, divmod(s, H)
                    if n == 13 and real(it, k + 1):
                        ln.dve_lo(dve, r + k + 1)
                        if s < 0:
                            extra_key_weights()
                    j, i = divmod(s - 7, 4)
                    if i == 0 and j >= 0 and real(it, j // NQD):
                        for m in range(2):
                            xm = X[:, bass.ds((it + j // NQD) * GROUP + 2 * m, 2), :]
                            if j % NQD:
                                dve.wait_ge(added, r * 2 * NQD + 2 * j)
                            dve.wait_ge(outp, r * 2 * NQD + 2 * j + m + 1)
                            dve.tensor_tensor(xm, psum["o", 2 * (j % NQD) + m][:, :]
                                              .rearrange("p (b d) -> p b d", b=2), xm, ALU.add).then_inc(added, 1)
                    c = s - 2
                    if c >= 0 and real(it, c // H):
                        ch = c % H
                        dve.wait_ge(pved, r * H + c + 1)
                        dve.wait_ge(extra_exp, r * H + c + 1)
                        dve.tensor_tensor(den[:, ch], psV[:, :, P], extra_p[:, ch], ALU.add).then_inc(den_set, 1)
                        dve.wait_ge(den_set, r * H + c + 1)
                        dve.reciprocal(rden[:, ch], den[:, ch]).then_inc(r_done, 1)
                        dve.wait_ge(r_done, r * H + c + 1)
                        if c >= 2:
                            dve.wait_ge(a_turned, r * H + c - 1)
                        dve.tensor_tensor(att[:, c % 2].rearrange("p (b n) -> p b n", b=GROUP), psV[:, :, 0:P],
                                          rden[:, ch].rearrange("p (b a) -> p b a", a=1)
                                          .to_broadcast([P, GROUP, P]), ALU.mult).then_inc(normed, 1)
                        if ch == 0 and c > 0:
                            dve.wait_ge(np_turned, r + c // H)
                        dve.tensor_tensor(norm_p[:, :, ch], rden[:, ch], extra_p[:, ch], ALU.mult).then_inc(np_set, 1)
                    c = s - 3
                    if c >= 0 and real(it, c // H):
                        dve.wait_ge(a_hi, r * H + c + 1)
                        dve.tensor_tensor(attT[:, 1, c % 4], psum["t", c % H][:, :],
                                          attT[:, 0, c % 4].bitcast(F32), ALU.subtract).then_inc(a_lo, 1)
                    if n == 0 and s >= 0 and real(it, k):
                        dve.wait_ge(c_set, a + 1)
                        dve.wait_ge(extra_sum, r + k + 1)
                        dve.tensor_tensor(extra[:, :, :], psum["x", 0][:, 0:GROUP * H]
                                          .rearrange("p (b h) -> p b h", b=GROUP),
                                          c_row[:, :].rearrange("p (a h) -> p a h", a=1).to_broadcast([P, GROUP, H]),
                                          ALU.add).then_inc(extra_set, 1)
                        dve.wait_ge(extra_set, r + k + 1)
                    if s >= 0 and real(it, k):
                        dve.wait_ge(scored, r * H + s + 1)
                        sc = psS[n % 2][:, :].rearrange("p (b m) -> p b m", b=GROUP)
                        dve.tensor_reduce(top[:, n], sc, AX.X, ALU.max).then_inc(topped, 1)
                        dve.wait_ge(topped, r * H + s + 1)
                        dve.tensor_tensor(peak[:, n], top[:, n], extra[:, :, n], ALU.max).then_inc(peaked, 1)
                        dve.wait_ge(peaked, r * H + s + 1)
                        if s >= 2:
                            dve.wait_ge(turned, r * H + s - 1)
                        dve.tensor_tensor(s_sb[:, n % 2].rearrange("p (b m) -> p b m", b=GROUP), sc,
                                          peak[:, n].rearrange("p (b a) -> p b a", a=1)
                                          .to_broadcast([P, GROUP, P]), ALU.subtract).then_inc(eased, 1)
                        dve.tensor_tensor(gap[:, n], extra[:, :, n], peak[:, n], ALU.subtract).then_inc(gapped, 1)
                    if n == 9 and real(it, k + 1):
                        ln.dve_statistics(dve, r + k + 1, lambda b: x(it + (k + 1), b))
                    if n == 11 and real(it, k + 1):
                        ln.dve_normalise(dve, r + k + 1, lambda b: x(it + (k + 1), b))

                pipeline(dve, step)
                dve.wait_ge(added, a * NG * 2 * NQD + NG * 2 * NQD)
                dve.memset(s_sb[:, 0, 0:1], 0.0).then_inc(done, 1)

        @block.tensor
        def _(pe):
            pe.wait_ge(consts, 5)
            with pe.Fori(0, 2) as a:
                pe.wait_ge(done, a + 1)
                pe.wait_ge(c_mul, a + 1)
                pe.matmul(psW[0][:, 0:H], ones[:, :], c_prod[:, :], start=True, stop=True).then_inc(c_sum, 1)
                pe.wait_ge(dv_set, a * 2 + 2)
                pe.wait_ge(wo_in, a * 16 + 16)
                for h in range(H):
                    pe.matmul(psW[1][0:H + 1, 0:D], dv[:, h * (H + 1):(h + 1) * (H + 1)],
                              whole_o[:, h * D:(h + 1) * D], start=h == 0, stop=False)
                pe.matmul(psW[1][0:H + 1, 0:D], pick[:, :], bo[:, :], start=False, stop=True).then_inc(g_sum, 1)
                pe.wait_ge(c_set, a + 1)
                pe.wait_ge(g_set, a + 1)
                freed = {"l": (ln.s_affine, KT), "x": (extra_set, 1), "q": (q_set, H), "k": (k_set, H),
                         "v": (v_set, H), "t": (a_lo, H), "o": (added, 2 * NQD), "n": (npT_set, 1)}

                def bank(it, s, kind, n):
                    pos = order[kind, n] + s // H * len(cycle)
                    for p in range(pos - 2, pos - 12, -2):
                        kind0, n0, k0 = cycle[p % len(cycle)]
                        k0 += p // len(cycle)
                        if real(it, k0):
                            sem, per = freed[kind0]
                            pe.wait_ge(sem, (a * NG + it + k0) * per + n0 + 1)
                            break
                    return psum[kind, n]

                def step(it, s):
                    r, (k, n) = a * NG + it, divmod(s, H)
                    if n == 2 and real(it, k - 1):
                        ps = bank(it, s, "n", 0)
                        pe.wait_ge(np_set, (r + k) * H)
                        for b in range(GROUP):
                            ins = pe.transpose(ps[0:H + 1, b * P:(b + 1) * P], norm_p[:, b, :], ident[:, :])
                        ins.then_inc(np_turned, 1)
                    c = s - 2
                    if c >= 0 and real(it, c // H):
                        Q, i = divmod(c, 4)
                        pe.wait_ge(expd, r * H + c + 1)
                        if i == 0:
                            pe.wait_ge(v_set, r * H + c + 4)
                        if c >= 1:
                            pe.wait_ge(normed, r * H + c)
                        for b in range(GROUP):
                            ins = pe.matmul(psV[:, b, 0:P + 1], probs[:, c % 2, b * P:(b + 1) * P],
                                            v[:, Q % 2, b, i, :], start=True, stop=True)
                        ins.then_inc(pved, 1)
                    j, i = divmod(s - 7, 4)
                    if i == 0 and j >= 0 and real(it, j // NQD):
                        Q = j % NQD
                        pe.wait_ge(a_lo, r * H + 4 * j + 4)
                        pe.wait_ge(w_lo, r * (4 * NQD) + CREDIT + 4 * j + 7)
                        if Q == NQD - 1:
                            pe.wait_ge(npT_set, r + j // NQD + 1)
                        for m in range(2):
                            ps = bank(it, s, "o", 2 * Q + m)
                            for e in range(2):
                                tok = slice((2 * m + e) * P, (2 * m + e + 1) * P)
                                out = ps[:, e * D:(e + 1) * D]
                                for i in range(QH):
                                    col = 3 * PART + i * D
                                    ins = mm3(pe, out, lambda s: attT[:, s, i, tok],
                                              lambda s: w[:, Q % 2, s, col:col + D],
                                              i == 0, i == QH - 1 and Q < NQD - 1)
                                if Q == NQD - 1:
                                    ins = pe.matmul(out, norm_pT[:, tok], big_g[:, :], start=False, stop=True)
                            ins.then_inc(outp, 1)
                    c = s - 3
                    if c >= 0 and real(it, c // H):
                        ps = bank(it, s, "t", c % H)
                        pe.wait_ge(normed, r * H + c + 1)
                        for b in range(GROUP):
                            ins = pe.transpose(ps[:, b * P:(b + 1) * P], att[:, c % 2, b * P:(b + 1) * P],
                                               ident[:, :])
                        ins.then_inc(a_turned, 1)
                    if s >= 0 and real(it, k):
                        pe.wait_ge(k_set, r * H + s + 1)
                        if s >= 2:
                            pe.wait_ge(eased, r * H + s - 1)
                        for b in range(GROUP):
                            tok = slice(b * P, (b + 1) * P)
                            ins = pe.matmul(psS[n % 2][:, tok], qk[:, n % SLOTS, tok], qk[:, SLOTS + n % SLOTS, tok],
                                            start=True, stop=True)
                        ins.then_inc(scored, 1)
                    h = s + LEAD
                    kh, m = divmod(h, H)
                    if h >= 0 and real(it, kh):
                        Q, i = divmod(m, 4)
                        if i == 0:
                            pe.wait_ge(w_lo, r * (4 * NQD) + CREDIT + h + 3)
                        if m == 0:
                            ln.pe_ready(pe, r + kh)
                        for kind, part, signal in (("q", 0, q_sum), ("k", 1, k_sum)):
                            ps = bank(it, s, kind, m)
                            if m == 0 and kind == "k":
                                pe.wait_ge(ctx_in, (r + kh) * 16 + 16)
                            for c in range(KT):
                                col = part * PART + c * QH * P + i * P
                                ins = mm3(pe, ps[:, :], lambda s: w[:, Q % 2, s, col:col + P],
                                          lambda s: ln.hT[:, s, c] if kind == "q" else cT[:, :, s, c],
                                          c == 0, c == KT - 1)
                            ins.then_inc(signal, 1)
                    c = s - 1
                    if c >= 0 and real(it, c // H):
                        pe.wait_ge(eased, r * H + c + 1)
                        if c >= 2:
                            pe.wait_ge(expd, r * H + c - 1)
                        for b in range(GROUP):
                            ins = pe.transpose(psT[c % 2][:, b * P:(b + 1) * P], s_sb[:, c % 2, b * P:(b + 1) * P],
                                               ident[:, :])
                        ins.then_inc(turned, 1)
                    if h >= 0 and real(it, kh):
                        ps = bank(it, s, "v", m)
                        for c in range(KT):
                            col = 2 * PART + c * QH * P
                            ins = mm3(pe, ps[:, :], lambda s: cT[:, i, s, c],
                                      lambda s: w[:, Q % 2, s, col:col + QH * P], c == 0, c == KT - 1)
                        ins.then_inc(v_sum, 1)
                    if n == 12 and real(it, k + 1):
                        for c in range(KT):
                            ln.pe_turn_tile(pe, r + k + 1, c, bank(it, s, "l", c), ident)
                    if n == 15 and real(it, k + 1):
                        ps = bank(it, s, "x", 0)
                        pe.wait_ge(u_set, a + 1)
                        for b in range(GROUP):
                            for c in range(KT):
                                ins = mm3(pe, ps[:, b * H:(b + 1) * H], lambda s: ln.hT[:, s, c, b * P:(b + 1) * P],
                                          lambda s: u_parts[:, s, c], c == 0, c == KT - 1)
                        ins.then_inc(extra_sum, 1)

                pipeline(pe, step)


def _columns(parts):
    import numpy as np
    return np.ascontiguousarray(np.concatenate(parts, axis=1))


def _stack_heads(wT, heads, dh, slot, parts=3):
    import numpy as np
    out = np.zeros((wT.shape[0], len(heads) * slot), wT.dtype)
    for i, h in enumerate(heads):
        for r in range(parts):
            out[:, i * slot + r * dh:i * slot + (r + 1) * dh] = wT[:, h * dh:(h + 1) * dh]
    return out


def _lo_rows(slot, dh, part):
    import numpy as np
    m = np.zeros((P, 1), np.float32)
    for i in range(P // slot):
        m[i * slot + part * dh:i * slot + (part + 1) * dh] = -1.0
    return m


def _layer0_arrays(i):
    import numpy as np
    wq, wk = i["L0_xattn_Wq"].T, i["L0_xattn_Wk"].T
    parts = [_stack_heads(wq, range(4 * n, 4 * n + 4), 8, 32) for n in range(4)]
    parts += [_stack_heads(wk, range(4 * n, 4 * n + 4), 8, 32) for n in range(4)]
    parts += [i["L0_xattn_Wv"].T, i["L0_xattn_Wo"].T]
    cols = [_lo_rows(32, 8, 1), _lo_rows(32, 8, 2), i["L0_xattn_bo"][:, None]]
    return {"l0_w": _columns(parts), "l0_cols": _columns(cols)}


def _tiles(w):
    return w.reshape(-1, P, w.shape[1]).transpose(1, 0, 2)


def _per_tile(v):
    return v.reshape(-1, P).T


def _layer1_arrays(i):
    import numpy as np
    g = {k[9:]: v for k, v in i.items() if k.startswith("L1_xattn_")}
    pairs = [range(2 * n, 2 * n + 2) for n in range(8)]
    w = np.concatenate([_stack_heads(g["q_w"], p, 16, 64) for p in pairs]
                       + [_stack_heads(g["k_w"], p, 16, 64) for p in pairs] + [g["v_w"], g["cproj_w"]], axis=1)
    cols = [_lo_rows(64, 16, 1), _lo_rows(64, 16, 2)]
    cols += [_stack_heads(g["q_b"][None], p, 16, 64).T for p in pairs]
    cols += [_stack_heads(g["k_b"][None], p, 16, 64).T for p in pairs]
    cols += [_per_tile(g["ln1_w"]), _per_tile(g["ln1_b"])]
    rows = [g["v_b"], g["cproj_b"], g["ln1_w"], g["ln1_b"]]
    return {"l1_w": _tiles(w), "l1_cols": _columns(cols), "l1_rows": np.concatenate(rows)[None],
            "l1_mask": i["mask_BxS2_bf1"].view(np.int32).reshape(NG, -1)}


def _mlp_arrays(name, fc_w, fc_b, proj_w, proj_b, gamma, beta):
    w = _columns([_tiles(fc_w).reshape(P, -1), _tiles(proj_w).reshape(P, -1)])
    return {name + "_w": w, name + "_cols": _columns([_per_tile(fc_b), _per_tile(gamma), _per_tile(beta)]),
            name + "_rows": proj_b[None]}


def _layer3_arrays(i):
    import numpy as np
    g = {k[9:]: v for k, v in i.items() if k.startswith("L3_xattn_")}
    quads = [[(4 * kt + s) * 4 + m for s in range(4)] for kt in range(2) for m in range(4)]
    kheads = [range(4 * kt, 4 * kt + 4) for kt in range(2)]
    w = np.concatenate([_stack_heads(g["Wq"], q, 8, 32) for q in quads]
                       + [_stack_heads(g["Wk"], k, 8, 32) for k in kheads] + [g["Wv"], g["Wo"]], axis=1)
    cols = [_lo_rows(32, 8, 1), _lo_rows(32, 8, 2)]
    cols += [_stack_heads(g["bq"][None], q, 8, 32).T for q in quads]
    cols += [_stack_heads(g["bk"][None], k, 8, 32).T for k in kheads]
    cols += [_per_tile(g["gamma"]), _per_tile(g["beta"])]
    rows = [g["bv"], g["bo"], g["gamma"], g["beta"]]
    return {"l3_w": _tiles(w), "l3_cols": _columns(cols), "l3_rows": np.concatenate(rows)[None],
            "l3_mask": i["mask_Bx1xSxS2_ff0"].reshape(BATCH, P, P)}


def _layer2_arrays(i):
    import numpy as np
    g = {k[9:]: v for k, v in i.items() if k.startswith("L2_xattn_")}
    qkv, o, cols, ek, bo = [], [], [], [], []
    for n in "12":
        for Q in range(4):
            at = slice(Q * 512, (Q + 1) * 512)
            qkv.append(np.concatenate([_tiles(g["w" + m + n][:, at]).reshape(P, -1) for m in "qkv"], axis=1))
            o.append(_tiles(g["wo" + n][at]).reshape(P, -1))
        cols.append(_columns([_per_tile(g["bq" + n]), _per_tile(g["bk" + n]), _per_tile(g[f"ln{n}_scale"]),
                              _per_tile(g[f"ln{n}_offset"]), _per_tile(g["bias_k" + n].reshape(-1)),
                              _per_tile(g["bias_v" + n].reshape(-1)), _per_tile(g["bv" + n])]))
        ek.append(g["bias_k" + n].reshape(-1))
        bo.append(g["bo" + n])
    return {"l2_qkv": np.stack(qkv), "l2_o": np.stack(o), "l2_cols": np.stack(cols), "l2_ek": np.stack(ek),
            "l2_bo": np.stack(bo)}


def kernel(**inputs):
    import numpy as _np
    import concourse.bacc as _bacc
    from concourse.bass_utils import run_bass_kernel_spmd as _run
    i = {k: _np.asarray(v) for k, v in inputs.items()}
    nc = _bacc.Bacc("TRN2", target_bir_lowering=False, num_devices=1)
    arrays = {"x": i["x"], "ctx": i["ctx_2048"], **_layer0_arrays(i),
              **_layer1_arrays(i),
              **_mlp_arrays("m1", *[i["L1_xattn_" + n] for n in ("fc_w", "fc_b", "proj_w", "proj_b", "ln2_w", "ln2_b")]),
              **_layer2_arrays(i),
              **_mlp_arrays("m2", *[i["L2_xattn_" + n] for n in ("w_fc1", "b_fc1", "w_fc2", "b_fc2", "ln_mlp_scale",
                                                          "ln_mlp_offset")]),
              **_layer3_arrays(i)}
    d = {}
    for name, a in arrays.items():
        a = arrays[name] = _np.ascontiguousarray(a)
        d[name] = nc.dram_tensor("in_" + name, a.shape, mybir.dt.from_np(a.dtype), kind="ExternalInput").ap()
    out = nc.dram_tensor("out", (BATCH, P, D), F32, kind="ExternalOutput").ap()
    ctxT = nc.dram_tensor("ctxT", (BATCH, P, 2 * KT * P), F32, kind="Internal").ap()
    with ExitStack() as ctx:
        X = ctx.enter_context(nc.sbuf_tensor("X", [P, BATCH, D], F32))
        ident = ctx.enter_context(nc.sbuf_tensor("ident", [P, P], F32))
        stage = Stage(nc, ctx, d)
        identity_phase(nc, ident)
        layer0_phase(nc, d["x"], d["ctx"], d["l0_w"], d["l0_cols"], X, ctxT, ident, stage, "l1")
        heads_phase(nc, 1, X, ctxT, d["l1_cols"], d["l1_rows"], d["l1_mask"], ident, stage, "m1")
        mlp_phase(nc, "m1", ACT.Gelu_apprx_tanh, X, d["m1_cols"], d["m1_rows"], ident, stage, "l2")
        clear_semaphores(nc)
        wide_phase(nc, X, ctxT, d, ident, stage, "m2")
        mlp_phase(nc, "m2", ACT.Gelu, X, d["m2_cols"], d["m2_rows"], ident, stage, "l3")
        heads_phase(nc, 3, X, ctxT, d["l3_cols"], d["l3_rows"], d["l3_mask"], ident, stage, out_dram=out)
    r = _run(nc, [{"in_" + k: a for k, a in arrays.items()}], core_ids=[0])
    return r.results[0]["out"]
```
